# Optimizing a Trainium2 kernel written in Bass

```python
import numpy as np
import jax
import jax.numpy as jnp

def _softmax(x, axis=-1):
    return jax.nn.softmax(x, axis=axis)

def _gelu(x):
    return jax.nn.gelu(x, approximate=True)

def _silu(x):
    return jax.nn.silu(x)

def _sigmoid(x):
    return jax.nn.sigmoid(x)

def _layernorm(x, axis=-1, eps=1e-05):
    m = jnp.mean(x, axis=axis, keepdims=True)
    v = jnp.var(x, axis=axis, keepdims=True)
    return (x - m) / jnp.sqrt(v + eps)

def _scatter_add(tgt, idx, src, axis=0):
    return tgt.at[idx].add(src)

def _segment_sum(src, seg, n):
    return jax.ops.segment_sum(src, seg, n)
kernel_name = 'mk_seq_postln_d1_jaxref_r4_2e080e'

def setup_inputs(seed: int=0):
    np.random.seed(seed)
    _w = jnp.asarray

    def _L0_attn_setup():
        import jax, jax.numpy as jnp
        import numpy as np
        D_MODEL = 512
        N_HEADS = 16
        HEAD_DIM = D_MODEL // N_HEADS
        LN_EPS = 1e-06
        NEG_INF = float('-inf')

        def _layernorm_scale_only(x, scale):
            mean = jnp.mean(x, axis=-1, keepdims=True)
            var = jnp.var(x, axis=-1, keepdims=True)
            return (x - mean) * jax.lax.rsqrt(var + LN_EPS) * scale
        key = jax.random.key(seed)
        ks = jax.random.split(key, 4)
        B, S = (2, 512)
        x = jax.random.normal(ks[0], (B, S, D_MODEL), dtype=jnp.float32)
        Wqkv = jax.random.normal(ks[1], (D_MODEL, 3 * D_MODEL), dtype=jnp.float32) * 0.02
        q_ln_scale = jnp.ones((D_MODEL,), dtype=jnp.float32)
        k_ln_scale = jnp.ones((D_MODEL,), dtype=jnp.float32)
        out_W = jax.random.normal(ks[2], (D_MODEL, D_MODEL), dtype=jnp.float32) * 0.02
        return {'x': x, 'Wqkv': Wqkv, 'q_ln_scale': q_ln_scale, 'k_ln_scale': k_ln_scale, 'out_W': out_W}
    _L0_attn_in = _L0_attn_setup()

    def _L0_ffn_setup():
        import jax, jax.numpy as jnp
        import numpy as np
        ZERO_POINT = 128.0

        def _dequant(wq, scale):
            return (wq.astype(jnp.float32) - ZERO_POINT) * scale[:, None]
        key = jax.random.key(seed)
        ks = jax.random.split(key, 7)
        H, I = (512, 2048)
        B, S = (2, 512)
        hidden_state = jax.random.normal(ks[0], (B, S, H), dtype=jnp.float32)
        gate_w = jax.random.randint(ks[1], (I, H), 0, 64, dtype=jnp.int32)
        up_w = jax.random.randint(ks[2], (I, H), 0, 64, dtype=jnp.int32)
        down_w = jax.random.randint(ks[3], (H, I), 0, 64, dtype=jnp.int32)
        gate_scale = jax.random.uniform(ks[4], (I,), dtype=jnp.float32) * 0.02
        up_scale = jax.random.uniform(ks[5], (I,), dtype=jnp.float32) * 0.02
        down_scale = jax.random.uniform(ks[6], (H,), dtype=jnp.float32) * 0.02
        return {'hidden_state': hidden_state, 'gate_w': gate_w, 'gate_scale': gate_scale, 'up_w': up_w, 'up_scale': up_scale, 'down_w': down_w, 'down_scale': down_scale}
    _L0_ffn_in = _L0_ffn_setup()
    _d = {'L0_attn_x': _L0_attn_in['x'], 'L0_attn_Wqkv': _L0_attn_in['Wqkv'], 'L0_attn_q_ln_scale': _L0_attn_in['q_ln_scale'], 'L0_attn_k_ln_scale': _L0_attn_in['k_ln_scale'], 'L0_attn_out_W': _L0_attn_in['out_W'], 'L0_ffn_gate_w': _L0_ffn_in['gate_w'], 'L0_ffn_gate_scale': _L0_ffn_in['gate_scale'], 'L0_ffn_up_w': _L0_ffn_in['up_w'], 'L0_ffn_up_scale': _L0_ffn_in['up_scale'], 'L0_ffn_down_w': _L0_ffn_in['down_w'], 'L0_ffn_down_scale': _L0_ffn_in['down_scale']}
    _x0 = _d['L0_attn_x']
    _d['L0_attn_x'] = jax.random.normal(jax.random.fold_in(jax.random.key(seed), 1), (1, 4096, 512), dtype=_x0.dtype)
    del _x0
    return _d

def reference(L0_attn_x, L0_attn_Wqkv, L0_attn_q_ln_scale, L0_attn_k_ln_scale, L0_attn_out_W, L0_ffn_gate_w, L0_ffn_gate_scale, L0_ffn_up_w, L0_ffn_up_scale, L0_ffn_down_w, L0_ffn_down_scale):

    def _L0_attn_ref(x, Wqkv, q_ln_scale, k_ln_scale, out_W):
        import jax, jax.numpy as jnp
        import numpy as np
        D_MODEL = 512
        N_HEADS = 16
        HEAD_DIM = D_MODEL // N_HEADS
        LN_EPS = 1e-06
        NEG_INF = float('-inf')

        def _layernorm_scale_only(x, scale):
            mean = jnp.mean(x, axis=-1, keepdims=True)
            var = jnp.var(x, axis=-1, keepdims=True)
            return (x - mean) * jax.lax.rsqrt(var + LN_EPS) * scale
        B, S, _ = x.shape
        qkv = jnp.einsum('bsd,de->bse', x, Wqkv)
        q, k, v = jnp.split(qkv, 3, axis=-1)
        q = _layernorm_scale_only(q, q_ln_scale)
        k = _layernorm_scale_only(k, k_ln_scale)
        q = q.reshape(B, S, N_HEADS, HEAD_DIM)
        k = k.reshape(B, S, N_HEADS, HEAD_DIM)
        v = v.reshape(B, S, N_HEADS, HEAD_DIM)
        scores = jnp.einsum('bshd,bthd->bhst', q / jnp.sqrt(jnp.float32(HEAD_DIM)), k)
        causal = jnp.triu(jnp.ones((S, S), dtype=bool), 1)
        scores = jnp.where(causal, NEG_INF, scores)
        attn = jax.nn.softmax(scores, axis=-1)
        ctx = jnp.einsum('bhst,bthd->bshd', attn, v)
        out = jnp.einsum('bsd,de->bse', ctx.reshape(B, S, D_MODEL), out_W)
        return out

    def _L0_ffn_ref(hidden_state, gate_w, gate_scale, up_w, up_scale, down_w, down_scale):
        import jax, jax.numpy as jnp
        import numpy as np
        ZERO_POINT = 128.0

        def _dequant(wq, scale):
            return (wq.astype(jnp.float32) - ZERO_POINT) * scale[:, None]
        Wg = _dequant(gate_w, gate_scale)
        Wu = _dequant(up_w, up_scale)
        Wd = _dequant(down_w, down_scale)
        g = jnp.einsum('bsh,ih->bsi', hidden_state, Wg)
        u = jnp.einsum('bsh,ih->bsi', hidden_state, Wu)
        h = jax.nn.silu(g) * u
        return jnp.einsum('bsi,hi->bsh', h, Wd)
    x = L0_attn_x
    x = _layernorm(x + _L0_attn_ref(x, L0_attn_Wqkv, L0_attn_q_ln_scale, L0_attn_k_ln_scale, L0_attn_out_W), axis=-1)
    x = _layernorm(x + _L0_ffn_ref(x, L0_ffn_gate_w, L0_ffn_gate_scale, L0_ffn_up_w, L0_ffn_up_scale, L0_ffn_down_w, L0_ffn_down_scale), axis=-1)
    return x

_drawn_inputs = setup_inputs


def setup_inputs(seed=0):
    import zlib

    import numpy as np

    out = dict(_drawn_inputs(seed))
    spreads = {'L0_attn_q_ln_scale': (1.0, 0.6), 'L0_attn_k_ln_scale': (1.0, 0.6)}
    factors = {}
    for name, (base, spread) in spreads.items():
        noise = np.random.default_rng([zlib.crc32(name.encode()), seed]).standard_normal(out[name].shape)
        drawn = base * np.exp(spread * noise) if base else spread * noise
        out[name] = jnp.asarray(drawn.astype(out[name].dtype))
    for name, factor in factors.items():
        out[name] = (out[name] * factor).astype(out[name].dtype)
    return out
```

```python
from contextlib import ExitStack

import concourse.bass as bass
from concourse import mybir

F32 = mybir.dt.float32
F32R = mybir.dt.float32r
BF16 = mybir.dt.bfloat16
I32 = mybir.dt.int32
ALU = mybir.AluOpType
ACT = mybir.ActivationFunctionType
AX = mybir.AxisListType

P = 128
S = 4096
D = 512
HEADS = 16
HD = D // HEADS
INNER = 2048
CH = 512
NCH = S // CH
ST = CH // P
DC = D // P
HG = P // HD
NG = HEADS // HG
IC = INNER // P
KB = S // P
QK_EPS = 1e-6
LN_EPS = 1e-5
ZERO_POINT = 128.0
BOUND = 60.0
WHOLE = 4096.0
ROWS = 3 * HD + 2


def project(nc, io, dr, keep):
    TB = 3
    order = [("x", 0), ("x", 1), ("qkv", 0), ("w", 0), ("w", 1), ("x", 2), ("qkv", 1), ("w", 2), ("x", 3),
             ("qkv", 2), ("w", 3), ("qkv", 3), ("w", 4), ("w", 5)]
    order += [("qk", i) for i in range(2 * DC)]
    jobs = [o for o in order if o[0] != "qkv"]
    NJ = len(jobs)
    at = {o: j for j, o in enumerate(jobs)}
    lows = [o for o in jobs if o[0] != "w"]
    NL = len(lows)

    def lows_before(j):
        if j < 0:
            return lows_before(j + NJ) - NL
        return sum(o[0] != "w" for o in jobs[:j])

    with ExitStack() as c:
        sb = lambda n, s, d=F32: c.enter_context(nc.sbuf_tensor(n, s, d))
        sem = lambda n: c.enter_context(nc.semaphore(n))
        x_in = sb("x_in", [P, ST, D])
        x_hi = sb("x_hi", [P, 2, D], F32R)
        x_lo = sb("x_lo", [P, 2, D], F32R)
        w_raw = sb("w_raw", [P, DC, 3 * D])
        w_hi = sb("w_hi", [P, DC, 3 * D], F32R)
        w_lo = sb("w_lo", [P, DC, 3 * D], F32R)
        normed = [sb("qn", [P, ST, D]), sb("kn", [P, ST, D])]
        part_hi = sb("part_hi", [P, 4, CH], F32R)
        part_lo = sb("part_lo", [P, 4, CH], F32R)
        squares = sb("squares", [P, 2, CH], BF16)
        v_out = sb("v_out", [P, 2, D])
        wq_int = sb("wq_int", [P, 2, D], I32)
        wq_f = sb("wq_f", [P, 2, D])
        wq_t = sb("wq_t", [P, 2, D])
        ident = sb("ident", [P, P])
        select = sb("select", [P, HD], BF16)
        stats = sb("stats", [P, 6])
        mv = sb("mv", [P, 2, 2])
        veps = sb("veps", [P, 2])
        rstd = sb("rstd", [P, 2])
        minus_half = sb("minus_half", [P, 1])
        quarter = sb("quarter", [P, DC])
        scales = sb("scales", [P, 2, DC])
        mix = sb("mix", [P, DC])
        mix_root = sb("mix_root", [P, DC])
        norm_max = sb("norm_max", [P, 2, NCH])
        whole_max = sb("whole_max", [P, 6, NCH])
        norm_top = sb("norm_top", [P, 2])
        checks = sb("checks", [P, 2])
        checks_all = sb("checks_all", [P, 2])
        flags_f = sb("flags_f", [P, 2])
        zeros = sb("zeros", [P, 2 * HEADS * S // P])

        turn = [c.enter_context(nc.psum_tensor(f"turn{i}", [P, 512], F32)) for i in range(TB)]
        acc = [c.enter_context(nc.psum_tensor(f"acc_{n}", [P, 512], F32)) for n in "qkv"]
        norms = [c.enter_context(nc.psum_tensor(f"norms_{n}", [P, 512], F32)) for n in "qk"]

        x_ready = sem("x_ready")
        wqkv_in = [sem(f"wqkv_in{dc}") for dc in range(DC)]
        w_high_done = sem("w_high_done")
        w_low_done = sem("w_low_done")
        ident_ready = sem("ident_ready")
        scales_ready = sem("scales_ready")
        dconst = sem("dconst")
        scales_in = sem("scales_in")
        turned = sem("turned")
        high_done = sem("high_done")
        low_done = sem("low_done")
        acc_full = sem("acc_full")
        v_taken = sem("v_taken")
        v_stored = [sem(f"v_stored{i}") for i in range(2)]
        vstat = sem("vstat")
        var_ready = sem("var_ready")
        rstd_ready = sem("rstd_ready")
        qk_normed = sem("qk_normed")
        sq_ready = sem("sq_ready")
        norms_done = sem("norms_done")
        norms_read = sem("norms_read")
        parts_stored = [sem(f"parts_stored{i}") for i in range(4)]
        int_in = [sem(f"int_in{i}") for i in range(2)]
        int_read = sem("int_read")
        float_ready = sem("float_ready")
        whole_read = sem("whole_read")
        wt_stored = [sem(f"wt_stored{i}") for i in range(2)]
        zero_stored = sem("zero_stored")
        fin = sem("fin")
        fin_pool = sem("fin_pool")
        block = c.enter_context(nc.Block())

        def weight_source(i, n, e):
            if i < 2:
                return (io["gate_w"], io["up_w"])[i].rearrange("(c p) h -> c p h", p=P)[bass.ds(n * 2 + e, 1)].rearrange(
                    "c p h -> p (c h)")
            return io["down_w"].rearrange("(c p) (j i) -> p j c i", p=P, i=P)[:, bass.ds(n * 2 + e, 1)].rearrange(
                "p j c i -> p (j c) i")

        @block.sync
        def _(sp):
            with nc.allow_non_contiguous_dma(reason="scales as columns"):
                for g in range(DC):
                    sp.dma_start(scales[:, 0, g:g + 1], io["q_scale"][g * P:(g + 1) * P].rearrange("(p a) -> p a", a=1)).then_inc(scales_in, 16)
                    sp.dma_start(scales[:, 1, g:g + 1], io["k_scale"][g * P:(g + 1) * P].rearrange("(p a) -> p a", a=1)).then_inc(scales_in, 16)
            xs = io["x"].rearrange("(n t p) d -> n p t d", t=ST, p=P)
            sp.dma_start(x_in[:], xs[0]).then_inc(x_ready, 16)
            for dc in range(DC):
                sp.dma_start(w_raw[:, dc, :], io["wqkv"][dc * P:(dc + 1) * P, :]).then_inc(wqkv_in[dc], 16)
            sp.wait_ge(dconst, 1)
            sp.dma_start(dr["shift"].rearrange("a h (u s) -> (a h u) s", u=4), zeros[:]).then_inc(zero_stored, 16)

            def load_int(n, w):
                sp.wait_ge(int_read, 6 * n + w + 1)
                sp.nop(nofuse=True)
                sp.dma_start(wq_int[:, w % 2, :] if w < 4 else wq_int[:, w % 2, :].rearrange("p (c i) -> p c i", c=DC),
                             weight_source(w // 2, n, w % 2)).then_inc(int_in[w % 2], 16)

            def chunk(n, more):
                for kind, i in order:
                    if kind == "x" and i == ST - 1 and more:
                        sp.wait_ge(turned, NJ * n + at["x", ST - 1] + 1)
                        sp.nop(nofuse=True)
                        sp.dma_start(x_in[:], xs[bass.ds(n + 1, 1)].rearrange("n p t d -> (n p) t d")).then_inc(x_ready, 16)
                    elif kind == "qkv":
                        sp.wait_ge(v_taken, ST * n + i + 2)
                        sp.nop(nofuse=True)
                        sp.dma_start(dr["v"].rearrange("(t p) d -> t p d", p=P)[bass.ds(n * ST + i, 1)].rearrange("t p d -> (t p) d"),
                                     v_out[:, i % 2, :]).then_inc(v_stored[i % 2], 16)
                    elif kind == "w":
                        sp.wait_ge(high_done, NJ * n + at["w", i] + 1 + TB)
                        sp.nop(nofuse=True)
                        sp.dma_start(dr[("wg", "wu", "wd")[i // 2]][bass.ds(n * 2 + i % 2, 1)].rearrange("c p x -> (c p) x"),
                                     wq_t[:, i % 2, :]).then_inc(wt_stored[i % 2], 16)
                        if i < 4:
                            load_int(n, i + 2)
                        elif more:
                            load_int(n + 1, i - 4)
                    elif kind == "qk":
                        sp.wait_ge(high_done, NJ * n + at["qk", i] + 1 + TB)
                        sp.nop(nofuse=True)
                        sp.wait_ge(low_done, NL * n + lows_before(at["qk", i] + 1) + TB)
                        sp.nop(nofuse=True)
                        g = i % DC
                        for src, to in ((part_hi, ("q_hi", "k_hi")), (part_lo, ("q_lo", "k_lo"))):
                            sp.dma_start(dr[to[i // DC]][g * P:(g + 1) * P, bass.ds(n * CH, CH)], src[:, i % 4, :].bitcast(F32))\
                               .then_inc(parts_stored[i % 4], 16)

            for s_, k in ((wt_stored, 16), (parts_stored, 32), (v_stored, 16)):
                for one in s_:
                    sp.sem_inc(one, k)
            load_int(0, 0)
            load_int(0, 1)
            with sp.Fori(0, NCH - 1) as n:
                chunk(n, True)
            chunk(NCH - 1, False)
            sp.wait_ge(zero_stored, 16)
            for s_, k in ((wt_stored, 16 + 48 * NCH), (parts_stored, 32 + 64 * NCH), (v_stored, 16 + 32 * NCH)):
                for one in s_:
                    sp.wait_ge(one, k)
                    sp.nop(nofuse=True)

        @block.gpsimd
        def _(pool):
            pool.memset(ident[:], 0.0).then_inc(fin_pool, 1)
            pool.wait_ge(fin_pool, 1)
            pool.affine_select(out=ident[:], in_=ident[:], compare_op=ALU.not_equal, fill=1.0, base=0,
                               pattern=[[-1, P]], channel_multiplier=1).then_inc(ident_ready, 1)
            pool.sem_inc(int_read, 2)
            pool.wait_ge(dconst, 4)
            pool.tensor_tensor(mix_root[:], mix[:], quarter[:], ALU.pow).then_inc(scales_ready, 1)

            def convert(n, w):
                pool.wait_ge(int_in[w % 2], 48 * n + 16 * (w // 2) + 16)
                pool.wait_ge(whole_read, 6 * n + w + 1)
                if w >= 2:
                    pool.wait_ge(turned, NJ * n + at["w", w - 2] + 1)
                pool.nop(nofuse=True)
                ins = pool.tensor_scalar(wq_f[:, w % 2, :], wq_int[:, w % 2, :], -ZERO_POINT, None, ALU.add)
                ins.then_inc(float_ready, 1)
                pool.wait_ge(float_ready, 6 * n + w + 1)
                pool.sem_inc(int_read, 1)

            def root(n, st, i):
                pool.wait_ge(var_ready, 2 * ST * n + 2 * st + i + 1)
                pool.tensor_tensor(rstd[:, i:i + 1], veps[:, i:i + 1], minus_half[:], ALU.pow).then_inc(rstd_ready, 1)

            with pool.Fori(0, NCH) as n:
                pool.wait_ge(turned, NJ * n + 1)
                convert(n, 0)
                convert(n, 1)
                for st in range(ST):
                    root(n, st, 0)
                    root(n, st, 1)
                    convert(n, st + 2)
            pool.wait_ge(fin, 3)
            pool.partition_all_reduce(checks_all[:], checks[:], P, bass.bass_isa.ReduceOp.max).then_inc(fin_pool, 1)

        @block.tensor
        def _(pe):
            pe.sem_inc(high_done, TB)
            pe.sem_inc(low_done, TB)
            pe.sem_inc(v_taken, 1)
            pe.wait_ge(ident_ready, 1)
            pe.wait_ge(dconst, 3)

            def bank(n, j):
                pe.wait_ge(high_done, NJ * n + j + 1)
                pe.wait_ge(low_done, NL * n + lows_before(j - TB + 1) + TB)
                return turn[j % TB]

            def job(n, kind, i):
                j = at[kind, i]
                b = bank(n, j)
                if kind == "x":
                    if i == 0:
                        pe.wait_ge(x_ready, 16 * n + 16)
                    src = [x_in[:, i, dc * P:(dc + 1) * P] for dc in range(DC)]
                elif kind == "w":
                    pe.wait_ge(float_ready, 6 * n + i + 1)
                    src = [wq_f[:, i % 2, dc * P:(dc + 1) * P] for dc in range(DC)]
                else:
                    pe.wait_ge(qk_normed, 2 * ST * (n + 1))
                    src = [normed[i // DC][:, st, (i % DC) * P:(i % DC + 1) * P] for st in range(ST)]
                for q in range(4):
                    ins = pe.transpose(b[:, q * P:(q + 1) * P], src[q], ident[:])
                ins.then_inc(turned, 1)

            def qkv(n, st):
                pe.wait_ge(high_done, NJ * n + at["x", st] + 1 + TB)
                pe.wait_ge(low_done, NL * n + lows_before(at["x", st] + 1) + TB)
                for m in range(3):
                    if m < 2:
                        if st:
                            pe.wait_ge(qk_normed, 2 * ST * n + 2 * st - 1 + m)
                    else:
                        pe.wait_ge(v_taken, ST * n + st + 1)
                    first = True
                    for dc in range(DC):
                        xs = [t[:, st % 2, dc * P:(dc + 1) * P] for t in (x_hi, x_lo)]
                        if m == 0 and st == 0:
                            pe.wait_ge(w_low_done, dc + 1)
                        for a, w in ((0, w_hi), (0, w_lo), (1, w_hi)):
                            ins = pe.matmul(acc[m][:], xs[a], w[:, dc, m * D:(m + 1) * D],
                                            start=first, stop=dc == DC - 1 and a == 1)
                            first = False
                    ins.then_inc(acc_full, 1)

            def norm(n, i):
                pe.wait_ge(sq_ready, 2 * DC * n + i + 1)
                if i % DC == 0:
                    pe.wait_ge(norms_read, 2 * n + i // DC + 1)
                g = i % DC
                pe.matmul(norms[i // DC][g * HD:(g + 1) * HD, :], select[:], squares[:, i % 2, :],
                          start=True, stop=True).then_inc(norms_done, 1)

            with pe.Fori(0, NCH) as n:
                for kind, i in order:
                    if kind == "qkv":
                        qkv(n, i)
                    else:
                        job(n, kind, i)
                    if kind == "qk" and i >= 2:
                        norm(n, i - 2)
                norm(n, 2 * DC - 2)
                norm(n, 2 * DC - 1)

        @block.scalar
        def _(act):
            for dc in range(DC):
                act.wait_ge(wqkv_in[dc], 16)
                act.activation(w_hi[:, dc, :], w_raw[:, dc, :], ACT.Copy).then_inc(w_high_done, 1)
            act.wait_ge(scales_ready, 2)

            def high(n, kind, i):
                j = at[kind, i]
                act.wait_ge(turned, NJ * n + j + 1)
                b = turn[j % TB]
                if kind == "x":
                    if i >= 2:
                        act.wait_ge(acc_full, 3 * ST * n + 3 * (i - 1))
                    act.activation(x_hi[:, i % 2, :], b[:], ACT.Copy).then_inc(high_done, 1)
                elif kind == "w":
                    act.wait_ge(wt_stored[i % 2], 48 * n + 16 * (i // 2) + 16)
                    act.activation(wq_t[:, i % 2, :], b[:], ACT.Copy).then_inc(high_done, 1)
                else:
                    act.wait_ge(parts_stored[i % 4], 64 * n + 32 * (i // 4) + 32)
                    if i >= 2:
                        act.wait_ge(norms_done, 2 * DC * n + i - 1)
                    g = i % DC
                    act.activation(squares[:, i % 2, :], b[:], ACT.Square, scale=mix_root[:, g:g + 1]).then_inc(sq_ready, 1)
                    act.activation(part_hi[:, i % 4, :], b[:], ACT.Copy, scale=scales[:, i // DC, g:g + 1]).then_inc(high_done, 1)

            def take_v(n, st):
                act.wait_ge(acc_full, 3 * ST * n + 3 * st + 3)
                act.wait_ge(v_stored[st % 2], 32 * n + 16 * (st // 2) + 16)
                act.activation(v_out[:, st % 2, :], acc[2][:], ACT.Copy).then_inc(v_taken, 1)

            with act.Fori(0, NCH) as n:
                for kind, i in order:
                    if kind == "qkv":
                        take_v(n, i)
                    else:
                        high(n, kind, i)

        @block.vector
        def _(dve):
            dve.memset(minus_half[:], -0.5)
            dve.memset(quarter[:], 0.25)
            dve.memset(zeros[:], 0.0).then_inc(dconst, 1)
            dve.memset(select[:], 0.0).then_inc(dconst, 1)
            dve.wait_ge(dconst, 2)
            for h in range(HG):
                ins = dve.memset(select[h * HD:(h + 1) * HD, h:h + 1], 1.0)
            ins.then_inc(dconst, 1)
            dve.wait_ge(scales_in, 16 * 2 * DC)
            root_hd = float(HD) ** -0.5
            dve.tensor_tensor(mix[:], scales[:, 0, :], scales[:, 1, :], ALU.mult).then_inc(vstat, 1)
            dve.wait_ge(vstat, 1)
            dve.tensor_scalar(mix_root[:], mix[:], root_hd, None, ALU.mult).then_inc(vstat, 1)
            dve.wait_ge(vstat, 2)
            dve.tensor_tensor(mix[:], mix_root[:], mix_root[:], ALU.mult).then_inc(dconst, 1)
            dve.tensor_scalar(scales[:, 0, :], scales[:, 0, :], root_hd, None, ALU.mult).then_inc(scales_ready, 1)
            for dc in range(DC):
                dve.wait_ge(w_high_done, dc + 1)
                dve.tensor_tensor(w_lo[:, dc, :], w_raw[:, dc, :], w_hi[:, dc, :].bitcast(F32), ALU.subtract).then_inc(w_low_done, 1)
            dve.sem_inc(whole_read, 2)
            dve.sem_inc(norms_read, 2)

            def low(n, kind, i):
                j = at[kind, i]
                dve.wait_ge(turned, NJ * n + j + 1)
                dve.wait_ge(high_done, NJ * n + j + 1 + TB)
                b = turn[j % TB]
                if kind == "x":
                    if i >= 2:
                        dve.wait_ge(acc_full, 3 * ST * n + 3 * (i - 1))
                    dve.tensor_tensor(x_lo[:, i % 2, :], b[:], x_hi[:, i % 2, :].bitcast(F32), ALU.subtract).then_inc(low_done, 1)
                else:
                    g = i % DC
                    dve.wait_ge(parts_stored[i % 4], 64 * n + 32 * (i // 4) + 32)
                    dve.scalar_tensor_tensor(part_lo[:, i % 4, :], b[:], scales[:, i // DC, g:g + 1],
                                             part_hi[:, i % 4, :].bitcast(F32), ALU.mult, ALU.subtract).then_inc(low_done, 1)

            SMALL = 2 * 2 * ST

            def measure(n, st, i):
                dve.wait_ge(acc_full, 3 * ST * n + 3 * st + i + 1)
                k = 2 * (2 * st + i)
                dve.bn_stats(stats[:], acc[i][:]).then_inc(vstat, 1)
                dve.wait_ge(vstat, SMALL * n + k + 3)
                dve.nop(nofuse=True)
                dve.bn_aggr(mv[:, i, :], stats[:]).then_inc(vstat, 1)
                dve.wait_ge(vstat, SMALL * n + k + 4)
                dve.tensor_scalar(veps[:, i:i + 1], mv[:, i, 1:2], QK_EPS, None, ALU.add).then_inc(var_ready, 1)

            def apply(n, st, i):
                dve.wait_ge(rstd_ready, 2 * ST * n + 2 * st + i + 1)
                dve.tensor_scalar(normed[i][:, st, :], acc[i][:], mv[:, i, 0:1], rstd[:, i:i + 1],
                                  ALU.subtract, ALU.mult).then_inc(qk_normed, 1)

            def whole(n, w):
                dve.wait_ge(float_ready, 6 * n + w + 1)
                dve.tensor_reduce(whole_max[:, w, bass.ds(n, 1)], wq_f[:, w % 2, :], AX.X, ALU.max,
                                  apply_absolute_value=True).then_inc(whole_read, 1)

            with dve.Fori(0, NCH) as n:
                low(n, "x", 0)
                whole(n, 0)
                for st in range(ST):
                    measure(n, st, 0)
                    if st + 1 < ST:
                        low(n, "x", st + 1)
                    apply(n, st, 0)
                    measure(n, st, 1)
                    whole(n, st + 1)
                    apply(n, st, 1)
                whole(n, 5)
                for i in range(2 * DC):
                    low(n, "qk", i)
                for i in range(2):
                    dve.wait_ge(norms_done, 2 * DC * n + DC * (i + 1))
                    dve.tensor_reduce(norm_max[:, i, bass.ds(n, 1)], norms[i][:], AX.X, ALU.max).then_inc(norms_read, 1)
            dve.wait_ge(norms_read, 2 + 2 * NCH)
            dve.wait_ge(whole_read, 2 + 6 * NCH)
            dve.tensor_reduce(norm_top[:], norm_max[:], AX.X, ALU.max).then_inc(fin, 1)
            dve.tensor_reduce(checks[:, 1:2], whole_max[:], AX.XY, ALU.max).then_inc(fin, 1)
            dve.wait_ge(fin, 2)
            dve.tensor_tensor(checks[:, 0:1], norm_top[:, 0:1], norm_top[:, 1:2], ALU.mult).then_inc(fin, 1)
            dve.wait_ge(fin_pool, 2)
            dve.tensor_scalar(flags_f[:, 0:1], checks_all[:, 0:1], BOUND * BOUND, None, ALU.is_gt).then_inc(fin, 1)
            dve.tensor_scalar(flags_f[:, 1:2], checks_all[:, 1:2], WHOLE, None, ALU.is_gt).then_inc(fin, 1)
            dve.wait_ge(fin, 5)
            dve.tensor_copy(keep["flags"][:], flags_f[:]).then_inc(fin, 1)


def attend(nc, dr, keep):
    LAG = 2
    PB = 6
    RING = 3
    steps = [(ch, kb) for ch in range(NCH) for kb in range(ST * (ch + 1))]
    NS = len(steps)
    first = [steps.index((ch, 0)) for ch in range(NCH)]
    last = [steps.index((ch, ST * ch + ST - 1)) for ch in range(NCH)]
    Q_CREDIT = 2 * (NS - last[NCH - 2])
    V_CREDIT = NS - first[NCH - 1]
    A_CREDIT = PB

    def cut(t):
        ch, kb = steps[t]
        return max(0, kb - ST * ch) * P

    def diagonal(t):
        return steps[t][1] >= ST * steps[t][0]

    def by_pe(t):
        ch, kb = steps[t]
        return ch == 0 or kb == 0 or kb >= ST * ch + 2 or kb % 8 == 5

    adds = [t for t in range(NS) if not by_pe(t)]
    NA = len(adds)
    NM = sum(diagonal(t) for t in range(NS))

    def adds_before(t):
        return adds_before(t + NS) - NA if t < 0 else sum(a < t for a in adds)

    def masks_before(t):
        return sum(diagonal(x) for x in range(t))

    with ExitStack() as c:
        sb = lambda n, s, d=F32: c.enter_context(nc.sbuf_tensor(n, s, d))
        sem = lambda n: c.enter_context(nc.semaphore(n))
        kstk = sb("kstk", [P, HG, S], F32R)
        qstk = sb("qstk", [P, 2, HG, CH], F32R)
        values = sb("values", [P, KB, P])
        probs = sb("probs", [P, PB, HG, CH])
        total = sb("total", [P, 2, HG, CH])
        ones = sb("ones", [P, HD])
        ctx_out = sb("ctx_out", [P, 2, CH])
        sums_out = sb("sums_out", [P, 2, CH])
        score = [c.enter_context(nc.psum_tensor(f"score{i}", [P, 2, CH], F32)) for i in range(RING)]
        ctx = c.enter_context(nc.psum_tensor("ctx_acc", [P, CH], F32))
        sums = c.enter_context(nc.psum_tensor("sums_acc", [P, CH], F32))

        k_in = [sem(f"k_in{j}") for j in range(NCH)]
        v_in = [sem(f"v_in{j}") for j in range(NCH)]
        q_in = [sem(f"q_in{b}") for b in range(2)]
        ones_ready = sem("ones_ready")
        scored = sem("scored")
        exped = sem("exped")
        masked = sem("masked")
        valued = sem("valued")
        added = sem("added")
        ctx_taken = sem("ctx_taken")
        sums_taken = sem("sums_taken")
        ctx_stored = [sem(f"ctx_stored{b}") for b in range(2)]
        g_in = sem("g_in")
        g_scored = sem("g_scored")
        g_copied = sem("g_copied")
        g_masked = sem("g_masked")
        g_read = sem("g_read")
        g_top = sem("g_top")
        g_turned = sem("g_turned")
        g_split = sem("g_split")
        g_out = sem("g_out")
        g_ident = sem("g_ident")
        block = c.enter_context(nc.Block())

        units = [(ch, h, qt, kc) for ch in range(NCH) for h in range(HG) for qt in range(ST) for kc in range(ch + 1)]
        NU = len(units)
        edges = [u for u, (ch, _, _, kc) in enumerate(units) if kc == ch]
        g_copy = total[:, 0, 0:2, :]
        g_part = total[:, 1, 0, 0:NCH]
        g_max = total[:, 1, 1, 0:P]
        g_idt = total[:, 1, 2, 0:P]
        g_hi = probs[:, 0, 0, 0:P].bitcast(F32R)
        g_lo = probs[:, 0, 1, 0:P].bitcast(F32R)
        g_full = probs[:, 0, 2, 0:P]

        def k_load(sp, g, j, s):
            for r, src in enumerate(("k_hi", "k_lo", "k_hi")):
                sp.dma_start(kstk[r * HD:(r + 1) * HD, :, j * CH:(j + 1) * CH].bitcast(F32),
                             dr[src].rearrange("(g h r) s -> g r h s", h=HG, r=HD)[bass.ds(g, 1), :, :, j * CH:(j + 1) * CH]
                             .rearrange("g r h s -> (g r) h s")).then_inc(s, 16)

        def q_load(sp, g, ch, b, s):
            for r, src in enumerate(("q_hi", "q_hi", "q_lo")):
                sp.dma_start(qstk[r * HD:(r + 1) * HD, b, :, :].bitcast(F32),
                             dr[src].rearrange("(g h r) s -> g r h s", h=HG, r=HD)[bass.ds(g, 1), :, :, ch * CH:(ch + 1) * CH]
                             .rearrange("g r h s -> (g r) h s")).then_inc(s, 16)
            sp.dma_start(qstk[3 * HD:ROWS, b, :, :].bitcast(F32),
                         dr["shift"].rearrange("a (g h) s -> a g h s", h=HG)[:, bass.ds(g, 1), :, ch * CH:(ch + 1) * CH]
                         .rearrange("a g h s -> a (g h) s")).then_inc(s, 16)

        @block.sync
        def _(sp):
            general = sp.value_load(keep["flags"][0:1, 0:1], min_val=0, max_val=1)
            with sp.If(general):
                with sp.Fori(0, NG) as g:
                    sp.wait_ge(g_split, g + 1)
                    sp.nop(nofuse=True)
                    for j in range(NCH):
                        k_load(sp, g, j, g_in)
                    for ch in range(NCH):
                        done = [u for u, x in enumerate(units) if x[0] < ch]
                        if ch:
                            sp.wait_ge(g_scored, NU * g + len(done))
                            sp.nop(nofuse=True)
                        q_load(sp, g, ch, 0, g_in)
                    sp.wait_ge(g_split, g + 2)
                    sp.nop(nofuse=True)
                    for a, part in ((0, g_hi), (1, g_lo)):
                        sp.dma_start(dr["shift"].rearrange("a (g h) (t q) -> a g (h t) q", h=HG, q=P)[a][bass.ds(g, 1)]
                                     .rearrange("g x q -> (g x) q"), part.bitcast(F32)).then_inc(g_out, 16)
                    sp.wait_ge(g_out, 32 * g + 32)
                    sp.nop(nofuse=True)
            with sp.Fori(0, NG) as g:
                def load(kind, j):
                    if kind == "q":
                        end = last[j - 2] + 1 if j >= 2 else last[NCH - 2 + j] + 1 - NS
                        sp.wait_ge(scored, 2 * NS * g + 2 * end + Q_CREDIT)
                        sp.nop(nofuse=True)
                        q_load(sp, g, j, j % 2, q_in[j % 2])
                        return
                    end = first[NCH - 1] + ST * (j + 1) - NS
                    sp.wait_ge(scored, 2 * NS * g + 2 * end + Q_CREDIT)
                    sp.nop(nofuse=True)
                    k_load(sp, g, j, k_in[j])
                    sp.wait_ge(valued, NS * g + end + V_CREDIT)
                    sp.nop(nofuse=True)
                    sp.dma_start(values[:, j * ST:(j + 1) * ST, :],
                                 dr["v"].rearrange("(b p) (g d) -> p b g d", p=P, d=P)[:, j * ST:(j + 1) * ST, bass.ds(g, 1), :]
                                 .rearrange("p b g d -> p b (g d)")).then_inc(v_in[j], 16)
                load("q", 0)
                load("kv", 0)
                load("kv", 1)
                load("q", 1)
                for j in range(2, NCH):
                    load("kv", j)
                for ch in range(2, NCH):
                    load("q", ch)

        @block.gpsimd
        def _(pool):
            general = pool.value_load(keep["flags"][0:1, 0:1], min_val=0, max_val=1)
            with pool.If(general):
                pool.memset(g_idt, 0.0).then_inc(g_ident, 1)
                pool.wait_ge(g_ident, 1)
                pool.affine_select(out=g_idt, in_=g_idt, compare_op=ALU.not_equal, fill=1.0, base=0,
                                   pattern=[[-1, P]], channel_multiplier=1).then_inc(g_ident, 1)
                with pool.Fori(0, NG) as g:
                    for e, u in enumerate(edges):
                        qt = units[u][2]
                        pool.wait_ge(g_copied, len(edges) * g + e + 1)
                        pool.nop(nofuse=True)
                        pool.affine_select(out=g_copy[:, e % 2, :], in_=g_copy[:, e % 2, :], compare_op=ALU.is_ge,
                                           fill=-3.0e38, base=qt * P, pattern=[[-1, CH]], channel_multiplier=1)\
                            .then_inc(g_masked, 1)
            with pool.Fori(0, NG) as g:
                for t in range(NS):
                    if diagonal(t):
                        pool.wait_ge(exped, 2 * NS * g + 2 * t + 2 + RING)
                        view = probs[:, t % PB, :, cut(t):cut(t) + P]
                        pool.nop(nofuse=True)
                        pool.affine_select(out=view, in_=view, compare_op=ALU.is_ge, fill=0.0, base=0,
                                           pattern=[[0, HG], [1, P]], channel_multiplier=-1).then_inc(masked, 1)

        @block.tensor
        def _(pe):
            general = pe.value_load(keep["flags"][0:1, 0:1], min_val=0, max_val=1)
            pe.wait_ge(ones_ready, 2)
            with pe.If(general):
                pe.sem_inc(g_read, 2)
                with pe.Fori(0, NG) as g:
                    for u, (ch, h, qt, kc) in enumerate(units):
                        if (h, qt, kc) == (0, 0, 0):
                            pe.wait_ge(g_in, 16 * ((3 + 1) * NCH + 3 * NCH) * g + 16 * (3 * NCH + 4 * (ch + 1)))
                        pe.wait_ge(g_read, NU * g + u + 1)
                        pe.matmul(score[u % 2][:, 0, :], qstk[0:ROWS, 0, h, qt * P:(qt + 1) * P],
                                  kstk[0:ROWS, h, kc * CH:(kc + 1) * CH], start=True, stop=True).then_inc(g_scored, 1)
                    pe.wait_ge(g_ident, 2)
                    pe.wait_ge(g_top, len(edges) * (g + 1))
                    pe.transpose(score[2][:, 0, 0:P], g_max, g_idt).then_inc(g_turned, 1)
                    pe.wait_ge(g_split, g + 2)
            pe.sem_inc(scored, Q_CREDIT)
            pe.sem_inc(valued, V_CREDIT)

            def scores(g, t):
                ch, kb = steps[t]
                if kb == 0:
                    pe.wait_ge(q_in[ch % 2], 64 * (NCH // 2) * g + 64 * (ch // 2 + 1))
                if kb == ST * ch:
                    pe.wait_ge(k_in[ch], 48 * g + 48)
                for p in range(2):
                    u = 2 * t + p
                    pe.wait_ge(exped, 2 * NS * g + u + 1)
                    for i in range(2):
                        h = 2 * p + i
                        ins = pe.matmul(score[u % RING][:, i, cut(t):], kstk[0:ROWS, h, kb * P:(kb + 1) * P],
                                        qstk[0:ROWS, ch % 2, h, cut(t):], start=True, stop=True)
                    ins.then_inc(scored, 1)

            def weigh(g, t):
                ch, kb = steps[t]
                end = kb == ST * ch + ST - 1
                pe.wait_ge(exped, 2 * NS * g + 2 * t + 2 + RING)
                if diagonal(t):
                    pe.wait_ge(masked, NM * g + masks_before(t) + 1)
                if kb == ST * ch:
                    pe.wait_ge(v_in[ch], 16 * g + 16)
                if kb == 0:
                    pe.wait_ge(ctx_taken, NCH * g + ch + 1)
                    pe.wait_ge(sums_taken, NCH * g + ch + 1)
                n0 = cut(t)
                for h in range(HG):
                    ins = pe.matmul(ctx[h * HD:(h + 1) * HD, n0:], values[:, kb, h * HD:(h + 1) * HD],
                                    probs[:, t % PB, h, n0:], start=kb == 0, stop=end)
                if by_pe(t):
                    for h in range(HG):
                        ins = pe.matmul(sums[h * HD:(h + 1) * HD, n0:], ones[:], probs[:, t % PB, h, n0:],
                                        start=kb == 0, stop=end and ch == 0)
                if end and ch:
                    pe.wait_ge(added, NA * g + adds_before(t) + A_CREDIT)
                    for h in range(HG):
                        ins = pe.matmul(sums[h * HD:(h + 1) * HD, :], ones[:], total[:, ch % 2, h, :],
                                        start=False, stop=True)
                ins.then_inc(valued, 1)

            with pe.Fori(0, NG) as g:
                for t in range(NS + LAG):
                    if t < NS:
                        scores(g, t)
                    if t >= LAG:
                        weigh(g, t - LAG)

        @block.scalar
        def _(act):
            general = act.value_load(keep["flags"][0:1, 0:1], min_val=0, max_val=1)
            with act.If(general):
                with act.Fori(0, NG) as g:
                    for e, u in enumerate(edges):
                        act.wait_ge(g_scored, NU * g + u + 1)
                        if e >= 2:
                            act.wait_ge(g_top, len(edges) * g + e - 1)
                        act.activation(g_copy[:, e % 2, :], score[u % 2][:, 0, :], ACT.Copy).then_inc(g_copied, 1)
            act.sem_inc(exped, RING)
            for b in range(2):
                act.sem_inc(ctx_stored[b], 32)

            def take_ctx(g, ch):
                b = ch % 2
                act.wait_ge(valued, NS * g + last[ch] + 1 + V_CREDIT)
                act.wait_ge(ctx_stored[b], 32 * (NCH // 2) * g + 32 * (ch // 2) + 32)
                act.activation(ctx_out[:, b, :], ctx[:], ACT.Copy).then_inc(ctx_taken, 1)
                act.wait_ge(ctx_taken, NCH * g + ch + 2)
                act.dma_start(dr["ctx"].rearrange("(g r) s -> g r s", r=P)[bass.ds(g, 1), :, ch * CH:(ch + 1) * CH]
                              .rearrange("g r s -> (g r) s"), ctx_out[:, b, :]).then_inc(ctx_stored[b], 16)
                act.wait_ge(sums_taken, NCH * g + ch + 2)
                act.dma_start(dr["sums"].rearrange("(g h) s -> g h s", h=HG)[bass.ds(g, 1), :, ch * CH:(ch + 1) * CH]
                              .rearrange("g h s -> (g h) s"), sums_out[0:P:HD, b, :]).then_inc(ctx_stored[b], 16)

            with act.Fori(0, NG) as g:
                for t in range(NS):
                    act.wait_ge(valued, NS * g + t - PB + 1 + V_CREDIT)
                    act.wait_ge(added, NA * g + adds_before(t - PB + 1) + A_CREDIT)
                    for p in range(2):
                        u = 2 * t + p
                        act.wait_ge(scored, 2 * NS * g + u + 1 + Q_CREDIT)
                        act.activation(probs[:, t % PB, 2 * p:2 * p + 2, cut(t):], score[u % RING][:, :, cut(t):],
                                       ACT.Exp).then_inc(exped, 1)
                    for ch in range(NCH - 1):
                        if t == last[ch] + LAG:
                            take_ctx(g, ch)
                take_ctx(g, NCH - 1)
            for b in range(2):
                act.wait_ge(ctx_stored[b], 32 * (NCH // 2) * NG + 32)

        @block.vector
        def _(dve):
            general = dve.value_load(keep["flags"][0:1, 0:1], min_val=0, max_val=1)
            dve.memset(ones[:], 1.0).then_inc(ones_ready, 1)
            dve.memset(kstk[3 * HD:P, :, :].bitcast(F32), 1.0).then_inc(ones_ready, 1)
            dve.sem_inc(g_split, 1)
            with dve.If(general):
                with dve.Fori(0, NG) as g:
                    for u, (ch, h, qt, kc) in enumerate(units):
                        if kc < ch:
                            dve.wait_ge(g_scored, NU * g + u + 1)
                            dve.tensor_reduce(g_part[:, kc:kc + 1], score[u % 2][:, 0, :], AX.X, ALU.max).then_inc(g_read, 1)
                        else:
                            e = edges.index(u)
                            dve.wait_ge(g_masked, len(edges) * g + e + 1)
                            dve.tensor_reduce(g_part[:, kc:kc + 1], g_copy[:, e % 2, :], AX.X, ALU.max).then_inc(g_read, 1)
                            dve.wait_ge(g_read, NU * g + u + 1 + 2)
                            col = h * KB + ch * ST + qt
                            dve.tensor_reduce(g_max[:, col:col + 1], g_part[:, 0:ch + 1], AX.X, ALU.max).then_inc(g_top, 1)
                    dve.wait_ge(g_turned, g + 1)
                    dve.tensor_scalar(g_full, score[2][:, 0, 0:P], -1.0, None, ALU.mult).then_inc(g_ident, 1)
                    dve.wait_ge(g_ident, 2 + 2 * g + 1)
                    dve.tensor_copy(g_hi, g_full).then_inc(g_ident, 1)
                    dve.wait_ge(g_ident, 2 + 2 * g + 2)
                    dve.tensor_tensor(g_lo, g_full, g_hi.bitcast(F32), ALU.subtract).then_inc(g_split, 1)
            dve.sem_inc(added, A_CREDIT)
            dve.sem_inc(ctx_taken, 1)
            dve.sem_inc(sums_taken, 1)

            def take_sums(g, ch):
                dve.wait_ge(valued, NS * g + last[ch] + 1 + V_CREDIT)
                dve.wait_ge(ctx_stored[ch % 2], 32 * (NCH // 2) * g + 32 * (ch // 2) + 32)
                dve.tensor_copy(sums_out[:, ch % 2, :], sums[:]).then_inc(sums_taken, 1)

            with dve.Fori(0, NG) as g:
                for t in range(NS):
                    ch, kb = steps[t]
                    if not by_pe(t) and kb > 1:
                        dve.wait_ge(exped, 2 * NS * g + 2 * t + 2 + RING)
                        if diagonal(t):
                            dve.wait_ge(masked, NM * g + masks_before(t) + 1)
                        now = probs[:, t % PB, :, cut(t):]
                        if kb == 2:
                            end = last[ch - 2] + 1 if ch >= 3 else 0
                            dve.wait_ge(valued, NS * g + end + V_CREDIT)
                            dve.tensor_tensor(total[:, ch % 2, :, :], probs[:, (t - 1) % PB, :, :], now, ALU.add).then_inc(added, 2)
                        else:
                            dve.wait_ge(added, NA * g + adds_before(t) + A_CREDIT)
                            dve.tensor_tensor(total[:, ch % 2, :, cut(t):], total[:, ch % 2, :, cut(t):], now, ALU.add).then_inc(added, 1)
                    for done in range(NCH - 1):
                        if t == last[done] + LAG:
                            take_sums(g, done)
                take_sums(g, NCH - 1)


def finish(nc, io, dr, keep):
    HALF = 2
    HC = HALF * P
    full = [("ic", i) for i in range(8)] + [("o", 0), ("ic", 8), ("ic", 9), ("o", 1), ("ic", 10), ("ic", 11), ("ic", 12),
                                            ("t", 0), ("ic", 13), ("ic", 14), ("t", 1), ("ic", 15)]
    short = [x for x in full if x[0] == "ic"]
    head = [("o", 0), ("o", 1), ("t", 0), ("t", 1)]
    NJ, NHEAD = len(full), len(head)
    FREE = 2

    with ExitStack() as c:
        sb = lambda n, s, d=F32: c.enter_context(nc.sbuf_tensor(n, s, d))
        sem = lambda n: c.enter_context(nc.semaphore(n))
        wg = sb("wg_sb", [P, IC, D], F32R)
        wu = sb("wu_sb", [P, IC, D], F32R)
        wd = sb("wd_sb", [P, IC, D], F32R)
        ow_hi = sb("ow_hi", [P, NG, D], F32R)
        ow_lo = sb("ow_lo", [P, NG, D], F32R)
        xt_hi = sb("xt_hi", [P, 2, DC, CH], F32R)
        xt_lo = sb("xt_lo", [P, 2, DC, CH], F32R)
        x1 = sb("x1", [P, 2, ST, D])
        ctx_in = sb("ctx_in", [P, NG, HC])
        inv_in = sb("inv_in", [P, NG, HC])
        x_in = sb("x_res", [P, HALF, D])
        cp_hi = sb("cp_hi", [P, NG, HC], F32R)
        cp_lo = sb("cp_lo", [P, NG, HC], F32R)
        hidden = sb("hidden", [P, 2, CH])
        h_hi = sb("h_hi", [P, 2, CH], F32R)
        h_lo = sb("h_lo", [P, 2, CH], F32R)
        y_raw = sb("y_raw", [P, ST, D])
        down_scale = sb("down_scale_sb", [P, D])
        gate_scale = sb("gate_scale_sb", [P, IC])
        up_scale = sb("up_scale_sb", [P, IC])
        ident = sb("ident3", [P, P])
        minus_half = sb("minus_half3", [P, 1])
        stats = sb("stats3", [P, 2, 6])
        mv = sb("mv3", [P, 2, ST, 2])
        veps = sb("veps3", [P, 2, ST])
        rstd = sb("rstd3", [P, 2, ST])
        ow_raw = y_raw
        sums_flat = hidden[:, 0, :]
        inv_flat = hidden[:, 1, :]

        slot = [[c.enter_context(nc.psum_tensor(f"slot{s}{b}", [P, CH], F32)) for b in range(2)] for s in range(2)]
        y = [c.enter_context(nc.psum_tensor(f"y{st}", [P, D], F32)) for st in range(ST)]

        w_in = [sem(f"w_in{i}") for i in range(IC)]
        ow_in = sem("ow_in")
        ow_high = sem("ow_high")
        ow_low = sem("ow_low")
        sums_in = sem("sums_in")
        inv_done = sem("inv_done")
        inv_stored = sem("inv_stored")
        small_in = sem("small_in")
        ident_zero = sem("ident_zero")
        ident_ready = sem("ident_ready3")
        half_ready = sem("half_ready")
        half_in = sem("half_in")
        half_used = sem("half_used")
        c_scaled = sem("c_scaled")
        c_high = sem("c_high")
        c_ready = sem("c_ready")
        slot_full = sem("slot_full")
        slot_free = sem("slot_free")
        high_ready = sem("high_ready")
        gated = sem("gated")
        h_made = sem("h_made")
        h_high = sem("h_high")
        h_ready = sem("h_ready")
        downed = sem("downed")
        y_taken = sem("y_taken")
        out_stored = [sem(f"out_stored{b}") for b in range(2)]
        summed = [sem(f"summed{k}") for k in range(2)]
        measured = [sem(f"measured{k}") for k in range(2)]
        averaged = [sem(f"averaged{k}") for k in range(2)]
        var_ready = [sem(f"var_ready3{k}") for k in range(2)]
        rooted = [sem(f"rooted{k}") for k in range(2)]
        normed = [sem(f"normed{k}") for k in range(2)]
        block = c.enter_context(nc.Block())

        def start(n):
            return NHEAD + NJ * n

        def t_end(n):
            return NHEAD if isinstance(n, int) and n == 0 else start(n - 1) + full.index(("t", 1)) + 1

        def over_chunks(engine, body):
            body(0, 0, False, True, 0)
            with engine.Fori(0, NCH // 2 - 1) as i:
                body(i * 2 + 1, 1, True, True, i)
                body(i * 2 + 2, 0, True, True, i + 1)
            body(NCH - 1, 1, True, False, NCH // 2 - 1)

        def half_load(sp, n, h):
            sp.wait_ge(half_used, HALF * n + h + 1)
            for to, src in ((ctx_in, dr["ctx"].rearrange("(g r) s -> r g s", r=P)),):
                sp.dma_start(to[:], src[:, :, bass.ds(n * CH + h * HC, HC)]).then_inc(half_in, 16)
            for g in range(NG):
                for hh in range(HG):
                    row = dr["inverse"][g * HG + hh:g * HG + hh + 1, bass.ds(n * CH + h * HC, HC)]
                    sp.dma_start(inv_in[hh * HD:(hh + 1) * HD, g, :], row.to_broadcast([HD, HC])).then_inc(half_in, 16)
            sp.dma_start(x_in[:], io["x"].rearrange("(m t p) d -> m p t d", t=HALF, p=P)[bass.ds(n * 2 + h, 1)]
                         .rearrange("m p t d -> (m p) t d")).then_inc(half_in, 16)

        HALF_IN = 16 * (2 + HEADS)

        @block.sync
        def _(sp):
            sp.dma_start(sums_flat, dr["sums"].rearrange("h (u s) -> (h u) s", s=CH)).then_inc(sums_in, 16)
            sp.dma_start(ow_raw[:], io["out_w"].rearrange("(g r) e -> r g e", r=P)).then_inc(ow_in, 16)
            with nc.allow_non_contiguous_dma(reason="scales as columns"):
                sp.dma_start(gate_scale[:], io["gate_scale"].rearrange("(c p) -> p c", p=P)).then_inc(small_in, 16)
                sp.dma_start(up_scale[:], io["up_scale"].rearrange("(c p) -> p c", p=P)).then_inc(small_in, 16)
            sp.dma_start(down_scale[:], io["down_scale"].rearrange("(a h) -> a h", a=1).to_broadcast([P, D])).then_inc(small_in, 16)
            sp.wait_ge(inv_done, 1)
            sp.dma_start(dr["inverse"].rearrange("h (u s) -> (h u) s", s=CH), inv_flat).then_inc(inv_stored, 16)
            sp.wait_ge(inv_stored, 16)
            half_load(sp, 0, 0)
            for i in range(2):
                for to, src in ((wg, "wg"), (wu, "wu"), (wd, "wd")):
                    sp.dma_start(to[:, i, :].bitcast(F32), dr[src][i]).then_inc(w_in[i], 16)
            half_load(sp, 0, 1)
            for i in range(2, IC):
                for to, src in ((wg, "wg"), (wu, "wu"), (wd, "wd")):
                    sp.dma_start(to[:, i, :].bitcast(F32), dr[src][i]).then_inc(w_in[i], 16)

            def store(n, par, st):
                sp.wait_ge(normed[1], ST * n + st + 1)
                sp.nop(nofuse=True)
                sp.dma_start(io["out"].rearrange("(m p) d -> m p d", p=P)[bass.ds(n * ST + st, 1)]
                             .rearrange("m p d -> (m p) d"), x1[:, par, st, :]).then_inc(out_stored[par], 16)

            def body(n, par, before, after, pairs):
                if before:
                    for st in range(ST):
                        store(n - 1, 1 - par, st)
                if after:
                    half_load(sp, n + 1, 0)
                    half_load(sp, n + 1, 1)

            over_chunks(sp, body)
            for st in range(ST):
                store(NCH - 1, 1, st)
            for b in range(2):
                sp.wait_ge(out_stored[b], 16 * ST * (NCH // 2 + 1))

        @block.gpsimd
        def _(pool):
            pool.memset(ident[:], 0.0).then_inc(ident_zero, 1)
            pool.wait_ge(ident_zero, 1)
            pool.affine_select(out=ident[:], in_=ident[:], compare_op=ALU.not_equal, fill=1.0, base=0,
                               pattern=[[-1, P]], channel_multiplier=1).then_inc(ident_ready, 1)
            pool.wait_ge(half_ready, 1)

            def root(k, n, st):
                pool.wait_ge(var_ready[k], ST * n + st + 1)
                pool.tensor_tensor(rstd[:, k, st:st + 1], veps[:, k, st:st + 1], minus_half[:], ALU.pow).then_inc(rooted[k], 1)

            def body(n, par, before, after, pairs):
                if before:
                    for st in range(ST):
                        root(1, n - 1, st)
                if after:
                    for st in range(ST):
                        root(0, n + 1, st)

            for st in range(ST):
                root(0, 0, st)
            over_chunks(pool, body)
            for st in range(ST):
                root(1, NCH - 1, st)

        @block.tensor
        def _(pe):
            wide = pe.value_load(keep["flags"][0:1, 1:2], min_val=0, max_val=1)
            pe.sem_inc(slot_free, FREE)
            pe.wait_ge(ident_ready, 1)

            def program(v):
                def project_out(j, pos, n, h):
                    pe.wait_ge(slot_free, j + 1)
                    pe.wait_ge(c_ready, HALF * n + h + 1)
                    for q in range(HALF):
                        first = True
                        for g in range(NG):
                            for a, w in ((cp_hi, ow_hi), (cp_hi, ow_lo), (cp_lo, ow_hi)):
                                ins = pe.matmul(slot[pos % 2][q][:], a[:, g, q * P:(q + 1) * P], w[:, g, :],
                                                start=first, stop=g == NG - 1 and a is cp_lo)
                                first = False
                    ins.then_inc(slot_full, 1)

                def transpose(j, pos, n, par, p):
                    pe.wait_ge(slot_free, j + 1)
                    pe.wait_ge(normed[0], ST * n + ST)
                    for q in range(2):
                        dc = 2 * p + q
                        for st in range(ST):
                            ins = pe.transpose(slot[pos % 2][q][:, st * P:(st + 1) * P],
                                               x1[:, par, st, dc * P:(dc + 1) * P], ident[:])
                    ins.then_inc(slot_full, 1)

                def gate_up(j, pos, n, par, i, first_chunk):
                    pe.wait_ge(slot_free, j + 1)
                    if i == 0:
                        pe.wait_ge(slot_free, t_end(n) + FREE)
                    if first_chunk:
                        pe.wait_ge(w_in[i], 48)
                    for q, w in enumerate((wg, wu)):
                        for dc in range(DC):
                            for a, x in enumerate((xt_hi, xt_lo)):
                                ins = pe.matmul(slot[pos % 2][q][:], v(w[:, i, dc * P:(dc + 1) * P]), v(x[:, par, dc, :]),
                                                start=dc == 0 and a == 0, stop=dc == DC - 1 and a == 1)
                    ins.then_inc(slot_full, 1)

                def down(n, i, first_chunk):
                    pe.wait_ge(h_ready, IC * n + i + 1 + 2)
                    if i == 0 and not first_chunk:
                        pe.wait_ge(y_taken, ST * n)
                    for st in range(ST):
                        for a, x in enumerate((h_hi, h_lo)):
                            ins = pe.matmul(y[st][:], v(x[:, i % 2, st * P:(st + 1) * P]), v(wd[:, i, :]),
                                            start=i == 0 and a == 0, stop=i == IC - 1 and a == 1)
                    ins.then_inc(downed, 1)

                def body(n, par, before, after, pairs):
                    for pos, (kind, i) in enumerate(full if after else short):
                        j = start(n) + pos
                        if kind == "o":
                            project_out(j, pos, n + 1, i)
                        elif kind == "t":
                            transpose(j, pos, n + 1, 1 - par, i)
                        else:
                            gate_up(j, pos, n, par, i, not before)
                            if i:
                                down(n, i - 1, not before)
                            elif before:
                                down(n - 1, IC - 1, False)

                for pos, (kind, i) in enumerate(head):
                    if kind == "o":
                        if i == 0:
                            pe.wait_ge(ow_low, 1)
                        project_out(pos, pos, 0, i)
                    else:
                        transpose(pos, pos, 0, 0, i)
                over_chunks(pe, body)
                down(NCH - 1, IC - 1, False)

            with pe.If(wide):
                program(lambda ap: ap.bitcast(F32))
            with pe.Else():
                program(lambda ap: ap)

        @block.scalar
        def _(act):
            act.wait_ge(ow_in, 16)
            act.activation(ow_hi[:], ow_raw[:], ACT.Copy).then_inc(ow_high, 1)
            act.wait_ge(small_in, 48)

            def high(j, pos, n, par, p):
                act.wait_ge(slot_full, j + 1)
                for q in range(2):
                    act.activation(xt_hi[:, par, 2 * p + q, :], slot[pos % 2][q][:], ACT.Copy).then_inc(high_ready, 1)

            def body(n, par, before, after, pairs):
                for pos, (kind, i) in enumerate(full if after else short):
                    j = start(n) + pos
                    if kind == "t":
                        high(j, pos, n + 1, 1 - par, i)
                    elif kind == "ic":
                        act.wait_ge(slot_full, j + 1)
                        act.wait_ge(h_ready, IC * n + i + 1)
                        act.activation(hidden[:, i % 2, :], slot[pos % 2][0][:], ACT.Silu,
                                       scale=gate_scale[:, i:i + 1]).then_inc(gated, 1)

            for pos, (kind, i) in enumerate(head):
                if kind == "t":
                    high(pos, pos, 0, 0, i)
            over_chunks(act, body)

        @block.vector
        def _(dve):
            dve.memset(minus_half[:], -0.5).then_inc(half_ready, 1)
            dve.sem_inc(half_used, 1)
            dve.sem_inc(h_ready, 2)
            for b in range(2):
                dve.sem_inc(out_stored[b], 16 * ST)
            dve.wait_ge(sums_in, 16)
            dve.reciprocal(inv_flat, sums_flat).then_inc(inv_done, 1)
            dve.wait_ge(ow_high, 1)
            dve.tensor_tensor(ow_lo[:], ow_raw[:], ow_hi[:].bitcast(F32), ALU.subtract).then_inc(ow_low, 1)
            dve.wait_ge(inv_stored, 16)

            def context(n, h):
                k = HALF * n + h
                dve.wait_ge(half_in, HALF_IN * (k + 1))
                dve.tensor_tensor(ctx_in[:], ctx_in[:], inv_in[:], ALU.mult).then_inc(c_scaled, 1)
                dve.wait_ge(c_scaled, k + 1)
                dve.tensor_copy(cp_hi[:], ctx_in[:]).then_inc(c_high, 1)
                dve.wait_ge(c_high, k + 1)
                dve.tensor_tensor(cp_lo[:], ctx_in[:], cp_hi[:].bitcast(F32), ALU.subtract).then_inc(c_ready, 1)

            def norm_begin(k, n, par, st, eps):
                rows = x1[:, par, st, :]
                at = ST * n + st + 1
                dve.wait_ge(summed[k], at)
                dve.bn_stats(stats[:, k, :], rows).then_inc(measured[k], 1)
                dve.wait_ge(measured[k], at)
                dve.nop(nofuse=True)
                dve.bn_aggr(mv[:, k, st, :], stats[:, k, :]).then_inc(averaged[k], 1)
                dve.wait_ge(averaged[k], at)
                dve.tensor_scalar(veps[:, k, st:st + 1], mv[:, k, st, 1:2], eps, None, ALU.add).then_inc(var_ready[k], 1)

            def norm_end(k, n, par, st):
                rows = x1[:, par, st, :]
                dve.wait_ge(rooted[k], ST * n + st + 1)
                dve.tensor_scalar(rows, rows, mv[:, k, st, 0:1], rstd[:, k, st:st + 1], ALU.subtract, ALU.mult)\
                   .then_inc(normed[k], 1)

            def residual(j, pos, n, par, h, stored):
                dve.wait_ge(slot_full, j + 1)
                if h == 0:
                    dve.wait_ge(out_stored[par], stored)
                for q in range(HALF):
                    ins = dve.tensor_tensor(x1[:, par, h * HALF + q, :], slot[pos % 2][q][:], x_in[:, q, :], ALU.add)
                    ins.then_inc(summed[0], 1)
                dve.wait_ge(summed[0], ST * n + h * HALF + HALF)
                dve.sem_inc(slot_free, 1)
                dve.sem_inc(half_used, 1)
                for q in range(HALF):
                    norm_begin(0, n, par, h * HALF + q, LN_EPS)

            def low(j, pos, n, par, p):
                for q in range(2):
                    dc = 2 * p + q
                    dve.wait_ge(high_ready, DC * n + dc + 1)
                    ins = dve.tensor_tensor(xt_lo[:, par, dc, :], slot[pos % 2][q][:], xt_hi[:, par, dc, :].bitcast(F32),
                                            ALU.subtract)
                ins.then_inc(slot_free, 1)

            def make_hidden(j, pos, n, i):
                k = IC * n + i + 1
                dve.wait_ge(gated, k)
                hid = hidden[:, i % 2, :]
                dve.scalar_tensor_tensor(hid, slot[pos % 2][1][:], up_scale[:, i:i + 1], hid, ALU.mult, ALU.mult)\
                   .then_inc(slot_free, 1)
                dve.wait_ge(slot_free, j + 1 + FREE)
                if not (isinstance(n, int) and n == 0 and i < 2):
                    dve.wait_ge(downed, k - 2)
                dve.tensor_copy(h_hi[:, i % 2, :], hid).then_inc(h_high, 1)
                dve.wait_ge(h_high, k)
                dve.tensor_tensor(h_lo[:, i % 2, :], hid, h_hi[:, i % 2, :].bitcast(F32), ALU.subtract).then_inc(h_ready, 1)

            def take_y(n, par):
                dve.wait_ge(downed, IC * (n + 1))
                for st in range(ST):
                    dve.tensor_tensor(y_raw[:, st, :], y[st][:], down_scale[:], ALU.mult).then_inc(y_taken, 1)

            def add_y(n, par, st):
                dve.wait_ge(y_taken, ST * n + st + 1)
                dve.tensor_tensor(x1[:, par, st, :], x1[:, par, st, :], y_raw[:, st, :], ALU.add).then_inc(summed[1], 1)
                norm_begin(1, n, par, st, LN_EPS)

            def body(n, par, before, after, pairs):
                waiting = []
                for pos, (kind, i) in enumerate(full if after else short):
                    j = start(n) + pos
                    if kind == "o":
                        residual(j, pos, n + 1, 1 - par, i, 16 * ST * (pairs + par + 1))
                        waiting += [(0, n + 1, 1 - par, i * HALF + q) for q in range(HALF)]
                    elif kind == "t":
                        low(j, pos, n + 1, 1 - par, i)
                    else:
                        make_hidden(j, pos, n, i)
                        for w in waiting:
                            norm_end(*w)
                        waiting = []
                        if before and i == 0:
                            take_y(n - 1, 1 - par)
                        if before and 1 <= i <= ST:
                            add_y(n - 1, 1 - par, i - 1)
                            waiting = [(1, n - 1, 1 - par, i - 1)]
                        if after and i in (6, 8):
                            context(n + 1, i // 8)

            context(0, 0)
            for pos, (kind, i) in enumerate(head):
                if kind == "o":
                    residual(pos, pos, 0, 0, i, 16 * ST)
                    if i == 0:
                        context(0, 1)
                    else:
                        for st in range(ST):
                            norm_end(0, 0, 0, st)
                else:
                    low(pos, pos, 0, 0, i)
            over_chunks(dve, body)
            take_y(NCH - 1, 1)
            for st in range(ST):
                add_y(NCH - 1, 1, st)
                if st:
                    norm_end(1, NCH - 1, 1, st - 1)
            norm_end(1, NCH - 1, 1, ST - 1)


NAMES = ["L0_attn_x", "L0_attn_Wqkv", "L0_attn_q_ln_scale", "L0_attn_k_ln_scale", "L0_attn_out_W",
         "L0_ffn_gate_w", "L0_ffn_gate_scale", "L0_ffn_up_w", "L0_ffn_up_scale", "L0_ffn_down_w",
         "L0_ffn_down_scale"]
SHORT = ["x", "wqkv", "q_scale", "k_scale", "out_w", "gate_w", "gate_scale", "up_w", "up_scale",
         "down_w", "down_scale"]


def build(nc, io):
    def scratch(name, shape, dt):
        return nc.dram_tensor(name, shape, dt, kind="Internal").ap()

    dr = {
        "q_hi": scratch("q_hi", (D, S), F32), "q_lo": scratch("q_lo", (D, S), F32),
        "k_hi": scratch("k_hi", (D, S), F32), "k_lo": scratch("k_lo", (D, S), F32),
        "v": scratch("v_rows", (S, D), F32),
        "shift": scratch("shift", (2, HEADS, S), F32),
        "ctx": scratch("ctx", (D, S), F32),
        "sums": scratch("sums", (HEADS, S), F32),
        "inverse": scratch("inverse", (HEADS, S), F32),
        "wg": scratch("wg", (IC, P, D), F32), "wu": scratch("wu", (IC, P, D), F32),
        "wd": scratch("wd", (IC, P, D), F32),
    }
    with ExitStack() as c:
        keep = {"flags": c.enter_context(nc.sbuf_tensor("flags", [P, 2], I32))}
        project(nc, io, dr, keep)
        attend(nc, dr, keep)
        finish(nc, io, dr, keep)


def kernel(**inputs):
    import numpy as np
    import concourse.bacc as bacc
    from concourse.bass_utils import run_bass_kernel_spmd

    nc = bacc.Bacc("TRN2", target_bir_lowering=False, num_devices=1)
    arrays, io = {}, {}
    for name, short in zip(NAMES, SHORT):
        a = np.ascontiguousarray(inputs[name])
        if short == "x":
            a = a.reshape(S, D)
        arrays[f"in_{short}"] = a
        io[short] = nc.dram_tensor(f"in_{short}", a.shape, mybir.dt.from_np(a.dtype), kind="ExternalInput").ap()
    io["out"] = nc.dram_tensor("out_y", (S, D), F32, kind="ExternalOutput").ap()
    build(nc, io)
    r = run_bass_kernel_spmd(nc, [arrays], core_ids=[0])
    return r.results[0]["out_y"].reshape(1, S, D)
```

```python
from contextlib import ExitStack

import concourse.bass as bass
from concourse import mybir

F32 = mybir.dt.float32
F32R = mybir.dt.float32r
BF16 = mybir.dt.bfloat16
I32 = mybir.dt.int32
ALU = mybir.AluOpType
ACT = mybir.ActivationFunctionType
AX = mybir.AxisListType

P = 128
S = 4096
D = 512
HEADS = 16
HD = D // HEADS
INNER = 2048
CH = 512
NCH = S // CH
ST = CH // P
DC = D // P
HG = P // HD
NG = HEADS // HG
IC = INNER // P
KB = S // P
QK_EPS = 1e-6
LN_EPS = 1e-5
ZERO_POINT = 128.0
BOUND = 60.0
WHOLE = 4096.0
ROWS = 3 * HD + 2


def over_chunks(engine, body):
    body(0, -1, 0, False, True, 0)
    with engine.Fori(0, NCH // 2 - 1) as i:
        body(i * 2 + 1, i * 2, 1, True, True, i)
        body(i * 2 + 2, i * 2 + 1, 0, True, True, i + 1)
    body(NCH - 1, NCH - 2, 1, True, False, NCH // 2 - 1)


def project(nc, io, dr, keep):
    ACCS = 4
    NU, NJ = 3 * ST, 2 * DC
    usual = [(st, m) for st in range(ST) for m in range(3)]
    final = [(st, m) for st in range(ST) for m in range(2)] + [(st, 2) for st in range(ST)]

    x_parts = {0: (0,), 1: (1, 2), 2: (3,)}

    def plan(before, after):
        units = usual if after else final
        jobs = [[] for _ in units]
        if before:
            for i in range(NJ):
                jobs[2 + i if after else 1 + i * 6 // (NJ - 1)].append((False, i))
        if not after:
            for i in range(NJ):
                jobs[8 + i // 3].append((True, i))
        return list(zip(units, jobs))

    with ExitStack() as c:
        sb = lambda n, s, d=F32: c.enter_context(nc.sbuf_tensor(n, s, d))
        sem = lambda n: c.enter_context(nc.semaphore(n))
        x_raw = sb("x_raw", [P, DC, CH])
        x_hi = sb("x_hi", [P, 2, DC, CH], F32R)
        x_lo = sb("x_lo", [P, 2, DC, CH], F32R)
        w_raw = sb("w_raw", [P, DC, 3 * D])
        w_hi = sb("w_hi", [P, DC, 3 * D], F32R)
        w_lo = sb("w_lo", [P, DC, 3 * D], F32R)
        normed = sb("normed_qk", [P, 2, 2, ST, D])
        part_hi = sb("part_hi", [P, 4, CH], F32R)
        part_lo = sb("part_lo", [P, 4, CH], F32R)
        squares = sb("squares", [P, 2, CH], BF16)
        v_out = sb("v_out", [P, 2, D])
        ident = sb("ident", [P, P])
        select = sb("select", [P, HD], BF16)
        stats = sb("stats", [P, 6])
        mv = sb("mv", [P, 2, 2])
        veps = sb("veps", [P, 2])
        rstd = sb("rstd", [P, 2])
        minus_half = sb("minus_half", [P, 1])
        quarter = sb("quarter", [P, DC])
        scales = sb("scales", [P, 2, DC])
        mix = sb("mix", [P, DC])
        mix_root = sb("mix_root", [P, DC])
        norm_max = sb("norm_max", [P, 2, NCH])
        norm_top = sb("norm_top", [P, 2])
        check = sb("check", [P, 1])
        check_all = sb("check_all", [P, 1])
        flag_f = sb("flag_f", [P, 1])
        zeros = sb("zeros", [P, 2 * HEADS * S // P])

        turn = [c.enter_context(nc.psum_tensor(f"turn{i}", [P, 512], F32)) for i in range(2)]
        acc = [c.enter_context(nc.psum_tensor(f"acc{i}", [P, 512], F32)) for i in range(ACCS)]
        norms = [c.enter_context(nc.psum_tensor(f"norms_{n}", [P, 512], F32)) for n in "qk"]

        x_in = [sem(f"x_in{dc}") for dc in range(DC)]
        x_high = sem("x_high")
        x_low = sem("x_low")
        wqkv_in = [sem(f"wqkv_in{dc}") for dc in range(DC)]
        w_high_done = sem("w_high_done")
        w_low_done = sem("w_low_done")
        ident_ready = sem("ident_ready")
        scales_ready = sem("scales_ready")
        dconst = sem("dconst")
        scales_in = sem("scales_in")
        turned = sem("turned")
        high_done = sem("high_done")
        low_done = sem("low_done")
        acc_full = sem("acc_full")
        v_taken = sem("v_taken")
        v_stored = [sem(f"v_stored{i}") for i in range(2)]
        vstat = sem("vstat")
        var_ready = sem("var_ready")
        rstd_ready = sem("rstd_ready")
        qk_normed = sem("qk_normed")
        sq_ready = sem("sq_ready")
        norms_done = sem("norms_done")
        norms_read = sem("norms_read")
        parts_stored = [sem(f"parts_stored{i}") for i in range(4)]
        zero_stored = sem("zero_stored")
        fin = sem("fin")
        fin_pool = sem("fin_pool")
        block = c.enter_context(nc.Block())

        xs = io["x_t"].rearrange("(c p) s -> c p s", p=P)

        @block.sync
        def _(sp):
            def load_x(n, dc):
                sp.dma_start(x_raw[:, dc, :], xs[dc][:, bass.ds(n * CH, CH)]).then_inc(x_in[dc], 16)

            for dc in range(DC):
                sp.dma_start(w_raw[:, dc, :], io["wqkv"][dc * P:(dc + 1) * P, :]).then_inc(wqkv_in[dc], 16)
                load_x(0, dc)
            sp.dma_start(scales[:, 0, :], io["q_scale"]).then_inc(scales_in, 16)
            sp.dma_start(scales[:, 1, :], io["k_scale"]).then_inc(scales_in, 16)
            sp.wait_ge(dconst, 1)
            sp.dma_start(dr["shift"].rearrange("a h (u s) -> (a h u) s", u=4), zeros[:]).then_inc(zero_stored, 16)
            for s_, k in ((parts_stored, 32), (v_stored, 16)):
                for one in s_:
                    sp.sem_inc(one, k)

            def body(n, c, par, before, after, half):
                for dc in range(DC if after else 0):
                    sp.wait_ge(x_low, DC * n + dc + 1)
                    sp.nop(nofuse=True)
                    load_x(n + 1, dc)
                for (st, m), jobs in plan(before, after):
                    if m == 2:
                        sp.wait_ge(v_taken, ST * n + st + 1)
                        sp.nop(nofuse=True)
                        sp.dma_start(dr["v"].rearrange("(t p) d -> t p d", p=P)[bass.ds(n * ST + st, 1)].rearrange("t p d -> (t p) d"),
                                     v_out[:, st % 2, :]).then_inc(v_stored[st % 2], 16)
                    for own, i in jobs:
                        o = n if own else c
                        sp.wait_ge(high_done, NJ * o + i + 1 + 2)
                        sp.nop(nofuse=True)
                        sp.wait_ge(low_done, NJ * o + i + 1 + 2)
                        sp.nop(nofuse=True)
                        g = i % DC
                        for part, to in ((part_hi, ("q_hi", "k_hi")), (part_lo, ("q_lo", "k_lo"))):
                            sp.dma_start(dr[to[i // DC]][g * P:(g + 1) * P, bass.ds(o * CH, CH)], part[:, i % 4, :].bitcast(F32))\
                               .then_inc(parts_stored[i % 4], 16)

            over_chunks(sp, body)
            sp.wait_ge(zero_stored, 16)
            for s_, k in ((parts_stored, 32 + 64 * NCH), (v_stored, 16 + 32 * NCH)):
                for one in s_:
                    sp.wait_ge(one, k)

        @block.gpsimd
        def _(pool):
            pool.memset(ident[:], 0.0).then_inc(fin_pool, 1)
            pool.wait_ge(fin_pool, 1)
            pool.affine_select(out=ident[:], in_=ident[:], compare_op=ALU.not_equal, fill=1.0, base=0,
                               pattern=[[-1, P]], channel_multiplier=1).then_inc(ident_ready, 1)
            pool.wait_ge(dconst, 4)
            pool.tensor_tensor(mix_root[:], mix[:], quarter[:], ALU.pow).then_inc(scales_ready, 1)

            def root(n, st, i):
                pool.wait_ge(var_ready, 2 * ST * n + 2 * st + i + 1)
                pool.tensor_tensor(rstd[:, i:i + 1], veps[:, i:i + 1], minus_half[:], ALU.pow).then_inc(rstd_ready, 1)

            with pool.Fori(0, NCH) as n:
                for st in range(ST):
                    root(n, st, 0)
                    root(n, st, 1)
            pool.wait_ge(fin, 2)
            pool.partition_all_reduce(check_all[:], check[:], P, bass.bass_isa.ReduceOp.max).then_inc(fin_pool, 1)

        @block.tensor
        def _(pe):
            pe.sem_inc(high_done, 2)
            pe.sem_inc(low_done, 2)

            def wait_bank(n, c, units, u):
                if u < ACCS:
                    if isinstance(n, int) and n == 0:
                        return
                    n, (st, m) = c, usual[u - ACCS]
                else:
                    st, m = units[u - ACCS]
                if m == 2:
                    pe.wait_ge(v_taken, ST * n + st + 1)
                else:
                    pe.wait_ge(qk_normed, 2 * ST * n + 2 * st + m + 1)

            def product(bank, par, st, m, dc):
                rows = slice(st * P, (st + 1) * P)
                for a, (x, w) in enumerate(((x_hi, w_hi), (x_hi, w_lo), (x_lo, w_hi))):
                    ins = pe.matmul(bank[:], x[:, par, dc, rows], w[:, dc, m * D:(m + 1) * D],
                                    start=dc == 0 and a == 0, stop=dc == DC - 1 and a == 2)
                return ins

            def unit(n, c, par, units, u):
                st, m = units[u]
                wait_bank(n, c, units, u)
                if u == 0:
                    pe.wait_ge(x_low, DC * n + DC)
                for dc in range(DC):
                    ins = product(acc[u % ACCS], par, st, m, dc)
                ins.then_inc(acc_full, 1)

            def job(o, par, i):
                pe.wait_ge(high_done, NJ * o + i + 1)
                pe.wait_ge(low_done, NJ * o + i + 1)
                pe.wait_ge(qk_normed, 2 * ST * o + 2 * ST)
                for st in range(ST):
                    g = i % DC
                    ins = pe.transpose(turn[i % 2][:, st * P:(st + 1) * P], normed[:, par, i // DC, st, g * P:(g + 1) * P], ident[:])
                ins.then_inc(turned, 1)

            def norm(o, i):
                pe.wait_ge(sq_ready, NJ * o + i + 1)
                if i % DC == 0:
                    pe.wait_ge(norms_read, 2 * o + i // DC + 1)
                g = i % DC
                pe.matmul(norms[i // DC][g * HD:(g + 1) * HD, :], select[:], squares[:, i % 2, :],
                          start=True, stop=True).then_inc(norms_done, 1)

            def body(n, c, par, before, after, half):
                steps = plan(before, after)
                units = [x for x, _ in steps]
                due = []
                for u, (_, jobs) in enumerate(steps):
                    if before or u >= 3:
                        unit(n, c, par, units, u)
                    elif u == 0:
                        for dc in range(DC):
                            pe.wait_ge(w_low_done, dc + 1)
                            pe.wait_ge(x_low, dc + 1)
                            for m in range(3):
                                ins = product(acc[m], par, 0, m, dc)
                                if dc == DC - 1:
                                    ins.then_inc(acc_full, 1)
                    for own, i in jobs:
                        o = n if own else c
                        job(o, par if own else 1 - par, i)
                        if len(due) > 1:
                            norm(*due.pop(0))
                        due.append((o, i))
                    if not jobs and due:
                        norm(*due.pop(0))
                while due:
                    norm(*due.pop(0))

            pe.wait_ge(ident_ready, 1)
            pe.wait_ge(dconst, 3)
            over_chunks(pe, body)

        @block.scalar
        def _(act):
            def high_x(n, par, dc):
                act.wait_ge(x_in[dc], 16 * n + 16)
                act.activation(x_hi[:, par, dc, :], x_raw[:, dc, :], ACT.Copy).then_inc(x_high, 1)

            for dc in range(DC):
                act.wait_ge(wqkv_in[dc], 16)
                act.activation(w_hi[:, dc, :], w_raw[:, dc, :], ACT.Copy).then_inc(w_high_done, 1)
                high_x(0, 0, dc)
            act.wait_ge(scales_ready, 2)
            act.sem_inc(norms_done, 2)

            def high(o, i):
                act.wait_ge(turned, NJ * o + i + 1)
                b = turn[i % 2]
                act.wait_ge(parts_stored[i % 4], 64 * o + 32 * (i // 4) + 32)
                act.wait_ge(norms_done, NJ * o + i + 1)
                g = i % DC
                act.activation(squares[:, i % 2, :], b[:], ACT.Square, scale=mix_root[:, g:g + 1]).then_inc(sq_ready, 1)
                act.activation(part_hi[:, i % 4, :], b[:], ACT.Copy, scale=scales[:, i // DC, g:g + 1]).then_inc(high_done, 1)

            def take_v(n, u, st):
                act.wait_ge(acc_full, NU * n + u + 1)
                act.wait_ge(v_stored[st % 2], 32 * n + 16 * (st // 2) + 16)
                act.activation(v_out[:, st % 2, :], acc[u % ACCS][:], ACT.Copy).then_inc(v_taken, 1)

            def body(n, c, par, before, after, half):
                for u, ((st, m), jobs) in enumerate(plan(before, after)):
                    if m == 1 and after and st in x_parts:
                        if before and st == 0:
                            act.wait_ge(acc_full, NU * n)
                        for dc in x_parts[st]:
                            high_x(n + 1, 1 - par, dc)
                    if m == 2:
                        take_v(n, u, st)
                    for own, i in jobs:
                        high(n if own else c, i)

            over_chunks(act, body)

        @block.vector
        def _(dve):
            dve.memset(minus_half[:], -0.5)
            dve.memset(quarter[:], 0.25)
            dve.memset(zeros[:], 0.0).then_inc(dconst, 1)
            dve.memset(select[:], 0.0).then_inc(dconst, 1)
            dve.wait_ge(dconst, 2)
            for h in range(HG):
                ins = dve.memset(select[h * HD:(h + 1) * HD, h:h + 1], 1.0)
            ins.then_inc(dconst, 1)

            def low_x(n, par, dc):
                dve.wait_ge(x_high, DC * n + dc + 1)
                dve.tensor_tensor(x_lo[:, par, dc, :], x_raw[:, dc, :], x_hi[:, par, dc, :].bitcast(F32), ALU.subtract).then_inc(x_low, 1)

            for dc in range(DC):
                dve.wait_ge(w_high_done, dc + 1)
                dve.tensor_tensor(w_lo[:, dc, :], w_raw[:, dc, :], w_hi[:, dc, :].bitcast(F32), ALU.subtract).then_inc(w_low_done, 1)
                low_x(0, 0, dc)
            dve.wait_ge(scales_in, 32)
            root_hd = float(HD) ** -0.5
            dve.tensor_tensor(mix[:], scales[:, 0, :], scales[:, 1, :], ALU.mult).then_inc(vstat, 1)
            dve.wait_ge(vstat, 1)
            dve.tensor_scalar(mix_root[:], mix[:], root_hd, None, ALU.mult).then_inc(vstat, 1)
            dve.wait_ge(vstat, 2)
            dve.tensor_tensor(mix[:], mix_root[:], mix_root[:], ALU.mult).then_inc(dconst, 1)
            dve.tensor_scalar(scales[:, 0, :], scales[:, 0, :], root_hd, None, ALU.mult).then_inc(scales_ready, 1)
            dve.sem_inc(norms_read, 2)

            def low(o, i):
                g = i % DC
                dve.wait_ge(high_done, NJ * o + i + 1 + 2)
                dve.scalar_tensor_tensor(part_lo[:, i % 4, :], turn[i % 2][:], scales[:, i // DC, g:g + 1],
                                         part_hi[:, i % 4, :].bitcast(F32), ALU.mult, ALU.subtract).then_inc(low_done, 1)

            def measure(n, u, st, i):
                dve.wait_ge(acc_full, NU * n + u + 1)
                k = 2 * (2 * st + i) + 2
                dve.bn_stats(stats[:], acc[u % ACCS][:]).then_inc(vstat, 1)
                dve.wait_ge(vstat, 4 * ST * n + k + 1)
                dve.nop(nofuse=True)
                dve.bn_aggr(mv[:, i, :], stats[:]).then_inc(vstat, 1)
                dve.wait_ge(vstat, 4 * ST * n + k + 2)
                dve.tensor_scalar(veps[:, i:i + 1], mv[:, i, 1:2], QK_EPS, None, ALU.add).then_inc(var_ready, 1)

            def apply(n, par, u, st, i):
                dve.wait_ge(rstd_ready, 2 * ST * n + 2 * st + i + 1)
                dve.tensor_scalar(normed[:, par, i, st, :], acc[u % ACCS][:], mv[:, i, 0:1], rstd[:, i:i + 1],
                                  ALU.subtract, ALU.mult).then_inc(qk_normed, 1)

            def top(o, i):
                dve.wait_ge(norms_done, NJ * o + DC * (i + 1) + 2)
                dve.tensor_reduce(norm_max[:, i, bass.ds(o, 1)], norms[i][:], AX.X, ALU.max).then_inc(norms_read, 1)

            def body(n, c, par, before, after, half):
                steps = plan(before, after)
                waiting = []
                tops = []
                for u, ((st, m), jobs) in enumerate(steps):
                    if m < 2:
                        measure(n, u, st, m)
                    for w in waiting:
                        apply(*w)
                    waiting = [(n, par, u, st, m)] if m < 2 else []
                    if m == 2 and after and st in x_parts:
                        for dc in x_parts[st]:
                            low_x(n + 1, 1 - par, dc)
                    for t in tops:
                        if t[2] <= u:
                            top(*t[:2])
                    tops = [t for t in tops if t[2] > u]
                    for own, i in jobs:
                        low(n if own else c, i)
                        if i % DC == DC - 1:
                            tops.append((n if own else c, i // DC, u + 3))
                for t in tops:
                    top(*t[:2])

            over_chunks(dve, body)
            dve.wait_ge(norms_read, 2 + 2 * NCH)
            dve.tensor_reduce(norm_top[:], norm_max[:], AX.X, ALU.max).then_inc(fin, 1)
            dve.wait_ge(fin, 1)
            dve.tensor_tensor(check[:], norm_top[:, 0:1], norm_top[:, 1:2], ALU.mult).then_inc(fin, 1)
            dve.wait_ge(fin_pool, 2)
            dve.tensor_scalar(flag_f[:], check_all[:], BOUND * BOUND, None, ALU.is_gt).then_inc(fin, 1)
            dve.wait_ge(fin, 3)
            dve.tensor_copy(keep["flags"][:, 0:1], flag_f[:]).then_inc(fin, 1)


def attend(nc, io, dr, keep):
    LAG = 2
    PB = 6
    RING = 3
    steps = [(ch, kb) for ch in range(NCH) for kb in range(ST * (ch + 1))]
    NS = len(steps)
    first = [steps.index((ch, 0)) for ch in range(NCH)]
    last = [steps.index((ch, ST * ch + ST - 1)) for ch in range(NCH)]
    Q_CREDIT = 2 * (NS - last[NCH - 2])
    V_CREDIT = NS - first[NCH - 1]
    A_CREDIT = PB

    def cut(t):
        ch, kb = steps[t]
        return max(0, kb - ST * ch) * P

    def diagonal(t):
        return steps[t][1] >= ST * steps[t][0]

    def by_pe(t):
        ch, kb = steps[t]
        return ch == 0 or kb == 0 or kb >= ST * ch + 2 or kb % 8 == 5

    WT = 3 * IC // NG
    tiles_after = {ch: range(2 * (ch - 1), 2 * ch) for ch in range(1, NCH - 1)}
    assert sum(map(len, tiles_after.values())) == WT

    adds = [t for t in range(NS) if not by_pe(t)]
    NA = len(adds)
    NM = sum(diagonal(t) for t in range(NS))

    def adds_before(t):
        return adds_before(t + NS) - NA if t < 0 else sum(a < t for a in adds)

    def masks_before(t):
        return sum(diagonal(x) for x in range(t))

    with ExitStack() as c:
        sb = lambda n, s, d=F32: c.enter_context(nc.sbuf_tensor(n, s, d))
        sem = lambda n: c.enter_context(nc.semaphore(n))
        kstk = sb("kstk", [P, HG, S], F32R)
        qstk = sb("qstk", [P, 2, HG, CH], F32R)
        values = sb("values", [P, KB, P])
        probs = sb("probs", [P, PB, HG, CH])
        total = sb("total", [P, 2, HG, CH])
        ones = sb("ones", [P, HD])
        ctx_out = sb("ctx_out", [P, 2, CH])
        sums_out = sb("sums_out", [P, 2, CH])
        wq_int = sb("wq_int", [P, 2, D], I32)
        wq_f = sb("wq_f", [P, 2, D])
        wq_square = sb("wq_square", [P, D])
        whole = sb("whole", [P, D])
        check = sb("check_w", [P, 1])
        check_all = sb("check_w_all", [P, 1])
        flag_f = sb("flag_wide", [P, 1])
        score = [c.enter_context(nc.psum_tensor(f"score{i}", [P, 2, CH], F32)) for i in range(RING)]
        ctx = c.enter_context(nc.psum_tensor("ctx_acc", [P, CH], F32))
        sums = c.enter_context(nc.psum_tensor("sums_acc", [P, CH], F32))

        k_in = [sem(f"k_in{j}") for j in range(NCH)]
        v_in = [sem(f"v_in{j}") for j in range(NCH)]
        q_in = [sem(f"q_in{b}") for b in range(2)]
        ones_ready = sem("ones_ready")
        scored = sem("scored")
        exped = sem("exped")
        masked = sem("masked")
        valued = sem("valued")
        added = sem("added")
        ctx_taken = sem("ctx_taken")
        sums_taken = sem("sums_taken")
        ctx_stored = [sem(f"ctx_stored{b}") for b in range(2)]
        int_in = [sem(f"int_in{b}") for b in range(2)]
        floated = sem("floated")
        wq_squared = sem("wq_squared")
        whole_done = sem("whole_done")
        wq_stored = [sem(f"wq_stored{b}") for b in range(2)]
        whole_zero = sem("whole_zero")
        checked = sem("checked")
        checked_all = sem("checked_all")
        g_in = sem("g_in")
        g_scored = sem("g_scored")
        g_copied = sem("g_copied")
        g_masked = sem("g_masked")
        g_read = sem("g_read")
        g_top = sem("g_top")
        g_turned = sem("g_turned")
        g_split = sem("g_split")
        g_out = sem("g_out")
        g_ident = sem("g_ident")
        block = c.enter_context(nc.Block())

        units = [(ch, h, qt, kc) for ch in range(NCH) for h in range(HG) for qt in range(ST) for kc in range(ch + 1)]
        NU = len(units)
        edges = [u for u, (ch, _, _, kc) in enumerate(units) if kc == ch]
        g_copy = total[:, 0, 0:2, :]
        g_part = total[:, 1, 0, 0:NCH]
        g_max = total[:, 1, 1, 0:P]
        g_idt = total[:, 1, 2, 0:P]
        g_hi = probs[:, 0, 0, 0:P].bitcast(F32R)
        g_lo = probs[:, 0, 1, 0:P].bitcast(F32R)
        g_full = probs[:, 0, 2, 0:P]

        def k_load(sp, g, j, s):
            for r, src in enumerate(("k_hi", "k_lo", "k_hi")):
                sp.dma_start(kstk[r * HD:(r + 1) * HD, :, j * CH:(j + 1) * CH].bitcast(F32),
                             dr[src].rearrange("(g h r) s -> g r h s", h=HG, r=HD)[bass.ds(g, 1), :, :, j * CH:(j + 1) * CH]
                             .rearrange("g r h s -> (g r) h s")).then_inc(s, 16)

        def q_load(sp, g, ch, b, s):
            for r, src in enumerate(("q_hi", "q_hi", "q_lo")):
                sp.dma_start(qstk[r * HD:(r + 1) * HD, b, :, :].bitcast(F32),
                             dr[src].rearrange("(g h r) s -> g r h s", h=HG, r=HD)[bass.ds(g, 1), :, :, ch * CH:(ch + 1) * CH]
                             .rearrange("g r h s -> (g r) h s")).then_inc(s, 16)
            sp.dma_start(qstk[3 * HD:ROWS, b, :, :].bitcast(F32),
                         dr["shift"].rearrange("a (g h) s -> a g h s", h=HG)[:, bass.ds(g, 1), :, ch * CH:(ch + 1) * CH]
                         .rearrange("a g h s -> a (g h) s")).then_inc(s, 16)

        @block.sync
        def _(sp):
            general = sp.value_load(keep["flags"][0:1, 0:1], min_val=0, max_val=1)
            with sp.If(general):
                with sp.Fori(0, NG) as g:
                    sp.wait_ge(g_split, g + 1)
                    sp.nop(nofuse=True)
                    for j in range(NCH):
                        k_load(sp, g, j, g_in)
                    for ch in range(NCH):
                        done = [u for u, x in enumerate(units) if x[0] < ch]
                        if ch:
                            sp.wait_ge(g_scored, NU * g + len(done))
                            sp.nop(nofuse=True)
                        q_load(sp, g, ch, 0, g_in)
                    sp.wait_ge(g_split, g + 2)
                    sp.nop(nofuse=True)
                    for a, part in ((0, g_hi), (1, g_lo)):
                        sp.dma_start(dr["shift"].rearrange("a (g h) (t q) -> a g (h t) q", h=HG, q=P)[a][bass.ds(g, 1)]
                                     .rearrange("g x q -> (g x) q"), part.bitcast(F32)).then_inc(g_out, 16)
                    sp.wait_ge(g_out, 32 * g + 32)
                    sp.nop(nofuse=True)
            with sp.Fori(0, NG) as g:
                def load(kind, j):
                    if kind == "q":
                        end = last[j - 2] + 1 if j >= 2 else last[NCH - 2 + j] + 1 - NS
                        sp.wait_ge(scored, 2 * NS * g + 2 * end + Q_CREDIT)
                        sp.nop(nofuse=True)
                        q_load(sp, g, j, j % 2, q_in[j % 2])
                        return
                    end = first[NCH - 1] + ST * (j + 1) - NS
                    sp.wait_ge(scored, 2 * NS * g + 2 * end + Q_CREDIT)
                    sp.nop(nofuse=True)
                    k_load(sp, g, j, k_in[j])
                    sp.wait_ge(valued, NS * g + end + V_CREDIT)
                    sp.nop(nofuse=True)
                    sp.dma_start(values[:, j * ST:(j + 1) * ST, :],
                                 dr["v"].rearrange("(b p) (g d) -> p b g d", p=P, d=P)[:, j * ST:(j + 1) * ST, bass.ds(g, 1), :]
                                 .rearrange("p b g d -> p b (g d)")).then_inc(v_in[j], 16)
                def store(ch):
                    sp.wait_ge(sums_taken, NCH * g + ch + 2)
                    sp.nop(nofuse=True)
                    sp.dma_start(dr["sums"].rearrange("n (g h) s -> n g h s", h=HG)[ch, bass.ds(g, 1), :, :]
                                 .rearrange("g h s -> (g h) s"), sums_out[0:P:HD, ch % 2, :]).then_inc(ctx_stored[ch % 2], 16)
                    sp.wait_ge(ctx_taken, NCH * g + ch + 2)
                    sp.nop(nofuse=True)
                    sp.dma_start(dr["ctx"].rearrange("(g r) s -> g r s", r=P)[bass.ds(g, 1), :, ch * CH:(ch + 1) * CH]
                                 .rearrange("g r s -> (g r) s"), ctx_out[:, ch % 2, :]).then_inc(ctx_stored[ch % 2], 16)

                def load_int(j):
                    sp.wait_ge(floated, WT * g + j + 1)
                    sp.nop(nofuse=True)
                    sp.dma_start(wq_int[:, j % 2, :], io["wq"][bass.ds(g * WT + j, 1)].rearrange("a p x -> (a p) x"))\
                      .then_inc(int_in[j % 2], 16)

                def store_float(j):
                    sp.wait_ge(floated, WT * g + j + 1 + 2)
                    sp.nop(nofuse=True)
                    sp.dma_start(dr["wq"][bass.ds(g * WT + j, 1)].rearrange("a p x -> (a p) x"), wq_f[:, j % 2, :])\
                      .then_inc(wq_stored[j % 2], 16)

                load("q", 0)
                load("kv", 0)
                load("kv", 1)
                load("q", 1)
                load_int(0)
                load_int(1)
                for j in range(2, NCH):
                    load("kv", j)
                for ch in range(2, NCH):
                    load("q", ch)
                    store(ch - 2)
                    for j in tiles_after[ch - 1]:
                        store_float(j)
                        if j + 2 < WT:
                            load_int(j + 2)
                store(NCH - 2)
                store(NCH - 1)
            for b in range(2):
                sp.wait_ge(ctx_stored[b], 32 * (NCH // 2) * NG + 32)
                sp.wait_ge(wq_stored[b], 16 * (WT // 2) * NG + 16)

        @block.gpsimd
        def _(pool):
            general = pool.value_load(keep["flags"][0:1, 0:1], min_val=0, max_val=1)
            with pool.If(general):
                pool.memset(g_idt, 0.0).then_inc(g_ident, 1)
                pool.wait_ge(g_ident, 1)
                pool.affine_select(out=g_idt, in_=g_idt, compare_op=ALU.not_equal, fill=1.0, base=0,
                                   pattern=[[-1, P]], channel_multiplier=1).then_inc(g_ident, 1)
                with pool.Fori(0, NG) as g:
                    for e, u in enumerate(edges):
                        qt = units[u][2]
                        pool.wait_ge(g_copied, len(edges) * g + e + 1)
                        pool.nop(nofuse=True)
                        pool.affine_select(out=g_copy[:, e % 2, :], in_=g_copy[:, e % 2, :], compare_op=ALU.is_ge,
                                           fill=-3.0e38, base=qt * P, pattern=[[-1, CH]], channel_multiplier=1)\
                            .then_inc(g_masked, 1)
            pool.sem_inc(floated, 2)
            pool.sem_inc(whole_done, 2)
            for b in range(2):
                pool.sem_inc(wq_stored[b], 16)
            pool.wait_ge(whole_zero, 1)

            def turn_float(g, j):
                b = j % 2
                pool.wait_ge(int_in[b], 16 * (WT // 2) * g + 16 * (j // 2) + 16)
                pool.wait_ge(wq_stored[b], 16 * (WT // 2) * g + 16 * (j // 2) + 16)
                pool.wait_ge(whole_done, WT * g + j + 1)
                pool.nop(nofuse=True)
                pool.tensor_scalar(wq_f[:, b, :], wq_int[:, b, :], -ZERO_POINT, None, ALU.add).then_inc(floated, 1)
                pool.wait_ge(floated, WT * g + j + 1 + 2)
                pool.wait_ge(whole_done, WT * g + j + 2)
                pool.nop(nofuse=True)
                pool.tensor_tensor(wq_square[:], wq_f[:, b, :], wq_f[:, b, :], ALU.mult).then_inc(wq_squared, 1)
                pool.wait_ge(wq_squared, WT * g + j + 1)
                pool.nop(nofuse=True)
                pool.tensor_tensor(whole[:], whole[:], wq_square[:], ALU.add).then_inc(whole_done, 1)

            with pool.Fori(0, NG) as g:
                for t in range(NS):
                    if diagonal(t):
                        pool.wait_ge(exped, 2 * NS * g + 2 * t + 2 + RING)
                        view = probs[:, t % PB, :, cut(t):cut(t) + P]
                        pool.nop(nofuse=True)
                        pool.affine_select(out=view, in_=view, compare_op=ALU.is_ge, fill=0.0, base=0,
                                           pattern=[[0, HG], [1, P]], channel_multiplier=-1).then_inc(masked, 1)
                    if t in last and last.index(t) in tiles_after:
                        for j in tiles_after[last.index(t)]:
                            turn_float(g, j)
            pool.wait_ge(checked, 1)
            pool.partition_all_reduce(check_all[:], check[:], P, bass.bass_isa.ReduceOp.max).then_inc(checked_all, 1)

        @block.tensor
        def _(pe):
            general = pe.value_load(keep["flags"][0:1, 0:1], min_val=0, max_val=1)
            with pe.If(general):
                pe.wait_ge(ones_ready, 1 + NCH)
                pe.sem_inc(g_read, 2)
                with pe.Fori(0, NG) as g:
                    for u, (ch, h, qt, kc) in enumerate(units):
                        if (h, qt, kc) == (0, 0, 0):
                            pe.wait_ge(g_in, 16 * ((3 + 1) * NCH + 3 * NCH) * g + 16 * (3 * NCH + 4 * (ch + 1)))
                        pe.wait_ge(g_read, NU * g + u + 1)
                        pe.matmul(score[u % 2][:, 0, :], qstk[0:ROWS, 0, h, qt * P:(qt + 1) * P],
                                  kstk[0:ROWS, h, kc * CH:(kc + 1) * CH], start=True, stop=True).then_inc(g_scored, 1)
                    pe.wait_ge(g_ident, 2)
                    pe.wait_ge(g_top, len(edges) * (g + 1))
                    pe.transpose(score[2][:, 0, 0:P], g_max, g_idt).then_inc(g_turned, 1)
                    pe.wait_ge(g_split, g + 2)
            pe.sem_inc(scored, Q_CREDIT)
            pe.sem_inc(valued, V_CREDIT)

            def scores(g, t):
                ch, kb = steps[t]
                if kb == 0:
                    pe.wait_ge(q_in[ch % 2], 64 * (NCH // 2) * g + 64 * (ch // 2 + 1))
                if kb == ST * ch:
                    pe.wait_ge(ones_ready, 1 + ch + 1)
                    pe.wait_ge(k_in[ch], 48 * g + 48)
                for p in range(2):
                    u = 2 * t + p
                    pe.wait_ge(exped, 2 * NS * g + u + 1)
                    for i in range(2):
                        h = 2 * p + i
                        ins = pe.matmul(score[u % RING][:, i, cut(t):], kstk[0:ROWS, h, kb * P:(kb + 1) * P],
                                        qstk[0:ROWS, ch % 2, h, cut(t):], start=True, stop=True)
                    ins.then_inc(scored, 1)

            def weigh(g, t):
                ch, kb = steps[t]
                end = kb == ST * ch + ST - 1
                pe.wait_ge(exped, 2 * NS * g + 2 * t + 2 + RING)
                if diagonal(t):
                    pe.wait_ge(masked, NM * g + masks_before(t) + 1)
                if kb == ST * ch:
                    pe.wait_ge(v_in[ch], 16 * g + 16)
                if kb == 0:
                    pe.wait_ge(ctx_taken, NCH * g + ch + 1)
                    pe.wait_ge(sums_taken, NCH * g + ch + 1)
                n0 = cut(t)
                for h in range(HG):
                    ins = pe.matmul(ctx[h * HD:(h + 1) * HD, n0:], values[:, kb, h * HD:(h + 1) * HD],
                                    probs[:, t % PB, h, n0:], start=kb == 0, stop=end)
                if by_pe(t):
                    for h in range(HG):
                        ins = pe.matmul(sums[h * HD:(h + 1) * HD, n0:], ones[:], probs[:, t % PB, h, n0:],
                                        start=kb == 0, stop=end and ch == 0)
                if end and ch:
                    pe.wait_ge(added, NA * g + adds_before(t) + A_CREDIT)
                    for h in range(HG):
                        ins = pe.matmul(sums[h * HD:(h + 1) * HD, :], ones[:], total[:, ch % 2, h, :],
                                        start=False, stop=True)
                ins.then_inc(valued, 1)

            with pe.Fori(0, NG) as g:
                for t in range(NS + LAG):
                    if t < NS:
                        scores(g, t)
                    if t >= LAG:
                        weigh(g, t - LAG)

        @block.scalar
        def _(act):
            general = act.value_load(keep["flags"][0:1, 0:1], min_val=0, max_val=1)
            with act.If(general):
                with act.Fori(0, NG) as g:
                    for e, u in enumerate(edges):
                        act.wait_ge(g_scored, NU * g + u + 1)
                        if e >= 2:
                            act.wait_ge(g_top, len(edges) * g + e - 1)
                        act.activation(g_copy[:, e % 2, :], score[u % 2][:, 0, :], ACT.Copy).then_inc(g_copied, 1)
            act.sem_inc(exped, RING)

            def take_ctx(g, ch):
                act.wait_ge(valued, NS * g + last[ch] + 1 + V_CREDIT)
                act.wait_ge(ctx_stored[ch % 2], 32 * (NCH // 2) * g + 32 * (ch // 2) + 32)
                act.activation(ctx_out[:, ch % 2, :], ctx[:], ACT.Copy).then_inc(ctx_taken, 1)

            with act.Fori(0, NG) as g:
                for t in range(NS):
                    act.wait_ge(valued, NS * g + t - PB + 1 + V_CREDIT)
                    act.wait_ge(added, NA * g + adds_before(t - PB + 1) + A_CREDIT)
                    for p in range(2):
                        u = 2 * t + p
                        act.wait_ge(scored, 2 * NS * g + u + 1 + Q_CREDIT)
                        act.activation(probs[:, t % PB, 2 * p:2 * p + 2, cut(t):], score[u % RING][:, :, cut(t):],
                                       ACT.Exp).then_inc(exped, 1)
                    for ch in range(NCH - 1):
                        if t == last[ch] + LAG:
                            take_ctx(g, ch)
                take_ctx(g, NCH - 1)

        @block.vector
        def _(dve):
            general = dve.value_load(keep["flags"][0:1, 0:1], min_val=0, max_val=1)
            dve.memset(ones[:], 1.0).then_inc(ones_ready, 1)
            dve.memset(whole[:], 0.0).then_inc(whole_zero, 1)
            for j in range(NCH):
                dve.memset(kstk[3 * HD:P, :, j * CH:(j + 1) * CH].bitcast(F32), 1.0).then_inc(ones_ready, 1)
            dve.sem_inc(g_split, 1)
            with dve.If(general):
                with dve.Fori(0, NG) as g:
                    for u, (ch, h, qt, kc) in enumerate(units):
                        if kc == 0 and u:
                            dve.wait_ge(g_top, len(edges) * g + sum(x < u for x in edges))
                        if kc < ch:
                            dve.wait_ge(g_scored, NU * g + u + 1)
                            dve.tensor_reduce(g_part[:, kc:kc + 1], score[u % 2][:, 0, :], AX.X, ALU.max).then_inc(g_read, 1)
                        else:
                            e = edges.index(u)
                            dve.wait_ge(g_masked, len(edges) * g + e + 1)
                            dve.tensor_reduce(g_part[:, kc:kc + 1], g_copy[:, e % 2, :], AX.X, ALU.max).then_inc(g_read, 1)
                            dve.wait_ge(g_read, NU * g + u + 1 + 2)
                            col = h * KB + ch * ST + qt
                            dve.tensor_reduce(g_max[:, col:col + 1], g_part[:, 0:ch + 1], AX.X, ALU.max).then_inc(g_top, 1)
                    dve.wait_ge(g_turned, g + 1)
                    dve.tensor_scalar(g_full, score[2][:, 0, 0:P], -1.0, None, ALU.mult).then_inc(g_ident, 1)
                    dve.wait_ge(g_ident, 2 + 2 * g + 1)
                    dve.tensor_copy(g_hi, g_full).then_inc(g_ident, 1)
                    dve.wait_ge(g_ident, 2 + 2 * g + 2)
                    dve.tensor_tensor(g_lo, g_full, g_hi.bitcast(F32), ALU.subtract).then_inc(g_split, 1)
            dve.sem_inc(added, A_CREDIT)
            dve.sem_inc(ctx_taken, 1)
            dve.sem_inc(sums_taken, 1)
            for b in range(2):
                dve.sem_inc(ctx_stored[b], 32)

            def take_sums(g, ch):
                dve.wait_ge(valued, NS * g + last[ch] + 1 + V_CREDIT)
                dve.wait_ge(ctx_stored[ch % 2], 32 * (NCH // 2) * g + 32 * (ch // 2) + 32)
                dve.tensor_copy(sums_out[:, ch % 2, :], sums[:]).then_inc(sums_taken, 1)

            with dve.Fori(0, NG) as g:
                for t in range(NS):
                    ch, kb = steps[t]
                    if not by_pe(t) and kb > 1:
                        dve.wait_ge(exped, 2 * NS * g + 2 * t + 2 + RING)
                        if diagonal(t):
                            dve.wait_ge(masked, NM * g + masks_before(t) + 1)
                        now = probs[:, t % PB, :, cut(t):]
                        if kb == 2:
                            end = last[ch - 2] + 1 if ch >= 3 else 0
                            dve.wait_ge(valued, NS * g + end + V_CREDIT)
                            dve.tensor_tensor(total[:, ch % 2, :, :], probs[:, (t - 1) % PB, :, :], now, ALU.add).then_inc(added, 2)
                        else:
                            dve.wait_ge(added, NA * g + adds_before(t) + A_CREDIT)
                            dve.tensor_tensor(total[:, ch % 2, :, cut(t):], total[:, ch % 2, :, cut(t):], now, ALU.add).then_inc(added, 1)
                    for done in range(NCH - 1):
                        if t == last[done] + LAG:
                            take_sums(g, done)
                take_sums(g, NCH - 1)
            dve.wait_ge(whole_done, WT * NG + 2)
            dve.tensor_reduce(check[:], whole[:], AX.X, ALU.max).then_inc(checked, 1)
            dve.wait_ge(checked_all, 1)
            dve.tensor_scalar(flag_f[:], check_all[:], WHOLE * WHOLE, None, ALU.is_gt).then_inc(checked, 1)
            dve.wait_ge(checked, 2)
            dve.tensor_copy(keep["flags"][:, 1:2], flag_f[:]).then_inc(checked, 1)


def finish(nc, io, dr, keep):
    HALF = 2
    HC = HALF * P
    full = [("ic", i) for i in range(9)] + [("o", 0), ("ic", 9), ("ic", 10), ("o", 1), ("ic", 11), ("ic", 12), ("ic", 13),
                                            ("t", 0), ("ic", 14), ("t", 1), ("ic", 15)]
    short = [x for x in full if x[0] == "ic"]
    head = [("o", 0), ("o", 1), ("t", 0), ("t", 1)]
    NJ, NHEAD = len(full), len(head)
    FREE = 2

    with ExitStack() as c:
        sb = lambda n, s, d=F32: c.enter_context(nc.sbuf_tensor(n, s, d))
        sem = lambda n: c.enter_context(nc.semaphore(n))
        wg = sb("wg_sb", [P, IC, D], F32R)
        wu = sb("wu_sb", [P, IC, D], F32R)
        wd = sb("wd_sb", [P, IC, D], F32R)
        ow_hi = sb("ow_hi", [P, NG, D], F32R)
        ow_lo = sb("ow_lo", [P, NG, D], F32R)
        xt_hi = sb("xt_hi", [P, 2, DC, CH], F32R)
        xt_lo = sb("xt_lo", [P, 2, DC, CH], F32R)
        x1 = sb("x1", [P, 2, ST, D])
        ctx_in = sb("ctx_in", [P, 2, NG, HC])
        x_in = sb("x_res", [P, 2, HALF, D])
        cp_hi = sb("cp_hi", [P, NG, HC], F32R)
        cp_lo = sb("cp_lo", [P, NG, HC], F32R)
        hidden = sb("hidden", [P, 2, CH])
        h_hi = sb("h_hi", [P, 2, CH], F32R)
        h_lo = sb("h_lo", [P, 2, CH], F32R)
        y_raw = sb("y_raw", [P, ST, D])
        down_scale = sb("down_scale_sb", [P, D])
        gate_scale = sb("gate_scale_sb", [P, IC])
        up_scale = sb("up_scale_sb", [P, IC])
        ident = sb("ident3", [P, P])
        minus_half = sb("minus_half3", [P, 1])
        stats = sb("stats3", [P, 2, 6])
        mv = sb("mv3", [P, 2, ST, 2])
        veps = sb("veps3", [P, 2, ST])
        rstd = sb("rstd3", [P, 2, ST])
        inv_in = y_raw
        ow_raw = x1[:, 1, :, :]
        sums_flat = hidden[:, 0, :]
        inv_flat = hidden[:, 1, :]

        slot = [[c.enter_context(nc.psum_tensor(f"slot{s}{b}", [P, CH], F32)) for b in range(2)] for s in range(2)]
        y = [c.enter_context(nc.psum_tensor(f"y{st}", [P, D], F32)) for st in range(ST)]

        w_in = [sem(f"w_in{i}") for i in range(IC)]
        ow_in = sem("ow_in")
        ow_high = sem("ow_high")
        ow_low = sem("ow_low")
        small_in = sem("small_in")
        ident_zero = sem("ident_zero")
        ident_ready = sem("ident_ready3")
        half_ready = sem("half_ready")
        half_in = [sem(f"half_in{h}") for h in range(2)]
        half_used = sem("half_used")
        sums_in = [sem(f"sums_in{k}") for k in range(2)]
        inv_done = sem("inv_done")
        inv_stored = [sem(f"inv_stored{k}") for k in range(2)]
        inv_ready = sem("inv_ready")
        c_scaled = sem("c_scaled")
        c_high = sem("c_high")
        c_ready = sem("c_ready")
        slot_full = sem("slot_full")
        slot_free = sem("slot_free")
        high_ready = sem("high_ready")
        gated = sem("gated")
        h_made = sem("h_made")
        h_high = sem("h_high")
        h_ready = sem("h_ready")
        downed = sem("downed")
        y_taken = sem("y_taken")
        out_stored = [sem(f"out_stored{b}") for b in range(2)]
        summed = [sem(f"summed{k}") for k in range(2)]
        measured = [sem(f"measured{k}") for k in range(2)]
        averaged = [sem(f"averaged{k}") for k in range(2)]
        var_ready = [sem(f"var_ready3{k}") for k in range(2)]
        rooted = [sem(f"rooted{k}") for k in range(2)]
        normed = [sem(f"normed{k}") for k in range(2)]
        block = c.enter_context(nc.Block())

        def start(n):
            return NHEAD + NJ * n

        def t_end(n):
            return NHEAD if isinstance(n, int) and n == 0 else start(n - 1) + full.index(("t", 1)) + 1

        def half_load(sp, n, h):
            sp.wait_ge(half_used, HALF * n + h + 1)
            sp.dma_start(ctx_in[:, h, :, :], dr["ctx"].rearrange("(g r) s -> r g s", r=P)[:, :, bass.ds(n * CH + h * HC, HC)])\
              .then_inc(half_in[h], 16)
            sp.dma_start(x_in[:, h, :, :], io["x"].rearrange("(m t p) d -> m p t d", t=HALF, p=P)[bass.ds(n * 2 + h, 1)]
                         .rearrange("m p t d -> (m p) t d")).then_inc(half_in[h], 16)

        def inv_load(sp, n):
            for h in range(HG):
                sp.dma_start(inv_in[h * HD:(h + 1) * HD, :, :],
                             dr["inverse"].rearrange("n (g h) s -> n h g s", h=HG)[bass.ds(n, 1), h, :, :]
                             .to_broadcast([HD, NG, CH])).then_inc(inv_ready, 16)

        FLAT = CH * HEADS // P
        flat_parts = ((0, FLAT), (FLAT, FLAT * NCH))

        @block.sync
        def _(sp):
            for k, (a, b) in enumerate(flat_parts):
                sp.dma_start(sums_flat[:, a:b].rearrange("p (n s) -> p n s", s=FLAT),
                             dr["sums"].rearrange("n h (u s) -> (h u) n s", s=FLAT)[:, a // FLAT:b // FLAT, :]).then_inc(sums_in[k], 16)
            half_load(sp, 0, 0)
            sp.dma_start(ow_raw[:], io["out_w"].rearrange("(g r) e -> r g e", r=P)).then_inc(ow_in, 16)
            sp.dma_start(gate_scale[:], io["gate_scale"]).then_inc(small_in, 16)
            sp.dma_start(up_scale[:], io["up_scale"]).then_inc(small_in, 16)
            sp.dma_start(down_scale[:], io["down_scale"].rearrange("(a h) -> a h", a=1).to_broadcast([P, D])).then_inc(small_in, 16)
            for k, (a, b) in enumerate(flat_parts):
                sp.wait_ge(inv_done, k + 1)
                sp.dma_start(dr["inverse"].rearrange("n h (u s) -> (h u) n s", s=FLAT)[:, a // FLAT:b // FLAT, :],
                             inv_flat[:, a:b].rearrange("p (n s) -> p n s", s=FLAT)).then_inc(inv_stored[k], 16)
            sp.wait_ge(inv_stored[0], 16)
            inv_load(sp, 0)
            half_load(sp, 0, 1)
            sp.wait_ge(inv_stored[1], 16)
            for i in range(2):
                for k, to in enumerate((wg, wu, wd)):
                    sp.dma_start(to[:, i, :].bitcast(F32), dr["wq"][3 * i + k]).then_inc(w_in[i], 16)
            for i in range(2, IC):
                for k, to in enumerate((wg, wu, wd)):
                    sp.dma_start(to[:, i, :].bitcast(F32), dr["wq"][3 * i + k]).then_inc(w_in[i], 16)

            def store(n, par, st):
                sp.wait_ge(normed[1], ST * n + st + 1)
                sp.nop(nofuse=True)
                sp.dma_start(io["out"].rearrange("(m p) d -> m p d", p=P)[bass.ds(n * ST + st, 1)]
                             .rearrange("m p d -> (m p) d"), x1[:, par, st, :]).then_inc(out_stored[par], 16)

            def body(n, c, par, before, after, pairs):
                if after:
                    half_load(sp, n + 1, 0)
                    half_load(sp, n + 1, 1)
                    if before:
                        sp.wait_ge(summed[1], ST * n)
                    else:
                        sp.wait_ge(c_ready, HALF)
                    sp.nop(nofuse=True)
                    inv_load(sp, n + 1)
                if before:
                    for st in range(ST):
                        store(n - 1, 1 - par, st)

            over_chunks(sp, body)
            for st in range(ST):
                store(NCH - 1, 1, st)
            for b in range(2):
                sp.wait_ge(out_stored[b], 16 * ST * (NCH // 2 + 1))

        @block.gpsimd
        def _(pool):
            pool.memset(ident[:], 0.0).then_inc(ident_zero, 1)
            pool.wait_ge(ident_zero, 1)
            pool.affine_select(out=ident[:], in_=ident[:], compare_op=ALU.not_equal, fill=1.0, base=0,
                               pattern=[[-1, P]], channel_multiplier=1).then_inc(ident_ready, 1)
            pool.wait_ge(half_ready, 1)

            def root(k, n, st):
                pool.wait_ge(var_ready[k], ST * n + st + 1)
                pool.tensor_tensor(rstd[:, k, st:st + 1], veps[:, k, st:st + 1], minus_half[:], ALU.pow).then_inc(rooted[k], 1)

            def body(n, c, par, before, after, pairs):
                if before:
                    for st in range(ST):
                        root(1, n - 1, st)
                if after:
                    for st in range(ST):
                        root(0, n + 1, st)

            for st in range(ST):
                root(0, 0, st)
            over_chunks(pool, body)
            for st in range(ST):
                root(1, NCH - 1, st)

        @block.tensor
        def _(pe):
            wide = pe.value_load(keep["flags"][0:1, 1:2], min_val=0, max_val=1)
            pe.sem_inc(slot_free, FREE)
            pe.wait_ge(ident_ready, 1)

            def program(v):
                def project_out(j, pos, n, h):
                    pe.wait_ge(slot_free, j + 1)
                    pe.wait_ge(c_ready, HALF * n + h + 1)
                    for q in range(HALF):
                        first = True
                        for g in range(NG):
                            for a, w in ((cp_hi, ow_hi), (cp_hi, ow_lo), (cp_lo, ow_hi)):
                                ins = pe.matmul(slot[pos % 2][q][:], a[:, g, q * P:(q + 1) * P], w[:, g, :],
                                                start=first, stop=g == NG - 1 and a is cp_lo)
                                first = False
                    ins.then_inc(slot_full, 1)

                def transpose(j, pos, n, par, p):
                    pe.wait_ge(slot_free, j + 1)
                    pe.wait_ge(normed[0], ST * n + ST)
                    for q in range(2):
                        dc = 2 * p + q
                        for st in range(ST):
                            ins = pe.transpose(slot[pos % 2][q][:, st * P:(st + 1) * P],
                                               x1[:, par, st, dc * P:(dc + 1) * P], ident[:])
                    ins.then_inc(slot_full, 1)

                def gate_up(j, pos, n, par, i, first_chunk):
                    pe.wait_ge(slot_free, j + 1)
                    if i == 0:
                        pe.wait_ge(slot_free, t_end(n) + FREE)
                    if first_chunk:
                        pe.wait_ge(w_in[i], 48)
                    for q, w in enumerate((wg, wu)):
                        for dc in range(DC):
                            for a, x in enumerate((xt_hi, xt_lo)):
                                ins = pe.matmul(slot[pos % 2][q][:], v(w[:, i, dc * P:(dc + 1) * P]), v(x[:, par, dc, :]),
                                                start=dc == 0 and a == 0, stop=dc == DC - 1 and a == 1)
                    ins.then_inc(slot_full, 1)

                def down(n, i, first_chunk):
                    pe.wait_ge(h_ready, IC * n + i + 1 + 2)
                    if i == 0 and not first_chunk:
                        pe.wait_ge(y_taken, ST * n)
                    for st in range(ST):
                        for a, x in enumerate((h_hi, h_lo)):
                            ins = pe.matmul(y[st][:], v(x[:, i % 2, st * P:(st + 1) * P]), v(wd[:, i, :]),
                                            start=i == 0 and a == 0, stop=i == IC - 1 and a == 1)
                    ins.then_inc(downed, 1)

                def body(n, c, par, before, after, pairs):
                    for pos, (kind, i) in enumerate(full if after else short):
                        j = start(n) + pos
                        if kind == "o":
                            project_out(j, pos, n + 1, i)
                        elif kind == "t":
                            transpose(j, pos, n + 1, 1 - par, i)
                        else:
                            gate_up(j, pos, n, par, i, not before)
                            if i:
                                down(n, i - 1, not before)
                            elif before:
                                down(n - 1, IC - 1, False)

                for pos, (kind, i) in enumerate(head):
                    if kind == "o":
                        if i == 0:
                            pe.wait_ge(ow_low, 1)
                        project_out(pos, pos, 0, i)
                    else:
                        transpose(pos, pos, 0, 0, i)
                over_chunks(pe, body)
                down(NCH - 1, IC - 1, False)

            with pe.If(wide):
                program(lambda ap: ap.bitcast(F32))
            with pe.Else():
                program(lambda ap: ap)

        @block.scalar
        def _(act):
            act.wait_ge(ow_in, 16)
            act.activation(ow_hi[:], ow_raw[:], ACT.Copy).then_inc(ow_high, 1)
            act.wait_ge(small_in, 48)

            def high(j, pos, n, par, p):
                act.wait_ge(slot_full, j + 1)
                for q in range(2):
                    act.activation(xt_hi[:, par, 2 * p + q, :], slot[pos % 2][q][:], ACT.Copy).then_inc(high_ready, 1)

            def body(n, c, par, before, after, pairs):
                for pos, (kind, i) in enumerate(full if after else short):
                    j = start(n) + pos
                    if kind == "t":
                        high(j, pos, n + 1, 1 - par, i)
                    elif kind == "ic":
                        act.wait_ge(slot_full, j + 1)
                        act.wait_ge(h_ready, IC * n + i + 1)
                        act.activation(hidden[:, i % 2, :], slot[pos % 2][0][:], ACT.Silu,
                                       scale=gate_scale[:, i:i + 1]).then_inc(gated, 1)

            for pos, (kind, i) in enumerate(head):
                if kind == "t":
                    high(pos, pos, 0, 0, i)
            over_chunks(act, body)

        @block.vector
        def _(dve):
            dve.memset(minus_half[:], -0.5).then_inc(half_ready, 1)
            dve.sem_inc(half_used, 2)
            dve.sem_inc(h_ready, 2)
            for b in range(2):
                dve.sem_inc(out_stored[b], 16 * ST)
            for k, (a, b) in enumerate(flat_parts):
                dve.wait_ge(sums_in[k], 16)
                dve.reciprocal(inv_flat[:, a:b], sums_flat[:, a:b]).then_inc(inv_done, 1)
            dve.wait_ge(ow_high, 1)
            dve.tensor_tensor(ow_lo[:], ow_raw[:], ow_hi[:].bitcast(F32), ALU.subtract).then_inc(ow_low, 1)

            def context(n, h):
                k = HALF * n + h
                dve.wait_ge(half_in[h], 32 * n + 32)
                if h == 0:
                    dve.wait_ge(inv_ready, 16 * HG * n + 16 * HG)
                dve.tensor_tensor(ctx_in[:, h, :, :], ctx_in[:, h, :, :], inv_in[:, :, h * HC:(h + 1) * HC], ALU.mult).then_inc(c_scaled, 1)
                dve.wait_ge(c_scaled, k + 1)
                dve.tensor_copy(cp_hi[:], ctx_in[:, h, :, :]).then_inc(c_high, 1)
                dve.wait_ge(c_high, k + 1)
                dve.tensor_tensor(cp_lo[:], ctx_in[:, h, :, :], cp_hi[:].bitcast(F32), ALU.subtract).then_inc(c_ready, 1)

            def norm_begin(k, n, par, st, eps):
                rows = x1[:, par, st, :]
                at = ST * n + st + 1
                dve.wait_ge(summed[k], at)
                dve.bn_stats(stats[:, k, :], rows).then_inc(measured[k], 1)
                dve.wait_ge(measured[k], at)
                dve.nop(nofuse=True)
                dve.bn_aggr(mv[:, k, st, :], stats[:, k, :]).then_inc(averaged[k], 1)
                dve.wait_ge(averaged[k], at)
                dve.tensor_scalar(veps[:, k, st:st + 1], mv[:, k, st, 1:2], eps, None, ALU.add).then_inc(var_ready[k], 1)

            def norm_end(k, n, par, st):
                rows = x1[:, par, st, :]
                dve.wait_ge(rooted[k], ST * n + st + 1)
                dve.tensor_scalar(rows, rows, mv[:, k, st, 0:1], rstd[:, k, st:st + 1], ALU.subtract, ALU.mult)\
                   .then_inc(normed[k], 1)

            def residual(j, pos, n, par, h, stored):
                dve.wait_ge(slot_full, j + 1)
                if h == 0:
                    dve.wait_ge(out_stored[par], stored)
                for q in range(HALF):
                    ins = dve.tensor_tensor(x1[:, par, h * HALF + q, :], slot[pos % 2][q][:], x_in[:, h, q, :], ALU.add)
                    ins.then_inc(summed[0], 1)
                dve.wait_ge(summed[0], ST * n + h * HALF + HALF)
                dve.sem_inc(slot_free, 1)
                dve.sem_inc(half_used, 1)
                for q in range(HALF):
                    norm_begin(0, n, par, h * HALF + q, LN_EPS)

            def low(j, pos, n, par, p):
                for q in range(2):
                    dc = 2 * p + q
                    dve.wait_ge(high_ready, DC * n + dc + 1)
                    ins = dve.tensor_tensor(xt_lo[:, par, dc, :], slot[pos % 2][q][:], xt_hi[:, par, dc, :].bitcast(F32),
                                            ALU.subtract)
                ins.then_inc(slot_free, 1)

            def make_hidden(j, pos, n, i):
                k = IC * n + i + 1
                dve.wait_ge(gated, k)
                hid = hidden[:, i % 2, :]
                dve.scalar_tensor_tensor(hid, slot[pos % 2][1][:], up_scale[:, i:i + 1], hid, ALU.mult, ALU.mult)\
                   .then_inc(slot_free, 1)
                dve.wait_ge(slot_free, j + 1 + FREE)
                if not (isinstance(n, int) and n == 0 and i < 2):
                    dve.wait_ge(downed, k - 2)
                dve.tensor_copy(h_hi[:, i % 2, :], hid).then_inc(h_high, 1)
                dve.wait_ge(h_high, k)
                dve.tensor_tensor(h_lo[:, i % 2, :], hid, h_hi[:, i % 2, :].bitcast(F32), ALU.subtract).then_inc(h_ready, 1)

            def take_y(n, par):
                dve.wait_ge(downed, IC * (n + 1))
                for st in range(ST):
                    dve.tensor_tensor(y_raw[:, st, :], y[st][:], down_scale[:], ALU.mult).then_inc(y_taken, 1)

            def add_y(n, par, st):
                dve.wait_ge(y_taken, ST * n + st + 1)
                dve.tensor_tensor(x1[:, par, st, :], x1[:, par, st, :], y_raw[:, st, :], ALU.add).then_inc(summed[1], 1)
                norm_begin(1, n, par, st, LN_EPS)

            def body(n, c, par, before, after, pairs):
                waiting = []
                for pos, (kind, i) in enumerate(full if after else short):
                    j = start(n) + pos
                    if kind == "o":
                        residual(j, pos, n + 1, 1 - par, i, 16 * ST * (pairs + par + 1))
                        waiting += [(0, n + 1, 1 - par, i * HALF + q) for q in range(HALF)]
                    elif kind == "t":
                        low(j, pos, n + 1, 1 - par, i)
                    else:
                        make_hidden(j, pos, n, i)
                        for w in waiting:
                            norm_end(*w)
                        waiting = []
                        if before and i == 0:
                            take_y(n - 1, 1 - par)
                        if before and 1 <= i <= ST:
                            add_y(n - 1, 1 - par, i - 1)
                            waiting = [(1, n - 1, 1 - par, i - 1)]
                        if after and i in (7, 9):
                            context(n + 1, i // 9)

            context(0, 0)
            for pos, (kind, i) in enumerate(head):
                if kind == "o":
                    residual(pos, pos, 0, 0, i, 16 * ST)
                    if i == 0:
                        context(0, 1)
                    else:
                        for st in range(ST):
                            norm_end(0, 0, 0, st)
                else:
                    low(pos, pos, 0, 0, i)
            over_chunks(dve, body)
            take_y(NCH - 1, 1)
            for st in range(ST):
                add_y(NCH - 1, 1, st)
                if st:
                    norm_end(1, NCH - 1, 1, st - 1)
            norm_end(1, NCH - 1, 1, ST - 1)


NAMES = ["L0_attn_x", "L0_attn_Wqkv", "L0_attn_q_ln_scale", "L0_attn_k_ln_scale", "L0_attn_out_W",
         "L0_ffn_gate_w", "L0_ffn_gate_scale", "L0_ffn_up_w", "L0_ffn_up_scale", "L0_ffn_down_w",
         "L0_ffn_down_scale"]


def build(nc, io):
    def scratch(name, shape, dt):
        return nc.dram_tensor(name, shape, dt, kind="Internal").ap()

    dr = {
        "q_hi": scratch("q_hi", (D, S), F32), "q_lo": scratch("q_lo", (D, S), F32),
        "k_hi": scratch("k_hi", (D, S), F32), "k_lo": scratch("k_lo", (D, S), F32),
        "v": scratch("v_rows", (S, D), F32),
        "shift": scratch("shift", (2, HEADS, S), F32),
        "ctx": scratch("ctx", (D, S), F32),
        "sums": scratch("sums", (NCH, HEADS, CH), F32),
        "inverse": scratch("inverse", (NCH, HEADS, CH), F32),
        "wq": scratch("wq_float", (3 * IC, P, D), F32),
    }
    with ExitStack() as c:
        keep = {"flags": c.enter_context(nc.sbuf_tensor("flags", [P, 2], I32))}
        project(nc, io, dr, keep)
        attend(nc, io, dr, keep)
        finish(nc, io, dr, keep)


def kernel(**inputs):
    import numpy as np
    import concourse.bacc as bacc
    from concourse.bass_utils import run_bass_kernel_spmd

    x, wqkv, q_scale, k_scale, out_w, gate_w, gate_scale, up_w, up_scale, down_w, down_scale = (
        np.asarray(inputs[n]) for n in NAMES)
    x = x.reshape(S, D)
    gate, up = (w.reshape(IC, P, DC, P).transpose(0, 3, 2, 1).reshape(IC, 1, P, D) for w in (gate_w, up_w))
    down = down_w.T.reshape(IC, 1, P, D)
    laid = {
        "x": x, "x_t": x.T, "wqkv": wqkv, "out_w": out_w, "down_scale": down_scale,
        "q_scale": q_scale.reshape(DC, P).T, "k_scale": k_scale.reshape(DC, P).T,
        "gate_scale": gate_scale.reshape(IC, P).T, "up_scale": up_scale.reshape(IC, P).T,
        "wq": np.concatenate([gate, up, down], axis=1).reshape(3 * IC, P, D),
    }
    nc = bacc.Bacc("TRN2", target_bir_lowering=False, num_devices=1)
    arrays, io = {}, {}
    for name, a in laid.items():
        a = np.ascontiguousarray(a)
        arrays[f"in_{name}"] = a
        io[name] = nc.dram_tensor(f"in_{name}", a.shape, mybir.dt.from_np(a.dtype), kind="ExternalInput").ap()
    io["out"] = nc.dram_tensor("out_y", (S, D), F32, kind="ExternalOutput").ap()
    build(nc, io)
    r = run_bass_kernel_spmd(nc, [arrays], core_ids=[0])
    return r.results[0]["out_y"].reshape(1, S, D)
```

```python
from contextlib import ExitStack

import concourse.bass as bass
from concourse import mybir

F32 = mybir.dt.float32
F32R = mybir.dt.float32r
BF16 = mybir.dt.bfloat16
I32 = mybir.dt.int32
ALU = mybir.AluOpType
ACT = mybir.ActivationFunctionType
AX = mybir.AxisListType

P = 128
S = 4096
D = 512
HEADS = 16
HD = D // HEADS
INNER = 2048
CH = 512
NCH = S // CH
ST = CH // P
DC = D // P
HG = P // HD
NG = HEADS // HG
IC = INNER // P
KB = S // P
QK_EPS = 1e-6
LN_EPS = 1e-5
ZERO_POINT = 128.0
BOUND = 60.0
WHOLE = 4096.0
ROWS = 3 * HD + 2


def over_chunks(engine, body):
    body(0, -1, 0, False, True, 0)
    with engine.Fori(0, NCH // 2 - 1) as i:
        body(i * 2 + 1, i * 2, 1, True, True, i)
        body(i * 2 + 2, i * 2 + 1, 0, True, True, i + 1)
    body(NCH - 1, NCH - 2, 1, True, False, NCH // 2 - 1)


def project(nc, io, dr, keep):
    ACCS = 4
    NU, NJ = 3 * ST, 2 * DC
    usual = [(st, m) for st in range(ST) for m in range(3)]
    final = [(st, m) for st in range(ST) for m in range(2)] + [(st, 2) for st in range(ST)]

    x_parts = {0: (0,), 1: (1, 2), 2: (3,)}

    def plan(before, after):
        units = usual if after else final
        jobs = [[] for _ in units]
        if before:
            for i in range(NJ):
                jobs[2 + i if after else 1 + i * 6 // (NJ - 1)].append((False, i))
        if not after:
            for i in range(NJ):
                jobs[8 + i // 2].append((True, i))
        return list(zip(units, jobs))

    with ExitStack() as c:
        sb = lambda n, s, d=F32: c.enter_context(nc.sbuf_tensor(n, s, d))
        sem = lambda n: c.enter_context(nc.semaphore(n))
        x_raw = sb("x_raw", [P, DC, CH])
        x_hi = sb("x_hi", [P, 2, DC, CH], F32R)
        x_lo = sb("x_lo", [P, 2, DC, CH], F32R)
        w_raw = sb("w_raw", [P, DC, 3 * D])
        w_hi = sb("w_hi", [P, DC, 3 * D], F32R)
        w_lo = sb("w_lo", [P, DC, 3 * D], F32R)
        normed = sb("normed_qk", [P, 2, 2, ST, D])
        part_hi = sb("part_hi", [P, 4, CH], F32R)
        part_lo = sb("part_lo", [P, 4, CH], F32R)
        squares = sb("squares", [P, 2, CH], BF16)
        ow_raw = sb("ow_raw", [P, NG, D])
        ow_hi, ow_lo = keep["ow_hi"], keep["ow_lo"]
        v_out = sb("v_out", [P, 2, D])
        ident = sb("ident", [P, P])
        select = sb("select", [P, HD], BF16)
        stats = sb("stats", [P, 6])
        mv = sb("mv", [P, 2, 2])
        veps = sb("veps", [P, 2])
        rstd = sb("rstd", [P, 2])
        minus_half = sb("minus_half", [P, 1])
        quarter = sb("quarter", [P, DC])
        scales = sb("scales", [P, 2, DC])
        mix = sb("mix", [P, DC])
        mix_root = sb("mix_root", [P, DC])
        norm_max = sb("norm_max", [P, 2, NCH])
        norm_top = sb("norm_top", [P, 2])
        check = sb("check", [P, 1])
        check_top = sb("check_top", [1, 1])
        flag_f = sb("flag_f", [1, 1])
        zeros = sb("zeros", [P, 2 * HEADS * S // P])

        turn = [c.enter_context(nc.psum_tensor(f"turn{i}", [P, 512], F32)) for i in range(2)]
        acc = [c.enter_context(nc.psum_tensor(f"acc{i}", [P, 512], F32)) for i in range(ACCS)]
        norms = [c.enter_context(nc.psum_tensor(f"norms_{n}", [P, 512], F32)) for n in "qk"]

        x_in = [sem(f"x_in{dc}") for dc in range(DC)]
        x_high = sem("x_high")
        x_low = sem("x_low")
        wqkv_in = [[sem(f"wqkv_in{dc}{m}") for m in range(3)] for dc in range(DC)]
        w_high_done = sem("w_high_done")
        w_low_done = sem("w_low_done")
        ident_ready = sem("ident_ready")
        scales_ready = sem("scales_ready")
        dconst = sem("dconst")
        scales_in = sem("scales_in")
        turned = sem("turned")
        high_done = sem("high_done")
        low_done = sem("low_done")
        acc_full = sem("acc_full")
        v_taken = sem("v_taken")
        v_stored = keep["v_stored"]
        vstat = sem("vstat")
        var_ready = sem("var_ready")
        rstd_ready = sem("rstd_ready")
        qk_normed = sem("qk_normed")
        sq_ready = sem("sq_ready")
        norms_done = sem("norms_done")
        norms_read = sem("norms_read")
        parts_stored, zero_stored = keep["parts_stored"], keep["zero_stored"]
        ow_in = sem("ow_in")
        ow_high = sem("ow_high")
        fin = sem("fin")
        fin_pool = sem("fin_pool")
        check_turned = sem("check_turned")
        block = c.enter_context(nc.Block())

        xs = io["x_t"].rearrange("(c p) s -> c p s", p=P)

        @block.sync
        def _(sp):
            def load_x(n, dc):
                sp.dma_start(x_raw[:, dc, :], xs[dc][:, bass.ds(n * CH, CH)]).then_inc(x_in[dc], 16)

            for dc in range(DC):
                load_x(0, dc)
                for m in range(3):
                    cols = slice(m * D, (m + 1) * D)
                    sp.dma_start(w_raw[:, dc, cols], io["wqkv"][dc * P:(dc + 1) * P, cols]).then_inc(wqkv_in[dc][m], 16)
            sp.dma_start(scales[:, 0, :], io["q_scale"]).then_inc(scales_in, 16)
            sp.dma_start(scales[:, 1, :], io["k_scale"]).then_inc(scales_in, 16)
            sp.wait_ge(dconst, 1)
            sp.dma_start(dr["shift"].rearrange("a h (u s) -> (a h u) s", u=4), zeros[:]).then_inc(zero_stored, 16)
            sp.dma_start(ow_raw[:], io["out_w"].rearrange("(g r) e -> r g e", r=P)).then_inc(ow_in, 16)
            for s_, k in ((parts_stored, 32), (v_stored, 16)):
                for one in s_:
                    sp.sem_inc(one, k)

            def body(n, c, par, before, after, half):
                for dc in range(DC if after else 0):
                    sp.wait_ge(x_low, DC * n + dc + 1)
                    sp.nop(nofuse=True)
                    load_x(n + 1, dc)
                for (st, m), jobs in plan(before, after):
                    if m == 2:
                        sp.wait_ge(v_taken, ST * n + st + 1)
                        sp.nop(nofuse=True)
                        sp.dma_start(dr["v"].rearrange("(t p) d -> t p d", p=P)[bass.ds(n * ST + st, 1)].rearrange("t p d -> (t p) d"),
                                     v_out[:, st % 2, :]).then_inc(v_stored[st % 2], 16)
                    for own, i in jobs:
                        o = n if own else c
                        sp.wait_ge(high_done, NJ * o + i + 1 + 2)
                        sp.nop(nofuse=True)
                        sp.wait_ge(low_done, NJ * o + i + 1 + 2)
                        sp.nop(nofuse=True)
                        g = i % DC
                        for part, to in ((part_hi, ("q_hi", "k_hi")), (part_lo, ("q_lo", "k_lo"))):
                            sp.dma_start(dr[to[i // DC]][g * P:(g + 1) * P, bass.ds(o * CH, CH)], part[:, i % 4, :].bitcast(F32))\
                               .then_inc(parts_stored[i % 4], 16)

            over_chunks(sp, body)

        @block.gpsimd
        def _(pool):
            pool.memset(ident[:], 0.0).then_inc(fin_pool, 1)
            pool.wait_ge(fin_pool, 1)
            pool.affine_select(out=ident[:], in_=ident[:], compare_op=ALU.not_equal, fill=1.0, base=0,
                               pattern=[[-1, P]], channel_multiplier=1).then_inc(ident_ready, 1)
            pool.wait_ge(dconst, 4)
            pool.tensor_tensor(mix_root[:], mix[:], quarter[:], ALU.pow).then_inc(scales_ready, 1)

            def root(n, st, i):
                pool.wait_ge(var_ready, 2 * ST * n + 2 * st + i + 1)
                pool.tensor_tensor(rstd[:, i:i + 1], veps[:, i:i + 1], minus_half[:], ALU.pow).then_inc(rstd_ready, 1)

            with pool.Fori(0, NCH) as n:
                for st in range(ST):
                    root(n, st, 0)
                    root(n, st, 1)
            pool.wait_ge(ow_high, 1)
            pool.tensor_tensor(ow_lo[:], ow_raw[:], ow_hi[:].bitcast(F32), ALU.subtract).then_inc(fin_pool, 1)

        @block.tensor
        def _(pe):
            pe.sem_inc(high_done, 2)
            pe.sem_inc(low_done, 2)

            def wait_bank(n, c, units, u):
                if u < ACCS:
                    if isinstance(n, int) and n == 0:
                        return
                    n, (st, m) = c, usual[u - ACCS]
                else:
                    st, m = units[u - ACCS]
                if m == 2:
                    pe.wait_ge(v_taken, ST * n + st + 1)
                else:
                    pe.wait_ge(qk_normed, 2 * ST * n + 2 * st + m + 1)

            def product(bank, par, st, m, dc):
                rows = slice(st * P, (st + 1) * P)
                for a, (x, w) in enumerate(((x_hi, w_hi), (x_hi, w_lo), (x_lo, w_hi))):
                    ins = pe.matmul(bank[:], x[:, par, dc, rows], w[:, dc, m * D:(m + 1) * D],
                                    start=dc == 0 and a == 0, stop=dc == DC - 1 and a == 2)
                return ins

            def unit(n, c, par, units, u):
                st, m = units[u]
                wait_bank(n, c, units, u)
                if u == 0:
                    pe.wait_ge(x_low, DC * n + DC)
                for dc in range(DC):
                    ins = product(acc[u % ACCS], par, st, m, dc)
                ins.then_inc(acc_full, 1)

            def job(o, par, i):
                pe.wait_ge(high_done, NJ * o + i + 1)
                pe.wait_ge(low_done, NJ * o + i + 1)
                pe.wait_ge(qk_normed, 2 * ST * o + 2 * ST)
                for st in range(ST):
                    g = i % DC
                    ins = pe.transpose(turn[i % 2][:, st * P:(st + 1) * P], normed[:, par, i // DC, st, g * P:(g + 1) * P], ident[:])
                ins.then_inc(turned, 1)

            def norm(o, i):
                pe.wait_ge(sq_ready, NJ * o + i + 1)
                if i % DC == 0:
                    pe.wait_ge(norms_read, 2 * o + i // DC + 1)
                g = i % DC
                pe.matmul(norms[i // DC][g * HD:(g + 1) * HD, :], select[:], squares[:, i % 2, :],
                          start=True, stop=True).then_inc(norms_done, 1)

            def body(n, c, par, before, after, half):
                steps = plan(before, after)
                units = [x for x, _ in steps]
                due = []
                for u, (_, jobs) in enumerate(steps):
                    if before or u >= 3:
                        unit(n, c, par, units, u)
                    elif u == 0:
                        for dc in range(DC):
                            pe.wait_ge(x_low, dc + 1)
                            for m in range(3):
                                pe.wait_ge(w_low_done, 3 * dc + m + 1)
                                ins = product(acc[m], par, 0, m, dc)
                                if dc == DC - 1:
                                    ins.then_inc(acc_full, 1)
                    for own, i in jobs:
                        o = n if own else c
                        job(o, par if own else 1 - par, i)
                        if len(due) > 1:
                            norm(*due.pop(0))
                        due.append((o, i))
                    if not jobs and due:
                        norm(*due.pop(0))
                while due:
                    norm(*due.pop(0))

            pe.wait_ge(ident_ready, 1)
            pe.wait_ge(dconst, 3)
            over_chunks(pe, body)
            pe.wait_ge(high_done, NJ * NCH + 2)
            pe.wait_ge(low_done, NJ * NCH + 2)
            pe.wait_ge(fin, 2)
            pe.transpose(turn[0][0:1, 0:P], check[:], ident[:]).then_inc(check_turned, 1)

        @block.scalar
        def _(act):
            def high_x(n, par, dc):
                act.wait_ge(x_in[dc], 16 * n + 16)
                act.activation(x_hi[:, par, dc, :], x_raw[:, dc, :], ACT.Copy).then_inc(x_high, 1)

            for dc in range(DC):
                high_x(0, 0, dc)
                for m in range(3):
                    cols = slice(m * D, (m + 1) * D)
                    act.wait_ge(wqkv_in[dc][m], 16)
                    act.activation(w_hi[:, dc, cols], w_raw[:, dc, cols], ACT.Copy).then_inc(w_high_done, 1)
            act.wait_ge(scales_ready, 2)
            act.sem_inc(norms_done, 2)

            def high(o, i):
                act.wait_ge(turned, NJ * o + i + 1)
                b = turn[i % 2]
                act.wait_ge(parts_stored[i % 4], 64 * o + 32 * (i // 4) + 32)
                act.wait_ge(norms_done, NJ * o + i + 1)
                g = i % DC
                act.activation(squares[:, i % 2, :], b[:], ACT.Square, scale=mix_root[:, g:g + 1]).then_inc(sq_ready, 1)
                act.activation(part_hi[:, i % 4, :], b[:], ACT.Copy, scale=scales[:, i // DC, g:g + 1]).then_inc(high_done, 1)

            def take_v(n, u, st):
                act.wait_ge(acc_full, NU * n + u + 1)
                act.wait_ge(v_stored[st % 2], 32 * n + 16 * (st // 2) + 16)
                act.activation(v_out[:, st % 2, :], acc[u % ACCS][:], ACT.Copy).then_inc(v_taken, 1)

            def body(n, c, par, before, after, half):
                if not after:
                    act.wait_ge(ow_in, 16)
                    act.activation(ow_hi[:], ow_raw[:], ACT.Copy).then_inc(ow_high, 1)
                for u, ((st, m), jobs) in enumerate(plan(before, after)):
                    if m == 1 and after and st in x_parts:
                        if before and st == 0:
                            act.wait_ge(acc_full, NU * n)
                        for dc in x_parts[st]:
                            high_x(n + 1, 1 - par, dc)
                    if m == 2:
                        take_v(n, u, st)
                    for own, i in jobs:
                        high(n if own else c, i)

            over_chunks(act, body)

        @block.vector
        def _(dve):
            dve.memset(minus_half[:], -0.5)
            dve.memset(quarter[:], 0.25)
            dve.memset(zeros[:], 0.0).then_inc(dconst, 1)
            dve.memset(select[:], 0.0).then_inc(dconst, 1)
            dve.wait_ge(dconst, 2)
            for h in range(HG):
                ins = dve.memset(select[h * HD:(h + 1) * HD, h:h + 1], 1.0)
            ins.then_inc(dconst, 1)

            def low_x(n, par, dc):
                dve.wait_ge(x_high, DC * n + dc + 1)
                dve.tensor_tensor(x_lo[:, par, dc, :], x_raw[:, dc, :], x_hi[:, par, dc, :].bitcast(F32), ALU.subtract).then_inc(x_low, 1)

            for dc in range(DC):
                low_x(0, 0, dc)
                for m in range(3):
                    cols = slice(m * D, (m + 1) * D)
                    dve.wait_ge(w_high_done, 3 * dc + m + 1)
                    dve.tensor_tensor(w_lo[:, dc, cols], w_raw[:, dc, cols], w_hi[:, dc, cols].bitcast(F32), ALU.subtract)\
                       .then_inc(w_low_done, 1)
            dve.wait_ge(scales_in, 32)
            root_hd = float(HD) ** -0.5
            dve.tensor_tensor(mix[:], scales[:, 0, :], scales[:, 1, :], ALU.mult).then_inc(vstat, 1)
            dve.wait_ge(vstat, 1)
            dve.tensor_scalar(mix_root[:], mix[:], root_hd, None, ALU.mult).then_inc(vstat, 1)
            dve.wait_ge(vstat, 2)
            dve.tensor_tensor(mix[:], mix_root[:], mix_root[:], ALU.mult).then_inc(dconst, 1)
            dve.tensor_scalar(scales[:, 0, :], scales[:, 0, :], root_hd, None, ALU.mult).then_inc(scales_ready, 1)
            dve.sem_inc(norms_read, 2)

            def low(o, i):
                g = i % DC
                dve.wait_ge(high_done, NJ * o + i + 1 + 2)
                dve.scalar_tensor_tensor(part_lo[:, i % 4, :], turn[i % 2][:], scales[:, i // DC, g:g + 1],
                                         part_hi[:, i % 4, :].bitcast(F32), ALU.mult, ALU.subtract).then_inc(low_done, 1)

            def measure(n, u, st, i):
                dve.wait_ge(acc_full, NU * n + u + 1)
                k = 2 * (2 * st + i) + 2
                dve.bn_stats(stats[:], acc[u % ACCS][:]).then_inc(vstat, 1)
                dve.wait_ge(vstat, 4 * ST * n + k + 1)
                dve.nop(nofuse=True)
                dve.bn_aggr(mv[:, i, :], stats[:]).then_inc(vstat, 1)
                dve.wait_ge(vstat, 4 * ST * n + k + 2)
                dve.tensor_scalar(veps[:, i:i + 1], mv[:, i, 1:2], QK_EPS, None, ALU.add).then_inc(var_ready, 1)

            def apply(n, par, u, st, i):
                dve.wait_ge(rstd_ready, 2 * ST * n + 2 * st + i + 1)
                dve.tensor_scalar(normed[:, par, i, st, :], acc[u % ACCS][:], mv[:, i, 0:1], rstd[:, i:i + 1],
                                  ALU.subtract, ALU.mult).then_inc(qk_normed, 1)

            def top(o, i):
                dve.wait_ge(norms_done, NJ * o + DC * (i + 1) + 2)
                dve.tensor_reduce(norm_max[:, i, bass.ds(o, 1)], norms[i][:], AX.X, ALU.max).then_inc(norms_read, 1)

            def body(n, c, par, before, after, half):
                steps = plan(before, after)
                waiting = []
                tops = []
                for u, ((st, m), jobs) in enumerate(steps):
                    if m < 2:
                        measure(n, u, st, m)
                    for w in waiting:
                        apply(*w)
                    waiting = [(n, par, u, st, m)] if m < 2 else []
                    if m == 2 and after and st in x_parts:
                        for dc in x_parts[st]:
                            low_x(n + 1, 1 - par, dc)
                    for t in tops:
                        if t[2] <= u:
                            top(*t[:2])
                    tops = [t for t in tops if t[2] > u]
                    for own, i in jobs:
                        low(n if own else c, i)
                        if i % DC == DC - 1:
                            tops.append((n if own else c, i // DC, u + 3))
                for t in tops:
                    top(*t[:2])

            over_chunks(dve, body)
            dve.wait_ge(norms_read, 2 + 2 * NCH)
            dve.tensor_reduce(norm_top[:], norm_max[:], AX.X, ALU.max).then_inc(fin, 1)
            dve.wait_ge(fin, 1)
            dve.tensor_tensor(check[:], norm_top[:, 0:1], norm_top[:, 1:2], ALU.mult).then_inc(fin, 1)
            dve.wait_ge(check_turned, 1)
            dve.tensor_reduce(check_top[:], turn[0][0:1, 0:P], AX.X, ALU.max).then_inc(fin, 1)
            dve.wait_ge(fin, 3)
            dve.tensor_scalar(flag_f[:], check_top[:], BOUND * BOUND, None, ALU.is_gt).then_inc(fin, 1)
            dve.wait_ge(fin, 4)
            dve.tensor_copy(keep["flags"][0:1, 0:1], flag_f[:]).then_inc(fin, 1)


def attend(nc, io, dr, keep):
    LAG = 2
    T_LAG = LAG + 2
    PB = 6
    RING = 3
    steps = []
    for ch in range(NCH):
        short, full = list(range(ST * ch, ST * (ch + 1))), list(range(ST * ch))
        while short or full:
            steps += [(ch, q.pop(0)) for q in (short, full) if q]
    NS = len(steps)
    first = [next(t for t in range(NS) if steps[t][0] == ch) for ch in range(NCH)]
    last = [x - 1 for x in first[1:] + [NS]]
    key_end = [max(t for t in range(NS) if steps[t][1] // ST == j) for j in range(NCH)]
    q_buffer = [0, 1, 2, 0, 1, 0, 1, 2]
    q_chunks = [[ch for ch in range(NCH) if q_buffer[ch] == b] for b in range(3)]
    Q_CREDIT = 2 * (NS - last[q_chunks[0][-1]])
    V_CREDIT = NS - first[NCH - 1]
    A_CREDIT = PB

    def cut(t):
        ch, kb = steps[t]
        return max(0, kb - ST * ch) * P

    def diagonal(t):
        return steps[t][1] >= ST * steps[t][0]

    def by_pe(t):
        ch, kb = steps[t]
        return not diagonal(t) and t - first[ch] >= ST * 3 and (t - first[ch]) % 6 == 0

    WT = 3 * IC // NG
    tiles_after = {ch: range(2 * (ch - 2), 2 * (ch - 1)) for ch in range(2, NCH)}
    assert sum(map(len, tiles_after.values())) == WT

    adds = [t for t in range(NS) if not by_pe(t)]
    NA = len(adds)
    assert NS % PB == 0 and 2 * NS % RING == 0
    NM = sum(diagonal(t) for t in range(NS))

    def adds_before(t):
        return adds_before(t + NS) - NA if t < 0 else sum(a < t for a in adds)

    def masks_before(t):
        return sum(diagonal(x) for x in range(t))

    with ExitStack() as c:
        sb = lambda n, s, d=F32: c.enter_context(nc.sbuf_tensor(n, s, d))
        sem = lambda n: c.enter_context(nc.semaphore(n))
        kstk = sb("kstk", [P, HG, S], F32R)
        qstk = sb("qstk", [P, 3, HG, CH], F32R)
        values = sb("values", [P, KB, P])
        probs = sb("probs", [P, PB, HG, CH])
        total = sb("total", [P, 2, HG, CH])
        ones = sb("ones", [P, HD])
        ctx_out = sb("ctx_out", [P, 2, CH])
        sums_out = sb("sums_out", [P, 2, CH])
        wq_int = sb("wq_int", [P, 2, D], I32)
        wq_f = sb("wq_f", [P, 2, D])
        wq_square = sb("wq_square", [P, D])
        whole = keep["whole"]
        FLAT = HG * CH // P
        flat = sb("flat", [P, FLAT])
        flat_inv = sb("flat_inv", [P, FLAT])
        score = [c.enter_context(nc.psum_tensor(f"score{i}", [P, 2, CH], F32)) for i in range(RING)]
        ctx = c.enter_context(nc.psum_tensor("ctx_acc", [P, CH], F32))
        sums = c.enter_context(nc.psum_tensor("sums_acc", [P, CH], F32))

        k_in = [sem(f"k_in{j}") for j in range(NCH)]
        v_in = [sem(f"v_in{j}") for j in range(NCH)]
        q_in = [sem(f"q_in{b}") for b in range(3)]
        ones_ready = sem("ones_ready")
        scored = sem("scored")
        exped = sem("exped")
        masked = sem("masked")
        valued = sem("valued")
        added = sem("added")
        begun = sem("begun")
        totaled = sem("totaled")
        ctx_taken = sem("ctx_taken")
        sums_taken = sem("sums_taken")
        ctx_stored = keep["ctx_stored"]
        flat_in = sem("flat_in")
        inverted = sem("inverted")
        inverse_stored = sem("inverse_stored")
        int_in = [sem(f"int_in{b}") for b in range(2)]
        floated = sem("floated")
        wq_squared = sem("wq_squared")
        whole_done = sem("whole_done")
        wq_stored = [sem(f"wq_stored{b}") for b in range(2)]
        whole_zero = sem("whole_zero")
        g_in = sem("g_in")
        g_scored = sem("g_scored")
        g_copied = sem("g_copied")
        g_masked = sem("g_masked")
        g_read = sem("g_read")
        g_top = sem("g_top")
        g_turned = sem("g_turned")
        g_split = sem("g_split")
        g_out = sem("g_out")
        g_ident = sem("g_ident")
        block = c.enter_context(nc.Block())

        units = [(ch, h, qt, kc) for ch in range(NCH) for h in range(HG) for qt in range(ST) for kc in range(ch + 1)]
        NU = len(units)
        edges = [u for u, (ch, _, _, kc) in enumerate(units) if kc == ch]
        g_copy = total[:, 0, 0:2, :]
        g_part = total[:, 1, 0, 0:NCH]
        g_max = total[:, 1, 1, 0:P]
        g_idt = total[:, 1, 2, 0:P]
        g_hi = probs[:, 0, 0, 0:P].bitcast(F32R)
        g_lo = probs[:, 0, 1, 0:P].bitcast(F32R)
        g_full = probs[:, 0, 2, 0:P]

        def k_load(sp, g, j, s):
            for r, src in enumerate(("k_hi", "k_lo", "k_hi")):
                sp.dma_start(kstk[r * HD:(r + 1) * HD, :, j * CH:(j + 1) * CH].bitcast(F32),
                             dr[src].rearrange("(g h r) s -> g r h s", h=HG, r=HD)[bass.ds(g, 1), :, :, j * CH:(j + 1) * CH]
                             .rearrange("g r h s -> (g r) h s")).then_inc(s, 16)

        def q_load(sp, g, ch, b, s):
            for r, src in enumerate(("q_hi", "q_hi", "q_lo")):
                sp.dma_start(qstk[r * HD:(r + 1) * HD, b, :, :].bitcast(F32),
                             dr[src].rearrange("(g h r) s -> g r h s", h=HG, r=HD)[bass.ds(g, 1), :, :, ch * CH:(ch + 1) * CH]
                             .rearrange("g r h s -> (g r) h s")).then_inc(s, 16)
            sp.dma_start(qstk[3 * HD:ROWS, b, :, :].bitcast(F32),
                         dr["shift"].rearrange("a (g h) s -> a g h s", h=HG)[:, bass.ds(g, 1), :, ch * CH:(ch + 1) * CH]
                         .rearrange("a g h s -> a (g h) s")).then_inc(s, 16)

        def store(eng, g, ch):
            eng.wait_ge(sums_taken, NCH * g + ch + 2)
            eng.nop(nofuse=True)
            eng.dma_start(dr["sums"].rearrange("n (g h) s -> n g h s", h=HG)[ch, bass.ds(g, 1), :, :]
                          .rearrange("g h s -> (g h) s"), sums_out[0:P:HD, ch % 2, :]).then_inc(ctx_stored[ch % 2], 16)
            eng.wait_ge(ctx_taken, NCH * g + ch + 2)
            eng.nop(nofuse=True)
            eng.dma_start(dr["ctx"].rearrange("(g r) s -> g r s", r=P)[bass.ds(g, 1), :, ch * CH:(ch + 1) * CH]
                          .rearrange("g r s -> (g r) s"), ctx_out[:, ch % 2, :]).then_inc(ctx_stored[ch % 2], 16)

        @block.sync
        def _(sp):
            general = sp.value_load(keep["flags"][0:1, 0:1], min_val=0, max_val=1)

            def stored(chunks):
                for one in keep["parts_stored"]:
                    sp.wait_ge(one, 32 + 64 * chunks)
                for one in keep["v_stored"]:
                    sp.wait_ge(one, 16 + 32 * chunks)

            sp.wait_ge(keep["zero_stored"], 16)
            with sp.If(general):
                stored(NCH)
                with sp.Fori(0, NG) as g:
                    sp.wait_ge(g_split, g + 1)
                    sp.nop(nofuse=True)
                    for j in range(NCH):
                        k_load(sp, g, j, g_in)
                    for ch in range(NCH):
                        done = [u for u, x in enumerate(units) if x[0] < ch]
                        if ch:
                            sp.wait_ge(g_scored, NU * g + len(done))
                            sp.nop(nofuse=True)
                        q_load(sp, g, ch, 0, g_in)
                    sp.wait_ge(g_split, g + 2)
                    sp.nop(nofuse=True)
                    for a, part in ((0, g_hi), (1, g_lo)):
                        sp.dma_start(dr["shift"].rearrange("a (g h) (t q) -> a g (h t) q", h=HG, q=P)[a][bass.ds(g, 1)]
                                     .rearrange("g x q -> (g x) q"), part.bitcast(F32)).then_inc(g_out, 16)
                    sp.wait_ge(g_out, 32 * g + 32)
                    sp.nop(nofuse=True)
            def group(g, before):
                def load(kind, j):
                    if kind == "q":
                        mine = q_chunks[q_buffer[j]]
                        end = last[mine[mine.index(j) - 1]] + 1 - (NS if j == mine[0] else 0)
                        sp.wait_ge(scored, 2 * NS * g + 2 * end + Q_CREDIT)
                        sp.nop(nofuse=True)
                        q_load(sp, g, j, q_buffer[j], q_in[q_buffer[j]])
                        return
                    end = key_end[j] + 1 - NS
                    sp.wait_ge(scored, 2 * NS * g + 2 * end + Q_CREDIT)
                    sp.nop(nofuse=True)
                    k_load(sp, g, j, k_in[j])
                    sp.wait_ge(valued, NS * g + end + V_CREDIT)
                    sp.nop(nofuse=True)
                    sp.dma_start(values[:, j * ST:(j + 1) * ST, :],
                                 dr["v"].rearrange("(b p) (g d) -> p b g d", p=P, d=P)[:, j * ST:(j + 1) * ST, bass.ds(g, 1), :]
                                 .rearrange("p b g d -> p b (g d)")).then_inc(v_in[j], 16)
                def load_int(j):
                    sp.wait_ge(floated, WT * g + j + 1)
                    sp.nop(nofuse=True)
                    sp.dma_start(wq_int[:, j % 2, :], io["wq"][bass.ds(g * WT + j, 1)].rearrange("a p x -> (a p) x"))\
                      .then_inc(int_in[j % 2], 16)

                def store_float(j):
                    sp.wait_ge(floated, WT * g + j + 1 + 2)
                    sp.nop(nofuse=True)
                    sp.dma_start(dr["wq"][bass.ds(g * WT + j, 1)].rearrange("a p x -> (a p) x"), wq_f[:, j % 2, :])\
                      .then_inc(wq_stored[j % 2], 16)

                if before is None:
                    stored(1)
                load("q", 0)
                load("kv", 0)
                if before is None:
                    stored(NCH)
                load("q", 1)
                load_int(0)
                load_int(1)
                for j in range(1, NCH):
                    load("kv", j)
                if before is not None:
                    store(sp, before, NCH - 1)
                for ch in range(2, NCH):
                    load("q", ch)
                    store(sp, g, ch - 2)
                    for j in tiles_after.get(ch - 1, ()):
                        store_float(j)
                        load_int(j + 2)
                sp.wait_ge(ctx_stored[0], 32 * (NCH // 2) * g + 64)
                sp.nop(nofuse=True)
                sp.dma_start(flat[:], dr["sums"].rearrange("n (g h) (u s) -> n g h u s", h=HG, s=FLAT)[0, bass.ds(g, 1)]
                             .rearrange("g h u s -> (g h u) s")).then_inc(flat_in, 16)
                store(sp, g, NCH - 2)
                sp.wait_ge(inverted, g + 1)
                sp.nop(nofuse=True)
                sp.dma_start(dr["inverse"].rearrange("n (g h) (u s) -> n g h u s", h=HG, s=FLAT)[0, bass.ds(g, 1)]
                             .rearrange("g h u s -> (g h u) s"), flat_inv[:]).then_inc(inverse_stored, 16)
                for j in tiles_after[NCH - 1]:
                    store_float(j)

            group(0, None)
            with sp.Fori(0, NG - 1) as i:
                group(i + 1, i)
            store(sp, NG - 1, NCH - 1)
            for b in range(2):
                sp.wait_ge(wq_stored[b], 16 * (WT // 2) * NG + 16)
            sp.wait_ge(inverse_stored, 16 * NG + 16)

        @block.gpsimd
        def _(pool):
            general = pool.value_load(keep["flags"][0:1, 0:1], min_val=0, max_val=1)
            with pool.If(general):
                pool.memset(g_idt, 0.0).then_inc(g_ident, 1)
                pool.wait_ge(g_ident, 1)
                pool.affine_select(out=g_idt, in_=g_idt, compare_op=ALU.not_equal, fill=1.0, base=0,
                                   pattern=[[-1, P]], channel_multiplier=1).then_inc(g_ident, 1)
                with pool.Fori(0, NG) as g:
                    for e, u in enumerate(edges):
                        qt = units[u][2]
                        pool.wait_ge(g_copied, len(edges) * g + e + 1)
                        pool.nop(nofuse=True)
                        pool.affine_select(out=g_copy[:, e % 2, :], in_=g_copy[:, e % 2, :], compare_op=ALU.is_ge,
                                           fill=-3.0e38, base=qt * P, pattern=[[-1, CH]], channel_multiplier=1)\
                            .then_inc(g_masked, 1)
            pool.sem_inc(floated, 2)
            pool.sem_inc(whole_done, 2)
            for b in range(2):
                pool.sem_inc(wq_stored[b], 16)
            pool.wait_ge(whole_zero, 1)

            def turn_float(g, j):
                b = j % 2
                pool.wait_ge(int_in[b], 16 * (WT // 2) * g + 16 * (j // 2) + 16)
                pool.wait_ge(wq_stored[b], 16 * (WT // 2) * g + 16 * (j // 2) + 16)
                pool.wait_ge(whole_done, WT * g + j + 1)
                pool.nop(nofuse=True)
                pool.tensor_scalar(wq_f[:, b, :], wq_int[:, b, :], -ZERO_POINT, None, ALU.add).then_inc(floated, 1)
                pool.wait_ge(floated, WT * g + j + 1 + 2)
                pool.wait_ge(whole_done, WT * g + j + 2)
                pool.nop(nofuse=True)
                pool.tensor_tensor(wq_square[:], wq_f[:, b, :], wq_f[:, b, :], ALU.mult).then_inc(wq_squared, 1)
                pool.wait_ge(wq_squared, WT * g + j + 1)
                pool.nop(nofuse=True)
                pool.tensor_tensor(whole[:], whole[:], wq_square[:], ALU.add).then_inc(whole_done, 1)

            with pool.Fori(0, NG) as g:
                for t in range(NS):
                    if diagonal(t):
                        pool.wait_ge(exped, 2 * NS * g + 2 * t + 2 + RING)
                        view = probs[:, t % PB, :, cut(t):cut(t) + P]
                        pool.nop(nofuse=True)
                        pool.affine_select(out=view, in_=view, compare_op=ALU.is_ge, fill=0.0, base=0,
                                           pattern=[[0, HG], [1, P]], channel_multiplier=-1).then_inc(masked, 1)
                    if steps[t][1] == ST * steps[t][0] + ST - 1:
                        for j in tiles_after.get(steps[t][0], ()):
                            turn_float(g, j)

        @block.tensor
        def _(pe):
            general = pe.value_load(keep["flags"][0:1, 0:1], min_val=0, max_val=1)
            with pe.If(general):
                pe.wait_ge(ones_ready, 1 + NCH)
                pe.sem_inc(g_read, 2)
                with pe.Fori(0, NG) as g:
                    for u, (ch, h, qt, kc) in enumerate(units):
                        if (h, qt, kc) == (0, 0, 0):
                            pe.wait_ge(g_in, 16 * ((3 + 1) * NCH + 3 * NCH) * g + 16 * (3 * NCH + 4 * (ch + 1)))
                        pe.wait_ge(g_read, NU * g + u + 1)
                        pe.matmul(score[u % 2][:, 0, :], qstk[0:ROWS, 0, h, qt * P:(qt + 1) * P],
                                  kstk[0:ROWS, h, kc * CH:(kc + 1) * CH], start=True, stop=True).then_inc(g_scored, 1)
                    pe.wait_ge(g_ident, 2)
                    pe.wait_ge(g_top, len(edges) * (g + 1))
                    pe.transpose(score[2][:, 0, 0:P], g_max, g_idt).then_inc(g_turned, 1)
                    pe.wait_ge(g_split, g + 2)
            pe.sem_inc(scored, Q_CREDIT)
            pe.sem_inc(valued, V_CREDIT)
            pe.sem_inc(totaled, 2)

            def scores(g, t):
                ch, kb = steps[t]
                if t in first:
                    mine = q_chunks[q_buffer[ch]]
                    pe.wait_ge(q_in[q_buffer[ch]], 64 * len(mine) * g + 64 * (mine.index(ch) + 1))
                if kb == ST * ch:
                    pe.wait_ge(ones_ready, 1 + ch + 1)
                    pe.wait_ge(k_in[ch], 48 * g + 48)
                for p in range(2):
                    u = 2 * t + p
                    pe.wait_ge(exped, 2 * NS * g + u + 1)
                    for i in range(2):
                        h = 2 * p + i
                        ins = pe.matmul(score[u % RING][:, i, cut(t):], kstk[0:ROWS, h, kb * P:(kb + 1) * P],
                                        qstk[0:ROWS, q_buffer[ch], h, cut(t):], start=True, stop=True)
                    ins.then_inc(scored, 1)

            def weigh(g, t):
                ch, kb = steps[t]
                pe.wait_ge(exped, 2 * NS * g + 2 * t + 2 + RING)
                if diagonal(t):
                    pe.wait_ge(masked, NM * g + masks_before(t) + 1)
                if kb == ST * ch:
                    pe.wait_ge(v_in[ch], 16 * g + 16)
                if t in first:
                    pe.wait_ge(ctx_taken, NCH * g + ch + 1)
                n0 = cut(t)
                for h in range(HG):
                    ins = pe.matmul(ctx[h * HD:(h + 1) * HD, n0:], values[:, kb, h * HD:(h + 1) * HD],
                                    probs[:, t % PB, h, n0:], start=t in first, stop=t in last)
                if by_pe(t):
                    opens = not any(by_pe(x) for x in range(first[ch], t))
                    if opens:
                        pe.wait_ge(sums_taken, NCH * g + ch + 1)
                    for h in range(HG):
                        ins = pe.matmul(sums[h * HD:(h + 1) * HD, n0:], ones[:], probs[:, t % PB, h, n0:],
                                        start=opens, stop=False)
                ins.then_inc(valued, 1)

            def sum_total(g, ch):
                opens = not any(by_pe(x) for x in range(first[ch], last[ch] + 1))
                if opens:
                    pe.wait_ge(sums_taken, NCH * g + ch + 1)
                pe.wait_ge(added, NA * g + adds_before(last[ch] + 1) + A_CREDIT)
                for h in range(HG):
                    ins = pe.matmul(sums[h * HD:(h + 1) * HD, :], ones[:], total[:, ch % 2, h, :], start=opens, stop=True)
                ins.then_inc(totaled, 1)

            def group(g, after):
                for t in range(NS):
                    if t + LAG < NS:
                        scores(g, t + LAG)
                    elif after:
                        scores(g + 1, t + LAG - NS)
                    weigh(g, t)
                    if t + LAG - T_LAG in last:
                        sum_total(g, last.index(t + LAG - T_LAG))
                sum_total(g, NCH - 1)

            for t in range(LAG):
                scores(0, t)
            with pe.Fori(0, NG - 1) as g:
                group(g, True)
            group(NG - 1, False)

        @block.scalar
        def _(act):
            general = act.value_load(keep["flags"][0:1, 0:1], min_val=0, max_val=1)
            with act.If(general):
                with act.Fori(0, NG) as g:
                    for e, u in enumerate(edges):
                        act.wait_ge(g_scored, NU * g + u + 1)
                        if e >= 2:
                            act.wait_ge(g_top, len(edges) * g + e - 1)
                        act.activation(g_copy[:, e % 2, :], score[u % 2][:, 0, :], ACT.Copy).then_inc(g_copied, 1)
            act.sem_inc(exped, RING)

            def take_ctx(g, ch):
                act.wait_ge(valued, NS * g + last[ch] + 1 + V_CREDIT)
                act.wait_ge(ctx_stored[ch % 2], 32 * (NCH // 2) * g + 32 * (ch // 2) + 32)
                act.activation(ctx_out[:, ch % 2, :], ctx[:], ACT.Copy).then_inc(ctx_taken, 1)

            def group(g, before):
                for t in range(NS):
                    act.wait_ge(valued, NS * g + t - PB + 1 + V_CREDIT)
                    act.wait_ge(added, NA * g + adds_before(t - PB + 1) + A_CREDIT)
                    for p in range(2):
                        u = 2 * t + p
                        act.wait_ge(scored, 2 * NS * g + u + 1 + Q_CREDIT)
                        act.activation(probs[:, t % PB, 2 * p:2 * p + 2, cut(t):], score[u % RING][:, :, cut(t):],
                                       ACT.Exp).then_inc(exped, 1)
                        if p == 0 and t - LAG in last:
                            take_ctx(g, last.index(t - LAG))
                        elif p == 0 and t == LAG - 1 and before is not None:
                            take_ctx(before, NCH - 1)

            group(0, None)
            with act.Fori(0, NG - 1) as i:
                group(i + 1, i)
            take_ctx(NG - 1, NCH - 1)

        @block.vector
        def _(dve):
            general = dve.value_load(keep["flags"][0:1, 0:1], min_val=0, max_val=1)
            dve.memset(ones[:], 1.0).then_inc(ones_ready, 1)
            dve.memset(whole[:], 0.0).then_inc(whole_zero, 1)
            for j in range(NCH):
                dve.memset(kstk[3 * HD:P, :, j * CH:(j + 1) * CH].bitcast(F32), 1.0).then_inc(ones_ready, 1)
            dve.sem_inc(g_split, 1)
            with dve.If(general):
                with dve.Fori(0, NG) as g:
                    for u, (ch, h, qt, kc) in enumerate(units):
                        if kc == 0 and u:
                            dve.wait_ge(g_top, len(edges) * g + sum(x < u for x in edges))
                        if kc < ch:
                            dve.wait_ge(g_scored, NU * g + u + 1)
                            dve.tensor_reduce(g_part[:, kc:kc + 1], score[u % 2][:, 0, :], AX.X, ALU.max).then_inc(g_read, 1)
                        else:
                            e = edges.index(u)
                            dve.wait_ge(g_masked, len(edges) * g + e + 1)
                            dve.tensor_reduce(g_part[:, kc:kc + 1], g_copy[:, e % 2, :], AX.X, ALU.max).then_inc(g_read, 1)
                            dve.wait_ge(g_read, NU * g + u + 1 + 2)
                            col = h * KB + ch * ST + qt
                            dve.tensor_reduce(g_max[:, col:col + 1], g_part[:, 0:ch + 1], AX.X, ALU.max).then_inc(g_top, 1)
                    dve.wait_ge(g_turned, g + 1)
                    dve.tensor_scalar(g_full, score[2][:, 0, 0:P], -1.0, None, ALU.mult).then_inc(g_ident, 1)
                    dve.wait_ge(g_ident, 2 + 2 * g + 1)
                    dve.tensor_copy(g_hi, g_full).then_inc(g_ident, 1)
                    dve.wait_ge(g_ident, 2 + 2 * g + 2)
                    dve.tensor_tensor(g_lo, g_full, g_hi.bitcast(F32), ALU.subtract).then_inc(g_split, 1)
            dve.sem_inc(added, A_CREDIT)
            dve.sem_inc(ctx_taken, 1)
            dve.sem_inc(sums_taken, 1)
            dve.sem_inc(inverse_stored, 16)
            for b in range(2):
                dve.sem_inc(ctx_stored[b], 32)

            def take_sums(g, ch):
                dve.wait_ge(totaled, NCH * g + ch + 1 + 2)
                dve.wait_ge(ctx_stored[ch % 2], 32 * (NCH // 2) * g + 32 * (ch // 2) + 32)
                dve.tensor_copy(sums_out[:, ch % 2, :], sums[:]).then_inc(sums_taken, 1)

            with dve.Fori(0, NG) as g:
                for t in range(NS):
                    ch, kb = steps[t]
                    place = t - first[ch]
                    if not by_pe(t) and (place or not ch):
                        dve.wait_ge(exped, 2 * NS * g + 2 * t + 2 + RING)
                        if diagonal(t) or place == 1:
                            dve.wait_ge(masked, NM * g + masks_before(t + 1))
                        now = probs[:, t % PB, :, cut(t):]
                        into = total[:, ch % 2, :, cut(t):]
                        if place > 1:
                            dve.wait_ge(added, NA * g + adds_before(t) + A_CREDIT)
                            dve.tensor_tensor(into, into, now, ALU.add).then_inc(added, 1)
                        elif place == 1:
                            dve.wait_ge(totaled, NCH * g + ch + 1)
                            dve.tensor_tensor(into, probs[:, (t - 1) % PB, :, cut(t):], now, ALU.add).then_inc(added, 2)
                        else:
                            dve.wait_ge(totaled, NCH * g + ch + 1)
                            dve.tensor_copy(total[:, 0, :, 0:P], probs[:, t % PB, :, 0:P]).then_inc(begun, 1)
                    if t == first[NCH - 1] + 2 * ST:
                        dve.wait_ge(flat_in, 16 * g + 16)
                        dve.wait_ge(inverse_stored, 16 * g + 16)
                        dve.reciprocal(flat_inv[:], flat[:]).then_inc(inverted, 1)
                    if t - T_LAG - 1 in last:
                        take_sums(g, last.index(t - T_LAG - 1))
                take_sums(g, NCH - 1)


def finish(nc, io, dr, keep):
    HALF = 2
    HC = HALF * P
    full = [("ic", i) for i in range(9)] + [("o", 0), ("ic", 9), ("ic", 10), ("o", 1), ("ic", 11), ("ic", 12), ("ic", 13),
                                            ("t", 0), ("ic", 14), ("t", 1), ("ic", 15)]
    short = [x for x in full if x[0] == "ic"]
    head = [("o", 0), ("o", 1), ("t", 0), ("t", 1)]
    NJ, NHEAD = len(full), len(head)
    FREE = 2

    with ExitStack() as c:
        sb = lambda n, s, d=F32: c.enter_context(nc.sbuf_tensor(n, s, d))
        sem = lambda n: c.enter_context(nc.semaphore(n))
        wg = sb("wg_sb", [P, IC, D], F32R)
        wu = sb("wu_sb", [P, IC, D], F32R)
        wd = sb("wd_sb", [P, IC, D], F32R)
        ow_hi, ow_lo = keep["ow_hi"], keep["ow_lo"]
        xt_hi = sb("xt_hi", [P, 2, DC, CH], F32R)
        xt_lo = sb("xt_lo", [P, 2, DC, CH], F32R)
        x1 = sb("x1", [P, 2, ST, D])
        x_in = sb("x_res", [P, 2, HALF, D])
        cp_hi = sb("cp_hi", [P, 2, NG, HC], F32R)
        cp_lo = sb("cp_lo", [P, 2, NG, HC], F32R)
        hidden = sb("hidden", [P, 2, CH])
        h_hi = sb("h_hi", [P, 2, CH], F32R)
        h_lo = sb("h_lo", [P, 2, CH], F32R)
        y_raw = sb("y_raw", [P, ST, D])
        down_scale = keep["whole"]
        gate_scale = sb("gate_scale_sb", [P, IC])
        up_scale = sb("up_scale_sb", [P, IC])
        ident = sb("ident3", [P, P])
        check = sb("check3", [P, 1])
        check_top = sb("check_top3", [1, 1])
        flag_f = sb("flag_f3", [1, 1])
        minus_half = sb("minus_half3", [P, 1])
        stats = sb("stats3", [P, 2, 6])
        mv = sb("mv3", [P, 2, ST, 2])
        veps = sb("veps3", [P, 2, ST])
        rstd = sb("rstd3", [P, 2, ST])
        inv_in = y_raw
        sums_flat = hidden[:, 0, :]
        inv_flat = hidden[:, 1, :]

        slot = [[c.enter_context(nc.psum_tensor(f"slot{s}{b}", [P, CH], F32)) for b in range(2)] for s in range(2)]
        y = [c.enter_context(nc.psum_tensor(f"y{st}", [P, D], F32)) for st in range(ST)]

        w_in = [sem(f"w_in{i}") for i in range(IC)]
        small_in = sem("small_in")
        ident_zero = sem("ident_zero")
        ident_ready = sem("ident_ready3")
        half_ready = sem("half_ready")
        ctx_in = [sem(f"ctx_in{h}") for h in range(2)]
        x_res_in = [sem(f"x_res_in{h}") for h in range(2)]
        half_used = sem("half_used")
        sums_in = sem("sums_in")
        inv_done = sem("inv_done")
        inv_stored = sem("inv_stored")
        checked = sem("checked")
        check_turned = sem("check_turned3")
        inv_ready = sem("inv_ready")
        c_scaled = sem("c_scaled")
        c_high = sem("c_high")
        c_ready = sem("c_ready")
        slot_full = sem("slot_full")
        slot_free = sem("slot_free")
        high_ready = sem("high_ready")
        gated = sem("gated")
        h_high = sem("h_high")
        h_ready = sem("h_ready")
        downed = sem("downed")
        y_taken = sem("y_taken")
        y_scaled = sem("y_scaled")
        out_stored = [sem(f"out_stored{b}") for b in range(2)]
        summed = [sem(f"summed{k}") for k in range(2)]
        measured = [sem(f"measured{k}") for k in range(2)]
        averaged = [sem(f"averaged{k}") for k in range(2)]
        var_ready = [sem(f"var_ready3{k}") for k in range(2)]
        rooted = [sem(f"rooted{k}") for k in range(2)]
        normed = [sem(f"normed{k}") for k in range(2)]
        block = c.enter_context(nc.Block())

        def start(n):
            return NHEAD + NJ * n

        def t_end(n):
            return NHEAD if isinstance(n, int) and n == 0 else start(n - 1) + full.index(("t", 1)) + 1

        def tile_of(xt, par, st):
            return xt[:, par, :, st * P:(st + 1) * P]

        def chunks_of(bank):
            return bank[:].rearrange("p (c r) -> p c r", c=DC)

        def ctx_load(sp, n, h):
            sp.wait_ge(half_used, HALF * n + h + 1)
            sp.dma_start(cp_lo[:, h, :, :].bitcast(F32), dr["ctx"].rearrange("(g r) s -> r g s", r=P)[:, :, bass.ds(n * CH + h * HC, HC)])\
              .then_inc(ctx_in[h], 16)

        def x_load(sp, n, h):
            sp.dma_start(x_in[:, h, :, :], io["x"].rearrange("(m t p) d -> m p t d", t=HALF, p=P)[bass.ds(n * 2 + h, 1)]
                         .rearrange("m p t d -> (m p) t d")).then_inc(x_res_in[h], 16)

        def inv_load(sp, n):
            for h in range(HG):
                sp.dma_start(inv_in[h * HD:(h + 1) * HD, :, :],
                             dr["inverse"].rearrange("n (g h) s -> n h g s", h=HG)[bass.ds(n, 1), h, :, :]
                             .to_broadcast([HD, NG, CH])).then_inc(inv_ready, 16)

        FLAT = CH * HEADS // P
        REST = slice(0, FLAT * (NCH - 1))

        def flat_rest(name):
            return dr[name].rearrange("n h (u s) -> (h u) n s", s=FLAT)[:, 1:, :]

        @block.sync
        def _(sp):
            ctx_load(sp, 0, 0)
            inv_load(sp, 0)
            ctx_load(sp, 0, 1)
            x_load(sp, 0, 0)
            x_load(sp, 0, 1)
            for b in range(2):
                sp.wait_ge(keep["ctx_stored"][b], 32 * (NCH // 2) * NG + 32)
            sp.dma_start(sums_flat[:, REST].rearrange("p (n s) -> p n s", s=FLAT), flat_rest("sums")).then_inc(sums_in, 16)
            sp.dma_start(gate_scale[:], io["gate_scale"]).then_inc(small_in, 16)
            sp.dma_start(up_scale[:], io["up_scale"]).then_inc(small_in, 16)
            sp.wait_ge(checked, 1)
            sp.dma_start(down_scale[:], io["down_scale"].rearrange("(a h) -> a h", a=1).to_broadcast([P, D])).then_inc(small_in, 16)
            for i in range(2):
                for k, to in enumerate((wg, wu, wd)):
                    sp.dma_start(to[:, i, :].bitcast(F32), dr["wq"][3 * i + k]).then_inc(w_in[i], 16)
            sp.wait_ge(inv_done, 1)
            sp.dma_start(flat_rest("inverse"), inv_flat[:, REST].rearrange("p (n s) -> p n s", s=FLAT)).then_inc(inv_stored, 16)
            for i in range(2, IC):
                for k, to in enumerate((wg, wu, wd)):
                    sp.dma_start(to[:, i, :].bitcast(F32), dr["wq"][3 * i + k]).then_inc(w_in[i], 16)

            def store(n, par, st):
                sp.wait_ge(normed[1], ST * n + st + 1)
                sp.nop(nofuse=True)
                sp.dma_start(io["out"].rearrange("(m p) d -> m p d", p=P)[bass.ds(n * ST + st, 1)]
                             .rearrange("m p d -> (m p) d"), x1[:, par, st, :]).then_inc(out_stored[par], 16)

            def body(n, c, par, before, after, pairs):
                if after:
                    for h in range(2):
                        ctx_load(sp, n + 1, h)
                        x_load(sp, n + 1, h)
                    if before:
                        sp.wait_ge(summed[1], ST * n)
                    else:
                        sp.wait_ge(inv_stored, 16)
                        sp.wait_ge(c_ready, HALF)
                    sp.nop(nofuse=True)
                    inv_load(sp, n + 1)
                if before:
                    for st in range(ST):
                        store(n - 1, 1 - par, st)

            over_chunks(sp, body)
            for st in range(ST):
                store(NCH - 1, 1, st)
            for b in range(2):
                sp.wait_ge(out_stored[b], 16 * ST * (NCH // 2 + 1))

        @block.gpsimd
        def _(pool):
            pool.memset(ident[:], 0.0).then_inc(ident_zero, 1)
            pool.wait_ge(ident_zero, 1)
            pool.affine_select(out=ident[:], in_=ident[:], compare_op=ALU.not_equal, fill=1.0, base=0,
                               pattern=[[-1, P]], channel_multiplier=1).then_inc(ident_ready, 1)
            pool.wait_ge(half_ready, 1)

            def root(k, n, st):
                pool.wait_ge(var_ready[k], ST * n + st + 1)
                pool.tensor_tensor(rstd[:, k, st:st + 1], veps[:, k, st:st + 1], minus_half[:], ALU.pow).then_inc(rooted[k], 1)

            def body(n, c, par, before, after, pairs):
                if before:
                    for st in range(ST):
                        root(1, n - 1, st)
                if after:
                    for st in range(ST):
                        root(0, n + 1, st)

            for st in range(ST):
                root(0, 0, st)
            over_chunks(pool, body)
            for st in range(ST):
                root(1, NCH - 1, st)

        @block.tensor
        def _(pe):
            pe.sem_inc(slot_free, FREE)
            pe.wait_ge(ident_ready, 1)

            pe.wait_ge(checked, 1)
            pe.transpose(y[0][0:1, 0:P], check[:], ident[:]).then_inc(check_turned, 1)

            def project_out(j, pos, n, h):
                pe.wait_ge(slot_free, j + 1)
                pe.wait_ge(c_ready, HALF * n + h + 1)
                for q in range(HALF):
                    first = True
                    for g in range(NG):
                        for a, w in ((cp_hi, ow_hi), (cp_hi, ow_lo), (cp_lo, ow_hi)):
                            ins = pe.matmul(slot[pos % 2][q][:], a[:, h, g, q * P:(q + 1) * P], w[:, g, :],
                                            start=first, stop=g == NG - 1 and a is cp_lo)
                            first = False
                ins.then_inc(slot_full, 1)

            def transpose(j, pos, n, par, p):
                pe.wait_ge(slot_free, j + 1)
                pe.wait_ge(normed[0], ST * n + HALF * p + HALF)
                for q in range(HALF):
                    for dc in range(DC):
                        ins = pe.transpose(slot[pos % 2][q][:, dc * P:(dc + 1) * P],
                                           x1[:, par, HALF * p + q, dc * P:(dc + 1) * P], ident[:])
                ins.then_inc(slot_full, 1)

            def program(v):
                def gate_up(j, pos, n, par, i, first_chunk):
                    pe.wait_ge(slot_free, j + 1)
                    if i == 0:
                        pe.wait_ge(slot_free, t_end(n) + FREE)
                    if first_chunk:
                        pe.wait_ge(w_in[i], 48)
                    for q, w in enumerate((wg, wu)):
                        for dc in range(DC):
                            for a, x in enumerate((xt_hi, xt_lo)):
                                ins = pe.matmul(slot[pos % 2][q][:], v(w[:, i, dc * P:(dc + 1) * P]), v(x[:, par, dc, :]),
                                                start=dc == 0 and a == 0, stop=dc == DC - 1 and a == 1)
                    ins.then_inc(slot_full, 1)

                def down(n, i, first_chunk):
                    pe.wait_ge(h_ready, IC * n + i + 1 + 2)
                    if i == 0 and not first_chunk:
                        pe.wait_ge(y_taken, ST * n)
                    for st in range(ST):
                        for a, x in enumerate((h_hi, h_lo)):
                            ins = pe.matmul(y[st][:], v(x[:, i % 2, st * P:(st + 1) * P]), v(wd[:, i, :]),
                                            start=i == 0 and a == 0, stop=i == IC - 1 and a == 1)
                    ins.then_inc(downed, 1)

                def body(n, c, par, before, after, pairs):
                    for pos, (kind, i) in enumerate(full if after else short):
                        j = start(n) + pos
                        if kind == "o":
                            project_out(j, pos, n + 1, i)
                        elif kind == "t":
                            transpose(j, pos, n + 1, 1 - par, i)
                        else:
                            gate_up(j, pos, n, par, i, not before)
                            if i:
                                down(n, i - 1, not before)
                            elif before:
                                down(n - 1, IC - 1, False)

                over_chunks(pe, body)
                down(NCH - 1, IC - 1, False)

            for pos, (kind, i) in enumerate(head):
                if kind == "o":
                    project_out(pos, pos, 0, i)
                else:
                    transpose(pos, pos, 0, 0, i)
            pe.wait_ge(checked, 4)
            wide = pe.value_load(keep["flags"][0:1, 1:2], min_val=0, max_val=1)
            with pe.If(wide):
                program(lambda ap: ap.bitcast(F32))
            with pe.Else():
                program(lambda ap: ap)

        @block.scalar
        def _(act):
            act.wait_ge(small_in, 48)

            def high(j, pos, n, par, p):
                act.wait_ge(slot_full, j + 1)
                for q in range(HALF):
                    act.activation(tile_of(xt_hi, par, HALF * p + q), chunks_of(slot[pos % 2][q]), ACT.Copy).then_inc(high_ready, 1)

            def take_y(n, last_one=False):
                act.wait_ge(downed, IC * (n + 1))
                act.wait_ge(c_ready, HALF * n + 2 * HALF if not last_one else HALF * NCH)
                for st in range(ST):
                    act.activation(y_raw[:, st, :], y[st][:], ACT.Copy).then_inc(y_taken, 1)

            def body(n, c, par, before, after, pairs):
                for pos, (kind, i) in enumerate(full if after else short):
                    j = start(n) + pos
                    if before and pos == 1:
                        take_y(n - 1)
                    if kind == "t":
                        high(j, pos, n + 1, 1 - par, i)
                    elif kind == "ic":
                        act.wait_ge(slot_full, j + 1)
                        act.wait_ge(h_ready, IC * n + i + 1)
                        act.activation(hidden[:, i % 2, :], slot[pos % 2][0][:], ACT.Silu,
                                       scale=gate_scale[:, i:i + 1]).then_inc(gated, 1)

            for pos, (kind, i) in enumerate(head):
                if kind == "t":
                    high(pos, pos, 0, 0, i)
            act.wait_ge(inv_stored, 16)
            over_chunks(act, body)
            take_y(NCH - 1, True)

        @block.vector
        def _(dve):
            dve.memset(minus_half[:], -0.5).then_inc(half_ready, 1)
            dve.sem_inc(half_used, 2)
            dve.sem_inc(h_ready, 2)
            for b in range(2):
                dve.sem_inc(out_stored[b], 16 * ST)
            dve.tensor_reduce(check[:], keep["whole"][:], AX.X, ALU.max).then_inc(checked, 1)
            dve.wait_ge(check_turned, 1)
            dve.tensor_reduce(check_top[:], y[0][0:1, 0:P], AX.X, ALU.max).then_inc(checked, 1)
            dve.wait_ge(checked, 2)
            dve.tensor_scalar(flag_f[:], check_top[:], WHOLE * WHOLE, None, ALU.is_gt).then_inc(checked, 1)
            dve.wait_ge(checked, 3)
            dve.tensor_copy(keep["flags"][0:1, 1:2], flag_f[:]).then_inc(checked, 1)

            def context(n, h):
                k = HALF * n + h
                dve.wait_ge(ctx_in[h], 16 * n + 16)
                if h == 0:
                    dve.wait_ge(inv_ready, 16 * HG * n + 16 * HG)
                scaled = inv_in[:, :, h * HC:(h + 1) * HC]
                dve.tensor_tensor(scaled, cp_lo[:, h, :, :].bitcast(F32), scaled, ALU.mult).then_inc(c_scaled, 1)
                dve.wait_ge(c_scaled, k + 1)
                dve.tensor_copy(cp_hi[:, h, :, :], scaled).then_inc(c_high, 1)
                dve.wait_ge(c_high, k + 1)
                dve.tensor_tensor(cp_lo[:, h, :, :], scaled, cp_hi[:, h, :, :].bitcast(F32), ALU.subtract).then_inc(c_ready, 1)

            def norm_begin(k, n, par, st, eps):
                rows = x1[:, par, st, :]
                at = ST * n + st + 1
                dve.wait_ge(summed[k], at)
                dve.bn_stats(stats[:, k, :], rows).then_inc(measured[k], 1)
                dve.wait_ge(measured[k], at)
                dve.nop(nofuse=True)
                dve.bn_aggr(mv[:, k, st, :], stats[:, k, :]).then_inc(averaged[k], 1)
                dve.wait_ge(averaged[k], at)
                dve.tensor_scalar(veps[:, k, st:st + 1], mv[:, k, st, 1:2], eps, None, ALU.add).then_inc(var_ready[k], 1)

            def norm_end(k, n, par, st):
                rows = x1[:, par, st, :]
                dve.wait_ge(rooted[k], ST * n + st + 1)
                dve.tensor_scalar(rows, rows, mv[:, k, st, 0:1], rstd[:, k, st:st + 1], ALU.subtract, ALU.mult)\
                   .then_inc(normed[k], 1)

            def residual(j, pos, n, par, h, stored):
                dve.wait_ge(slot_full, j + 1)
                if h == 0:
                    dve.wait_ge(out_stored[par], stored)
                dve.wait_ge(x_res_in[h], 16 * n + 16)
                for q in range(HALF):
                    ins = dve.tensor_tensor(x1[:, par, h * HALF + q, :], slot[pos % 2][q][:], x_in[:, h, q, :], ALU.add)
                    ins.then_inc(summed[0], 1)
                dve.wait_ge(summed[0], ST * n + h * HALF + HALF)
                dve.sem_inc(slot_free, 1)
                dve.sem_inc(half_used, 1)
                for q in range(HALF):
                    norm_begin(0, n, par, h * HALF + q, LN_EPS)

            def low(j, pos, n, par, p):
                for q in range(HALF):
                    st = HALF * p + q
                    dve.wait_ge(high_ready, ST * n + st + 1)
                    ins = dve.tensor_tensor(tile_of(xt_lo, par, st), chunks_of(slot[pos % 2][q]),
                                            tile_of(xt_hi, par, st).bitcast(F32), ALU.subtract)
                ins.then_inc(slot_free, 1)

            def make_hidden(j, pos, n, i):
                k = IC * n + i + 1
                dve.wait_ge(gated, k)
                hid = hidden[:, i % 2, :]
                dve.scalar_tensor_tensor(hid, slot[pos % 2][1][:], up_scale[:, i:i + 1], hid, ALU.mult, ALU.mult)\
                   .then_inc(slot_free, 1)
                dve.wait_ge(slot_free, j + 1 + FREE)
                if not (isinstance(n, int) and n == 0 and i < 2):
                    dve.wait_ge(downed, k - 2)
                dve.tensor_copy(h_hi[:, i % 2, :], hid).then_inc(h_high, 1)
                dve.wait_ge(h_high, k)
                dve.tensor_tensor(h_lo[:, i % 2, :], hid, h_hi[:, i % 2, :].bitcast(F32), ALU.subtract).then_inc(h_ready, 1)

            def add_y(n, par, st):
                dve.wait_ge(y_taken, ST * n + st + 1)
                dve.tensor_tensor(y_raw[:, st, :], y_raw[:, st, :], down_scale[:], ALU.mult).then_inc(y_scaled, 1)
                dve.wait_ge(y_scaled, ST * n + st + 1)
                dve.tensor_tensor(x1[:, par, st, :], x1[:, par, st, :], y_raw[:, st, :], ALU.add).then_inc(summed[1], 1)
                norm_begin(1, n, par, st, LN_EPS)

            def body(n, c, par, before, after, pairs):
                waiting = []
                for pos, (kind, i) in enumerate(full if after else short):
                    j = start(n) + pos
                    if kind == "o":
                        residual(j, pos, n + 1, 1 - par, i, 16 * ST * (pairs + par + 1))
                        waiting += [(0, n + 1, 1 - par, i * HALF + q) for q in range(HALF)]
                    elif kind == "t":
                        low(j, pos, n + 1, 1 - par, i)
                    else:
                        make_hidden(j, pos, n, i)
                        for w in waiting:
                            norm_end(*w)
                        waiting = []
                        if before and 1 <= i <= ST:
                            add_y(n - 1, 1 - par, i - 1)
                            waiting = [(1, n - 1, 1 - par, i - 1)]
                        if after and i in (7, 9):
                            context(n + 1, i // 9)

            context(0, 0)
            context(0, 1)
            dve.wait_ge(sums_in, 16)
            dve.reciprocal(inv_flat[:, REST], sums_flat[:, REST]).then_inc(inv_done, 1)
            for pos, (kind, i) in enumerate(head):
                if kind == "o":
                    residual(pos, pos, 0, 0, i, 16 * ST)
                    for q in range(HALF):
                        norm_end(0, 0, 0, i * HALF + q)
                else:
                    low(pos, pos, 0, 0, i)
            over_chunks(dve, body)
            for st in range(ST):
                add_y(NCH - 1, 1, st)
                if st:
                    norm_end(1, NCH - 1, 1, st - 1)
            norm_end(1, NCH - 1, 1, ST - 1)


NAMES = ["L0_attn_x", "L0_attn_Wqkv", "L0_attn_q_ln_scale", "L0_attn_k_ln_scale", "L0_attn_out_W",
         "L0_ffn_gate_w", "L0_ffn_gate_scale", "L0_ffn_up_w", "L0_ffn_up_scale", "L0_ffn_down_w",
         "L0_ffn_down_scale"]


def build(nc, io):
    def scratch(name, shape, dt):
        return nc.dram_tensor(name, shape, dt, kind="Internal").ap()

    dr = {
        "q_hi": scratch("q_hi", (D, S), F32), "q_lo": scratch("q_lo", (D, S), F32),
        "k_hi": scratch("k_hi", (D, S), F32), "k_lo": scratch("k_lo", (D, S), F32),
        "v": scratch("v_rows", (S, D), F32),
        "shift": scratch("shift", (2, HEADS, S), F32),
        "ctx": scratch("ctx", (D, S), F32),
        "sums": scratch("sums", (NCH, HEADS, CH), F32),
        "inverse": scratch("inverse", (NCH, HEADS, CH), F32),
        "wq": scratch("wq_float", (3 * IC, P, D), F32),
    }
    with ExitStack() as c:
        sb = lambda n, s, d: c.enter_context(nc.sbuf_tensor(n, s, d))
        sem = lambda n: c.enter_context(nc.semaphore(n))
        keep = {
            "flags": sb("flags", [P, 2], I32), "ow_hi": sb("ow_hi", [P, NG, D], F32R), "ow_lo": sb("ow_lo", [P, NG, D], F32R),
            "whole": sb("whole", [P, D], F32),
            "parts_stored": [sem(f"parts_stored{i}") for i in range(4)], "v_stored": [sem(f"v_stored{i}") for i in range(2)],
            "zero_stored": sem("zero_stored"), "ctx_stored": [sem(f"ctx_stored{b}") for b in range(2)],
        }
        project(nc, io, dr, keep)
        attend(nc, io, dr, keep)
        finish(nc, io, dr, keep)


def kernel(**inputs):
    import numpy as np
    import concourse.bacc as bacc
    from concourse.bass_utils import run_bass_kernel_spmd

    x, wqkv, q_scale, k_scale, out_w, gate_w, gate_scale, up_w, up_scale, down_w, down_scale = (
        np.asarray(inputs[n]) for n in NAMES)
    x = x.reshape(S, D)
    gate, up = (w.reshape(IC, P, DC, P).transpose(0, 3, 2, 1).reshape(IC, 1, P, D) for w in (gate_w, up_w))
    down = down_w.T.reshape(IC, 1, P, D)
    laid = {
        "x": x, "x_t": x.T, "wqkv": wqkv, "out_w": out_w, "down_scale": down_scale,
        "q_scale": q_scale.reshape(DC, P).T, "k_scale": k_scale.reshape(DC, P).T,
        "gate_scale": gate_scale.reshape(IC, P).T, "up_scale": up_scale.reshape(IC, P).T,
        "wq": np.concatenate([gate, up, down], axis=1).reshape(3 * IC, P, D),
    }
    nc = bacc.Bacc("TRN2", target_bir_lowering=False, num_devices=1)
    arrays, io = {}, {}
    for name, a in laid.items():
        a = np.ascontiguousarray(a)
        arrays[f"in_{name}"] = a
        io[name] = nc.dram_tensor(f"in_{name}", a.shape, mybir.dt.from_np(a.dtype), kind="ExternalInput").ap()
    io["out"] = nc.dram_tensor("out_y", (S, D), F32, kind="ExternalOutput").ap()
    build(nc, io)
    r = run_bass_kernel_spmd(nc, [arrays], core_ids=[0])
    return r.results[0]["out_y"].reshape(1, S, D)
```
